# Optimizing a Trainium2 kernel written in Bass

```python
import numpy as np
import jax
import jax.numpy as jnp

def _softmax(x, axis=-1):
    return jax.nn.softmax(x, axis=axis)

def _gelu(x):
    return jax.nn.gelu(x, approximate=True)

def _silu(x):
    return jax.nn.silu(x)

def _sigmoid(x):
    return jax.nn.sigmoid(x)

def _layernorm(x, axis=-1, eps=1e-05):
    m = jnp.mean(x, axis=axis, keepdims=True)
    v = jnp.var(x, axis=axis, keepdims=True)
    return (x - m) / jnp.sqrt(v + eps)

def _scatter_add(tgt, idx, src, axis=0):
    return tgt.at[idx].add(src)

def _segment_sum(src, seg, n):
    return jax.ops.segment_sum(src, seg, n)
kernel_name = 'mk_flamingo_gated_d2_seqx_r4_b79a64'

def setup_inputs(seed: int=0):
    np.random.seed(seed)
    _w = jnp.asarray

    def _rec_inputs():
        import jax
        import jax.numpy as jnp
        _rk = jax.random.key(seed)
        x = -0.0003929 + 0.9999 * jax.random.normal(jax.random.fold_in(_rk, 1), (2, 512, 512), jnp.float32)
        _lenS = 512 - jax.random.randint(jax.random.fold_in(_rk, 7), (2,), 0, max(1, 512 // 4) + 1, jnp.int32)
        _lenS2 = 1024 - jax.random.randint(jax.random.fold_in(_rk, 8), (2,), 0, max(1, 1024 // 4) + 1, jnp.int32)
        _ctx_1024P = jax.random.normal(jax.random.fold_in(_rk, 11), (2, 16, 256), jnp.float32)
        _ctx_1024c = jax.random.dirichlet(jax.random.fold_in(_rk, 511), 0.3 * jnp.ones((16,), jnp.float32), (2, 1024))
        _ctx_1024t = jnp.einsum('bsk,bkd->bsd', _ctx_1024c, _ctx_1024P)
        _ctx_1024t = _ctx_1024t * jax.lax.rsqrt(jnp.mean(jnp.square(_ctx_1024t)) + 1e-12) * 0.953939
        ctx_1024 = -0.000494167 + 1.00018 * (_ctx_1024t + 0.3 * jax.random.normal(jax.random.fold_in(_rk, 611), (2, 1024, 256), jnp.float32))
        _validS = jnp.arange(512)[None, :] < _lenS[:, None]
        _validS2 = jnp.arange(1024)[None, :] < _lenS2[:, None]
        _causal = jnp.tril(jnp.ones((512, 512), dtype=bool))
        mask_BxS2_bf1 = jnp.ones((2, 1024), dtype=bool)
        _g = jax.random.normal(jax.random.fold_in(_rk, 9001), (2, 2), jnp.float32)
        _g = jnp.sign(_g) * jnp.maximum(jnp.abs(_g), 1.0) + (_g == 0) * 1.0
        g_xattn = _g[0]
        g_ffn = _g[1]
        return (x, ctx_1024, mask_BxS2_bf1, g_xattn, g_ffn)
    x, ctx_1024, mask_BxS2_bf1, g_xattn, g_ffn = _rec_inputs()

    def _L0_xattn_setup():
        import jax, jax.numpy as jnp
        import numpy as np
        N_HEADS = 16
        N_KV_HEADS = 8
        HEAD_DIM = 128
        D_TEXT = 512
        D_VISION = 256
        GROUPS = N_HEADS // N_KV_HEADS
        key = jax.random.key(seed)
        ks = jax.random.split(key, 6)
        B, T_text, T_vis = (4, 512, 144)
        text_hidden = jax.random.normal(ks[0], (B, T_text, D_TEXT), dtype=jnp.float32)
        vision_tokens = jax.random.normal(ks[1], (B, T_vis, D_VISION), dtype=jnp.float32)
        vision_mask = jnp.ones((B, T_vis), dtype=bool)
        s = 0.02
        Wq = jax.random.normal(ks[2], (D_TEXT, N_HEADS * HEAD_DIM), dtype=jnp.float32) * s
        Wk = jax.random.normal(ks[3], (D_VISION, N_KV_HEADS * HEAD_DIM), dtype=jnp.float32) * s
        Wv = jax.random.normal(ks[4], (D_VISION, N_KV_HEADS * HEAD_DIM), dtype=jnp.float32) * s
        Wo = jax.random.normal(ks[5], (N_HEADS * HEAD_DIM, D_TEXT), dtype=jnp.float32) * s
        return {'text_hidden': text_hidden, 'vision_tokens': vision_tokens, 'vision_mask': vision_mask, 'Wq': Wq, 'Wk': Wk, 'Wv': Wv, 'Wo': Wo}
    _L0_xattn_all = _L0_xattn_setup()
    _L0_xattn_in = {k: v for k, v in _L0_xattn_all.items() if k in ('Wq', 'Wk', 'Wv', 'Wo')}
    del _L0_xattn_all

    def _L0_ffn_setup():
        import jax, jax.numpy as jnp
        import numpy as np
        EPS = 1e-05
        ROPE_BASE = 150000.0
        NHEADS = 32
        KVHEADS = 8
        HEAD_DIM = 64
        TOP_K = 4

        def _rms(x, w):
            return x * jax.lax.rsqrt(jnp.mean(x * x, -1, keepdims=True) + EPS) * w

        def _rope(q, k):
            S, hd = (q.shape[1], q.shape[-1])
            half = hd // 2
            inv = 1.0 / ROPE_BASE ** (jnp.arange(half, dtype=jnp.float32) / half)
            ang = jnp.arange(S, dtype=jnp.float32)[:, None] * inv
            cos = jnp.concatenate([jnp.cos(ang), jnp.cos(ang)], -1)[None, :, None, :]
            sin = jnp.concatenate([jnp.sin(ang), jnp.sin(ang)], -1)[None, :, None, :]

            def rot(t):
                t1, t2 = (t[..., :half], t[..., half:])
                return jnp.concatenate([-t2, t1], -1)
            return (q * cos + rot(q) * sin, k * cos + rot(k) * sin)
        key = jax.random.key(seed)
        ks = jax.random.split(key, 12)
        B, S, D, H, E = (1, 256, 512, 512, 16)
        s = 0.02
        return {'x': jax.random.normal(ks[0], (B, S, D), jnp.float32), 'ln_w': jnp.ones((D,), jnp.float32), 'ff_ln_w': jnp.ones((D,), jnp.float32), 'wq': jax.random.normal(ks[1], (D, NHEADS * HEAD_DIM), jnp.float32) * s, 'wk': jax.random.normal(ks[2], (D, KVHEADS * HEAD_DIM), jnp.float32) * s, 'wv': jax.random.normal(ks[3], (D, KVHEADS * HEAD_DIM), jnp.float32) * s, 'wo': jax.random.normal(ks[4], (NHEADS * HEAD_DIM, D), jnp.float32) * s, 'wg': jax.random.normal(ks[5], (D, E), jnp.float32) * s, 'w1': jax.random.normal(ks[6], (E, D, H), jnp.float32) * s, 'w3': jax.random.normal(ks[7], (E, D, H), jnp.float32) * s, 'w2': jax.random.normal(ks[8], (E, H, D), jnp.float32) * s}
    _L0_ffn_all = _L0_ffn_setup()
    _L0_ffn_in = {k: v for k, v in _L0_ffn_all.items() if k in ('ln_w', 'ff_ln_w', 'wq', 'wk', 'wv', 'wo', 'wg', 'w1', 'w3', 'w2')}
    del _L0_ffn_all

    def _L1_xattn_setup():
        import jax, jax.numpy as jnp
        import numpy as np
        B, S1, S2, DCA = (2, 512, 256, 16)
        QDIM, KDIM, H = (512, 256, 16)
        HD = QDIM // H
        SCALE = HD ** (-0.5)
        EPS = 1e-06
        DCA_WEIGHT = 1.0

        def _ln(t, w, b):
            m = jnp.mean(t, axis=-1, keepdims=True)
            v = jnp.var(t, axis=-1, keepdims=True)
            return (t - m) * jax.lax.rsqrt(v + EPS) * w + b

        def _attn(q, k, v):
            s = jnp.einsum('bhqd,bhkd->bhqk', q, k) * SCALE
            p = jax.nn.softmax(s, axis=-1)
            return jnp.einsum('bhqk,bhkd->bhqd', p, v)
        key = jax.random.key(seed)
        ks = jax.random.split(key, 8)
        w = lambda k, shape: jax.random.normal(k, shape, jnp.float32) * 0.02
        return {'x': jax.random.normal(ks[0], (B, S1, QDIM), jnp.float32), 'y': jax.random.normal(ks[1], (B, S2 + DCA, KDIM), jnp.float32), 'Wq': w(ks[2], (QDIM, QDIM)), 'bq': jnp.zeros((QDIM,), jnp.float32), 'Wk': w(ks[3], (KDIM, QDIM)), 'bk': jnp.zeros((QDIM,), jnp.float32), 'Wv': w(ks[4], (KDIM, QDIM)), 'bv': jnp.zeros((QDIM,), jnp.float32), 'Wkv_dca': w(ks[5], (KDIM, 2 * QDIM)), 'bkv_dca': jnp.zeros((2 * QDIM,), jnp.float32), 'qn_w': jnp.ones((HD,), jnp.float32), 'qn_b': jnp.zeros((HD,), jnp.float32), 'kn_w': jnp.ones((HD,), jnp.float32), 'kn_b': jnp.zeros((HD,), jnp.float32), 'kn_dca_w': jnp.ones((HD,), jnp.float32), 'kn_dca_b': jnp.zeros((HD,), jnp.float32), 'Wo': w(ks[6], (QDIM, QDIM)), 'bo': jnp.zeros((QDIM,), jnp.float32)}
    _L1_xattn_all = _L1_xattn_setup()
    _L1_xattn_in = {k: v for k, v in _L1_xattn_all.items() if k in ('Wq', 'bq', 'Wk', 'bk', 'Wv', 'bv', 'Wkv_dca', 'bkv_dca', 'qn_w', 'qn_b', 'kn_w', 'kn_b', 'kn_dca_w', 'kn_dca_b', 'Wo', 'bo')}
    del _L1_xattn_all

    def _L1_ffn_setup():
        import jax, jax.numpy as jnp
        import numpy as np
        EPS = 1e-05

        def _act_quant(x):
            scale = 127.0 / jnp.clip(jnp.max(jnp.abs(x), axis=-1, keepdims=True), EPS, None)
            return jnp.clip(jnp.round(x * scale), -128.0, 127.0) / scale

        def _weight_quant(w):
            scale = 1.0 / jnp.clip(jnp.mean(jnp.abs(w)), EPS, None)
            return jnp.clip(jnp.round(w * scale), -1.0, 1.0) / scale

        def _ste(x, q):
            return x + jax.lax.stop_gradient(q - x)

        def _bitlinear(x, w, b):
            xq = _ste(x, _act_quant(x))
            wq = _ste(w, _weight_quant(w))
            return jnp.einsum('bsd,hd->bsh', xq, wq) + b
        key = jax.random.key(seed)
        k1, k2, k3 = jax.random.split(key, 3)
        dim, hidden = (512, 2048)
        x = jax.random.normal(k1, (4, 512, dim), dtype=jnp.float32)
        w1 = jax.random.normal(k2, (hidden, dim), dtype=jnp.float32) * 0.02
        b1 = jnp.zeros((hidden,), dtype=jnp.float32)
        w2 = jax.random.normal(k3, (dim, hidden), dtype=jnp.float32) * 0.02
        b2 = jnp.zeros((dim,), dtype=jnp.float32)
        return {'x': x, 'w1': w1, 'b1': b1, 'w2': w2, 'b2': b2}
    _L1_ffn_all = _L1_ffn_setup()
    _L1_ffn_in = {k: v for k, v in _L1_ffn_all.items() if k in ('w1', 'b1', 'w2', 'b2')}
    del _L1_ffn_all
    return {'x': x, 'ctx_1024': ctx_1024, 'mask_BxS2_bf1': mask_BxS2_bf1, 'g_xattn': g_xattn, 'g_ffn': g_ffn, 'L0_xattn_Wq': _L0_xattn_in['Wq'], 'L0_xattn_Wk': _L0_xattn_in['Wk'], 'L0_xattn_Wv': _L0_xattn_in['Wv'], 'L0_xattn_Wo': _L0_xattn_in['Wo'], 'L0_ffn_ln_w': _L0_ffn_in['ln_w'], 'L0_ffn_ff_ln_w': _L0_ffn_in['ff_ln_w'], 'L0_ffn_wq': _L0_ffn_in['wq'], 'L0_ffn_wk': _L0_ffn_in['wk'], 'L0_ffn_wv': _L0_ffn_in['wv'], 'L0_ffn_wo': _L0_ffn_in['wo'], 'L0_ffn_wg': _L0_ffn_in['wg'], 'L0_ffn_w1': _L0_ffn_in['w1'], 'L0_ffn_w3': _L0_ffn_in['w3'], 'L0_ffn_w2': _L0_ffn_in['w2'], 'L1_xattn_Wq': _L1_xattn_in['Wq'], 'L1_xattn_bq': _L1_xattn_in['bq'], 'L1_xattn_Wk': _L1_xattn_in['Wk'], 'L1_xattn_bk': _L1_xattn_in['bk'], 'L1_xattn_Wv': _L1_xattn_in['Wv'], 'L1_xattn_bv': _L1_xattn_in['bv'], 'L1_xattn_Wkv_dca': _L1_xattn_in['Wkv_dca'], 'L1_xattn_bkv_dca': _L1_xattn_in['bkv_dca'], 'L1_xattn_qn_w': _L1_xattn_in['qn_w'], 'L1_xattn_qn_b': _L1_xattn_in['qn_b'], 'L1_xattn_kn_w': _L1_xattn_in['kn_w'], 'L1_xattn_kn_b': _L1_xattn_in['kn_b'], 'L1_xattn_kn_dca_w': _L1_xattn_in['kn_dca_w'], 'L1_xattn_kn_dca_b': _L1_xattn_in['kn_dca_b'], 'L1_xattn_Wo': _L1_xattn_in['Wo'], 'L1_xattn_bo': _L1_xattn_in['bo'], 'L1_ffn_w1': _L1_ffn_in['w1'], 'L1_ffn_b1': _L1_ffn_in['b1'], 'L1_ffn_w2': _L1_ffn_in['w2'], 'L1_ffn_b2': _L1_ffn_in['b2']}

def reference(x, ctx_1024, mask_BxS2_bf1, g_xattn, g_ffn, L0_xattn_Wq, L0_xattn_Wk, L0_xattn_Wv, L0_xattn_Wo, L0_ffn_ln_w, L0_ffn_ff_ln_w, L0_ffn_wq, L0_ffn_wk, L0_ffn_wv, L0_ffn_wo, L0_ffn_wg, L0_ffn_w1, L0_ffn_w3, L0_ffn_w2, L1_xattn_Wq, L1_xattn_bq, L1_xattn_Wk, L1_xattn_bk, L1_xattn_Wv, L1_xattn_bv, L1_xattn_Wkv_dca, L1_xattn_bkv_dca, L1_xattn_qn_w, L1_xattn_qn_b, L1_xattn_kn_w, L1_xattn_kn_b, L1_xattn_kn_dca_w, L1_xattn_kn_dca_b, L1_xattn_Wo, L1_xattn_bo, L1_ffn_w1, L1_ffn_b1, L1_ffn_w2, L1_ffn_b2):
    import jax
    import jax.numpy as jnp

    def _L0_xattn_ref(text_hidden, vision_tokens, vision_mask, Wq, Wk, Wv, Wo):
        import jax, jax.numpy as jnp
        import numpy as np
        N_HEADS = 16
        N_KV_HEADS = 8
        HEAD_DIM = 128
        D_TEXT = 512
        D_VISION = 256
        GROUPS = N_HEADS // N_KV_HEADS
        B, T_text, _ = text_hidden.shape
        T_vis = vision_tokens.shape[1]
        scale = jnp.float32(np.sqrt(HEAD_DIM))
        q = (text_hidden @ Wq).reshape(B, T_text, N_HEADS, HEAD_DIM).transpose(0, 2, 1, 3)
        k = (vision_tokens @ Wk).reshape(B, T_vis, N_KV_HEADS, HEAD_DIM).transpose(0, 2, 1, 3)
        v = (vision_tokens @ Wv).reshape(B, T_vis, N_KV_HEADS, HEAD_DIM).transpose(0, 2, 1, 3)
        k = jnp.repeat(k, GROUPS, axis=1)
        v = jnp.repeat(v, GROUPS, axis=1)
        scores = jnp.einsum('bhtd,bhsd->bhts', q, k) / scale
        mask = vision_mask[:, None, None, :]
        scores = jnp.where(mask, scores, -jnp.inf)
        attn = jax.nn.softmax(scores, axis=-1)
        attn = jnp.nan_to_num(attn, nan=0.0)
        out = jnp.einsum('bhts,bhsd->bhtd', attn, v)
        out = out.transpose(0, 2, 1, 3).reshape(B, T_text, N_HEADS * HEAD_DIM)
        return out @ Wo

    def _L0_ffn_ref(x, ln_w, ff_ln_w, wq, wk, wv, wo, wg, w1, w3, w2):
        import jax, jax.numpy as jnp
        import numpy as np
        EPS = 1e-05
        ROPE_BASE = 150000.0
        NHEADS = 32
        KVHEADS = 8
        HEAD_DIM = 64
        TOP_K = 4

        def _rms(x, w):
            return x * jax.lax.rsqrt(jnp.mean(x * x, -1, keepdims=True) + EPS) * w

        def _rope(q, k):
            S, hd = (q.shape[1], q.shape[-1])
            half = hd // 2
            inv = 1.0 / ROPE_BASE ** (jnp.arange(half, dtype=jnp.float32) / half)
            ang = jnp.arange(S, dtype=jnp.float32)[:, None] * inv
            cos = jnp.concatenate([jnp.cos(ang), jnp.cos(ang)], -1)[None, :, None, :]
            sin = jnp.concatenate([jnp.sin(ang), jnp.sin(ang)], -1)[None, :, None, :]

            def rot(t):
                t1, t2 = (t[..., :half], t[..., half:])
                return jnp.concatenate([-t2, t1], -1)
            return (q * cos + rot(q) * sin, k * cos + rot(k) * sin)
        B, S, D = x.shape
        h = _rms(x, ln_w)
        q = (h @ wq).reshape(B, S, NHEADS, HEAD_DIM)
        k = (h @ wk).reshape(B, S, KVHEADS, HEAD_DIM)
        v = (h @ wv).reshape(B, S, KVHEADS, HEAD_DIM)
        q, k = _rope(q, k)
        g = NHEADS // KVHEADS
        k = jnp.repeat(k, g, axis=2)
        v = jnp.repeat(v, g, axis=2)
        scores = jnp.einsum('bqhd,bkhd->bhqk', q, k) / np.float32(np.sqrt(HEAD_DIM))
        causal = jnp.tril(jnp.ones((S, S), bool))
        scores = jnp.where(causal[None, None], scores, jnp.float32(-1e+30))
        attn = jax.nn.softmax(scores, -1)
        o = jnp.einsum('bhqk,bkhd->bqhd', attn, v).reshape(B, S, NHEADS * HEAD_DIM)
        x = x + o @ wo
        h = _rms(x, ff_ln_w)
        logits = h @ wg
        topv, topi = jax.lax.top_k(logits, TOP_K)
        gate = jax.nn.softmax(topv, -1)
        bidx = jnp.arange(B)[:, None, None]
        sidx = jnp.arange(S)[None, :, None]
        weights = jnp.zeros_like(logits).at[bidx, sidx, topi].set(gate)
        a = jax.nn.silu(jnp.einsum('bsd,edh->bseh', h, w1)) * jnp.einsum('bsd,edh->bseh', h, w3)
        y = jnp.einsum('bseh,ehd->bsed', a, w2)
        moe = jnp.einsum('bsed,bse->bsd', y, weights)
        return x + moe

    def _L1_xattn_ref(x, y, Wq, bq, Wk, bk, Wv, bv, Wkv_dca, bkv_dca, qn_w, qn_b, kn_w, kn_b, kn_dca_w, kn_dca_b, Wo, bo):
        import jax, jax.numpy as jnp
        import numpy as np
        B, S1, S2, DCA = (2, 512, 256, 16)
        QDIM, KDIM, H = (512, 256, 16)
        HD = QDIM // H
        SCALE = HD ** (-0.5)
        EPS = 1e-06
        DCA_WEIGHT = 1.0

        def _ln(t, w, b):
            m = jnp.mean(t, axis=-1, keepdims=True)
            v = jnp.var(t, axis=-1, keepdims=True)
            return (t - m) * jax.lax.rsqrt(v + EPS) * w + b

        def _attn(q, k, v):
            s = jnp.einsum('bhqd,bhkd->bhqk', q, k) * SCALE
            p = jax.nn.softmax(s, axis=-1)
            return jnp.einsum('bhqk,bhkd->bhqd', p, v)
        b, s1, _ = x.shape
        y_dca = y[:, -DCA:, :]
        y_main = y[:, :-DCA, :]
        kv_dca = (y_dca @ Wkv_dca + bkv_dca).reshape(b, DCA, 2, H, HD)
        k_dca = _ln(kv_dca[:, :, 0], kn_dca_w, kn_dca_b)
        v_dca = kv_dca[:, :, 1]
        s2 = y_main.shape[1]
        q = _ln((x @ Wq + bq).reshape(b, s1, H, HD), qn_w, qn_b)
        kv = jnp.concatenate([y_main @ Wk + bk, y_main @ Wv + bv], axis=-1)
        kv = kv.reshape(b, s2, H, 2 * HD)
        k = _ln(kv[..., :HD], kn_w, kn_b)
        v = kv[..., HD:]
        qT = q.transpose(0, 2, 1, 3)
        ctx = _attn(qT, k.transpose(0, 2, 1, 3), v.transpose(0, 2, 1, 3))
        ctx = ctx.transpose(0, 2, 1, 3).reshape(b, s1, QDIM)
        ctx_dca = _attn(qT, k_dca.transpose(0, 2, 1, 3), v_dca.transpose(0, 2, 1, 3))
        ctx_dca = ctx_dca.transpose(0, 2, 1, 3).reshape(b, s1, QDIM)
        ctx = ctx + DCA_WEIGHT * ctx_dca
        return ctx @ Wo + bo

    def _L1_ffn_ref(x, w1, b1, w2, b2):
        import jax, jax.numpy as jnp
        import numpy as np
        EPS = 1e-05

        def _act_quant(x):
            scale = 127.0 / jnp.clip(jnp.max(jnp.abs(x), axis=-1, keepdims=True), EPS, None)
            return jnp.clip(jnp.round(x * scale), -128.0, 127.0) / scale

        def _weight_quant(w):
            scale = 1.0 / jnp.clip(jnp.mean(jnp.abs(w)), EPS, None)
            return jnp.clip(jnp.round(w * scale), -1.0, 1.0) / scale

        def _ste(x, q):
            return x + jax.lax.stop_gradient(q - x)

        def _bitlinear(x, w, b):
            xq = _ste(x, _act_quant(x))
            wq = _ste(w, _weight_quant(w))
            return jnp.einsum('bsd,hd->bsh', xq, wq) + b
        h = jax.nn.gelu(_bitlinear(x, w1, b1), approximate=False)
        return _bitlinear(h, w2, b2)
    x = x + jnp.tanh(g_xattn[0]) * _L0_xattn_ref(_layernorm(x, axis=-1), ctx_1024, mask_BxS2_bf1, L0_xattn_Wq, L0_xattn_Wk, L0_xattn_Wv, L0_xattn_Wo)
    x = x + jnp.tanh(g_ffn[0]) * _L0_ffn_ref(_layernorm(x, axis=-1), L0_ffn_ln_w, L0_ffn_ff_ln_w, L0_ffn_wq, L0_ffn_wk, L0_ffn_wv, L0_ffn_wo, L0_ffn_wg, L0_ffn_w1, L0_ffn_w3, L0_ffn_w2)
    x = x + jnp.tanh(g_xattn[1]) * _L1_xattn_ref(_layernorm(x, axis=-1), ctx_1024, L1_xattn_Wq, L1_xattn_bq, L1_xattn_Wk, L1_xattn_bk, L1_xattn_Wv, L1_xattn_bv, L1_xattn_Wkv_dca, L1_xattn_bkv_dca, L1_xattn_qn_w, L1_xattn_qn_b, L1_xattn_kn_w, L1_xattn_kn_b, L1_xattn_kn_dca_w, L1_xattn_kn_dca_b, L1_xattn_Wo, L1_xattn_bo)
    x = x + jnp.tanh(g_ffn[1]) * _L1_ffn_ref(_layernorm(x, axis=-1), L1_ffn_w1, L1_ffn_b1, L1_ffn_w2, L1_ffn_b2)
    return x

_drawn_inputs = setup_inputs


def setup_inputs(seed=0):
    import zlib

    import numpy as np

    out = dict(_drawn_inputs(seed))
    spreads = {'g_ffn': (-1.0, 0.2),
     'L0_ffn_ln_w': (1.0, 0.2),
     'L0_ffn_ff_ln_w': (1.0, 0.2),
     'L1_xattn_bq': (0.0, 0.1),
     'L1_xattn_bk': (0.0, 0.1),
     'L1_xattn_bv': (0.0, 0.1),
     'L1_xattn_bkv_dca': (0.0, 0.1),
     'L1_xattn_qn_w': (1.0, 0.2),
     'L1_xattn_qn_b': (0.0, 0.472),
     'L1_xattn_kn_w': (1.0, 0.6),
     'L1_xattn_kn_b': (0.0, 0.8),
     'L1_xattn_kn_dca_w': (1.0, 0.576),
     'L1_xattn_kn_dca_b': (0.0, 0.8),
     'L1_xattn_bo': (0.0, 0.1),
     'L1_ffn_b1': (0.0, 0.1),
     'L1_ffn_b2': (0.0, 0.1)}
    factors = {'L0_xattn_Wq': 5.746, 'L0_xattn_Wk': 5.846}
    for name, (base, spread) in spreads.items():
        noise = np.random.default_rng([zlib.crc32(name.encode()), seed]).standard_normal(out[name].shape)
        drawn = base * np.exp(spread * noise) if base else spread * noise
        out[name] = jnp.asarray(drawn.astype(out[name].dtype))
    for name, factor in factors.items():
        out[name] = (out[name] * factor).astype(out[name].dtype)
    return out
```

```python
from contextlib import ExitStack

import numpy as np

import concourse.bass as bass
from concourse import mybir

P = 128
BANK = 512
F32 = mybir.dt.float32
F32R = mybir.dt.float32r
BF16 = mybir.dt.bfloat16
U8 = mybir.dt.uint8
ALU = mybir.AluOpType
ACT = mybir.ActivationFunctionType
AX = mybir.AxisListType

B, S, D = 2, 512, 512
S2, DV = 1024, 256
T = B * S
NT = T // P
QT = S // P
KC = D // P
VC = DV // P
NC_T = B * S2 // P
BIG = 1.0e30


class Use:

    def __init__(self, plan):
        self.plan = plan
        self.total = len(plan)
        self.per = {e: sum(x == e for _, x in plan) for e in "AD"}
        self.index, self.nth, seen = {}, [], {"A": 0, "D": 0}
        for n, (name, e) in enumerate(plan):
            seen[e] += 1
            self.nth.append((e, seen[e]))
            self.index[name] = n

    def emptied(self, n, it):
        e, c = self.nth[n % self.total]
        return e, self.per[e] * (it + 1 + n // self.total) + c


def program(nc, a, out):
    ctx = ExitStack()
    with ctx:
        def sem(name):
            return ctx.enter_context(nc.semaphore(name))

        def keep(name, shape, dt=F32):
            return ctx.enter_context(nc.sbuf_tensor(name, shape, dt))

        pairs = [ctx.enter_context(nc.psum_tensor(f"pair{i}", [P, 2 * BANK], F32)) for i in range(4)]
        banks = [pairs[i // 2][:, (i % 2) * BANK:(i % 2 + 1) * BANK] for i in range(8)]

        x = keep("x", [P, NT * D])
        hslot = keep("hslot", [P, 2 * D])
        ident = keep("ident", [P, P])
        gates = keep("gates", [P, 4])
        tgate = keep("tgate", [P, 4])
        stats = keep("stats", [P, NT * 6])
        mv = keep("mv", [P, NT * 2])
        std = keep("std", [P, NT])
        rstd = keep("rstd", [P, NT])
        eps = keep("eps", [P, 2])
        scrap = keep("scrap", [P, 64])
        x3 = x[:, :].rearrange("p (t d) -> p t d", t=NT)

        s_const, s_x, s_gate, s_eps, s_out = sem("s_const"), sem("s_x"), sem("s_gate"), sem("s_eps"), sem("s_out")
        s_tgate = sem("s_tgate")

        programs = {"SP": [], "ACT": [], "PE": [], "DVE": [], "POOL": []}

        def layernorm(tag, before, hT3):
            s_stat, s_mv, s_std, s_rstd, s_h, s_tr, s_ev = [
                sem(f"{tag}_{n}") for n in ("stat", "mv", "std", "rstd", "h", "tr", "ev")]

            def vector(dve):
                dve.wait_ge(*before)
                for t in range(NT):
                    dve.bn_stats(stats[:, 6 * t:6 * t + 6], x3[:, t, :]).then_inc(s_stat, 1)
                for t in range(NT):
                    dve.wait_ge(s_stat, t + 1)
                    dve.bn_aggr(mv[:, 2 * t:2 * t + 2], stats[:, 6 * t:6 * t + 6]).then_inc(s_mv, 1)
                dve.wait_ge(s_std, 1)
                dve.reciprocal(rstd[:, :], std[:, :]).then_inc(s_rstd, 1)
                dve.wait_ge(s_rstd, 1)
                for t in range(NT):
                    if t >= 2:
                        dve.wait_ge(s_tr, t - 1)
                    dve.tensor_scalar(hslot[:, (t % 2) * D:(t % 2 + 1) * D], x3[:, t, :], mv[:, 2 * t:2 * t + 1],
                                      rstd[:, t:t + 1], ALU.subtract, ALU.mult).then_inc(s_h, 1)

            def scalar(act):
                act.wait_ge(s_eps, 1)
                act.wait_ge(s_mv, NT)
                act.activation(std[:, :], mv[:, :].rearrange("p (t k) -> p t k", k=2)[:, :, 1], ACT.Sqrt,
                               bias=eps[:, 0:1]).then_inc(s_std, 1)
                for t in range(NT):
                    act.wait_ge(s_tr, t + 1)
                    act.activation(hT3[:, :, t * P:(t + 1) * P],
                                   banks[t % 2][:, :].rearrange("p (c n) -> p c n", c=KC), ACT.Copy).then_inc(s_ev, 1)

            def tensor(pe):
                pe.wait_ge(s_const, 16)
                for t in range(NT):
                    pe.wait_ge(s_h, t + 1)
                    if t >= 2:
                        pe.wait_ge(s_ev, t - 1)
                    for c in range(KC):
                        mm = pe.transpose(banks[t % 2][:, c * P:(c + 1) * P],
                                          hslot[:, (t % 2) * D + c * P:(t % 2) * D + (c + 1) * P], ident[:, :])
                    mm.then_inc(s_tr, 1)

            programs["DVE"].append(vector)
            programs["ACT"].append(scalar)
            programs["PE"].append(tensor)
            return s_ev

        s_ones = sem("s_ones")

        def load_sync(sp):
            sp.dma_start(x3, a["x"].rearrange("b (t p) d -> p (b t) d", p=P)).then_inc(s_x, 16)
            sp.dma_start(ident[:, :], a["c_ident"]).then_inc(s_const, 16)
            sp.dma_start(gates[:, 0:2], a["g_xattn"].partition_broadcast(P)).then_inc(s_gate, 16)
            sp.dma_start(gates[:, 2:4], a["g_ffn"].partition_broadcast(P)).then_inc(s_gate, 16)

        def load_vector(dve):
            dve.memset(eps[:, 0:1], 1e-5).then_inc(s_ones, 1)
            dve.memset(eps[:, 1:2], 1e-6).then_inc(s_eps, 1)
            dve.memset(scrap[:, :], 0.0).then_inc(s_ones, 1)

        def load_scalar(act):
            act.wait_ge(s_gate, 32)
            act.wait_ge(s_ones, 2)
            act.activation(tgate[:, :], gates[:, :], ACT.Tanh).then_inc(s_tgate, 1)

        programs["SP"].append(load_sync)
        programs["DVE"].append(load_vector)
        programs["ACT"].append(load_scalar)

        phase = ExitStack()

        def sb(name, shape, dt=F32):
            return phase.enter_context(nc.sbuf_tensor(name, shape, dt))

        hT3 = sb("hT_x0", [P, KC * T])[:, :].rearrange("p (c t) -> p c t", c=KC)
        ctxT = sb("ctxT", [P, VC * B * S2])
        ctxT3 = ctxT[:, :].rearrange("p (c t) -> p c t", c=VC)
        cslot = sb("cslot", [P, 4 * DV])

        def transpose_context(tag, ctxT3, cslot, before=None):
            s_c = [sem(f"{tag}_in{i}") for i in range(2)]
            s_tr, s_ev = [sem(f"{tag}_{n}") for n in ("tr", "ev")]
            src = a["ctx_1024"].rearrange("b (t p) d -> p (b t) d", p=P)

            def sync(sp):
                if before:
                    sp.wait_ge(*before)
                for t in range(NC_T // 2):
                    if t >= 2:
                        sp.wait_ge(s_tr, t - 1)
                    sp.dma_start(cslot[:, (t % 2) * 2 * DV:(t % 2 + 1) * 2 * DV].rearrange("p (t d) -> p t d", t=2),
                                 src[:, 2 * t:2 * t + 2, :]).then_inc(s_c[t % 2], 16)

            def tensor(pe):
                pe.wait_ge(s_const, 16)
                for t in range(NC_T // 2):
                    pe.wait_ge(s_c[t % 2], 16 * (t // 2 + 1))
                    if t >= 2:
                        pe.wait_ge(s_ev, t - 1)
                    for c in range(VC):
                        for j in range(2):
                            mm = pe.transpose(banks[4 + t % 2][:, (c * 2 + j) * P:(c * 2 + j + 1) * P],
                                              cslot[:, ((t % 2) * 2 + j) * DV + c * P:((t % 2) * 2 + j) * DV + (c + 1) * P],
                                              ident[:, :])
                    mm.then_inc(s_tr, 1)

            def scalar(act):
                for t in range(NC_T // 2):
                    act.wait_ge(s_tr, t + 1)
                    act.activation(ctxT3[:, :, t * 2 * P:(t + 1) * 2 * P],
                                   banks[4 + t % 2][:, :].rearrange("p (c n) -> p c n", c=VC), ACT.Copy).then_inc(s_ev, 1)

            programs["SP"].append(sync)
            programs["PE"].append(tensor)
            programs["ACT"].append(scalar)
            return s_ev

        s_ctx = transpose_context("c0", ctxT3, cslot)
        s_h0 = layernorm("n0", (s_x, 16), hT3)

        def cross_attention_0():
            NKV, HPG, HD = 8, 2, 128
            UN = B * HPG
            NK = S2 // P
            GW = HPG * HD
            SCALE = 1.0 / float(np.sqrt(HD))
            wk = [sb(f"x_wk{s}", [P, VC, HD]) for s in range(2)]
            wv = [sb(f"x_wv{s}", [P, VC, HD]) for s in range(2)]
            wq = [sb(f"x_wq{s}", [P, KC, GW]) for s in range(2)]
            wo = [sb(f"x_wo{s}", [P, HPG, D]) for s in range(2)]
            kT = [sb(f"x_kT{b}", [P, S2]) for b in range(B)]
            v = [sb(f"x_v{b}", [P, NK, HD]) for b in range(B)]
            qT = [sb(f"x_qT{u}", [P, S]) for u in range(UN)]
            p = [sb(f"x_p{i}", [P, QT, S2]) for i in range(2)]
            pT = sb("x_pT", [P, NK, S])
            oT = [sb(f"x_oT{u}", [P, S]) for u in range(UN)]
            least = sb("x_least", [P, 2 * QT])
            total = sb("x_total", [P, 2 * QT])
            rtotal = sb("x_rtotal", [P, 2 * QT])
            carry = sb("x_carry", [P, 2 * QT])
            mask8 = sb("x_mask8", [P, B * S2], U8)
            mrow8 = sb("x_mrow8", [B * NK, P], U8)
            mrow = sb("x_mrow", [B * NK, P])
            mcol = sb("x_mcol", [P, B * NK])
            lower = sb("x_lower", [P, B * S2])

            use = Use([(f"k{b}{j}", "A") for b in (0,) for j in range(2)] + [("v00", "D"), ("v01", "D"), ("q0", "A"), ("q1", "A")]
                      + [("k10", "A"), ("k11", "A"), ("v10", "D"), ("v11", "D"), ("q2", "A"), ("q3", "A")]
                      + [("o0", "A"), ("o1", "A"), ("o2", "A")] + [(f"w0{t}", "D") for t in range(QT)]
                      + [("o3", "A")] + [(f"w1{t}", "D") for t in range(QT)])
            assert use.total % 2 == 0
            PJ, SC, TR = banks[0:2], pairs[1:3], banks[6:8]
            NS = UN * QT

            s_mask, s_mrow, s_mtr, s_low, s_mcol = [sem(f"x_{n}") for n in ("mask", "mrow", "mtr", "low", "mcol")]
            s_w = [sem(f"x_w{i}") for i in range(2)]
            s_pj, s_pja, s_pjd, s_sc, s_sm, s_ex, s_rt, s_pn, s_tr, s_ta, s_td = [
                sem(f"x_{n}") for n in ("pj", "pja", "pjd", "sc", "sm", "ex", "rt", "pn", "tr", "ta", "td")]
            emptied = {"A": s_pja, "D": s_pjd}
            LOADS = 4

            def load(sp, g, s):
                if isinstance(g, int):
                    c1, c2 = slice(g * HD, (g + 1) * HD), slice(g * GW, (g + 1) * GW)
                else:
                    c1, c2 = bass.ds(g * HD, HD), bass.ds(g * GW, GW)
                sp.dma_start(wk[s][:, :, :], a["L0_xattn_Wk"].rearrange("(c p) n -> p c n", p=P)[:, :, c1]).then_inc(s_w[s], 16)
                sp.dma_start(wv[s][:, :, :], a["L0_xattn_Wv"].rearrange("(c p) n -> p c n", p=P)[:, :, c1]).then_inc(s_w[s], 16)
                sp.dma_start(wq[s][:, :, :], a["L0_xattn_Wq"].rearrange("(c p) n -> p c n", p=P)[:, :, c2]).then_inc(s_w[s], 16)
                sp.dma_start(wo[s][:, :, :], a["L0_xattn_Wo"][c2, :].rearrange("(c p) n -> p c n", p=P)).then_inc(s_w[s], 16)

            def sync(sp):
                m = a["mask_BxS2_bf1"]
                sp.dma_start(mask8[:, :], m.rearrange("b s -> (b s)").partition_broadcast(P)).then_inc(s_mask, 16)
                sp.dma_start(mrow8[:, :], m.rearrange("b (t p) -> (b t) p", p=P)).then_inc(s_mask, 16)
                load(sp, 0, 0)
                load(sp, 1, 1)
                with sp.Fori(0, NKV // 2 - 1) as i:
                    for s in range(2):
                        sp.wait_ge(s_pjd, (i * 2 + s + 2) * use.per["D"])
                        load(sp, i * 2 + (2 + s), s)

            def vector(dve):
                dve.wait_ge(s_mask, 32)
                dve.tensor_scalar(lower[:, :], mask8[:, :], -1.0, BIG, ALU.add, ALU.mult).then_inc(s_low, 1)
                dve.tensor_copy(mrow[:, :], mrow8[:, :]).then_inc(s_mrow, 1)
                dve.wait_ge(s_mtr, 1)
                dve.tensor_copy(mcol[:, :], PJ[0][:, 0:B * NK]).then_inc(s_mcol, 1)
                dve.wait_ge(s_ones, 2)
                dve.memset(scrap[:, 0:1], 0.0).then_inc(s_pjd, use.per["D"])
                dve.memset(scrap[:, 1:2], 0.0).then_inc(s_sm, NS)
                dve.memset(scrap[:, 2:3], 0.0).then_inc(s_td, NS)
                dve.wait_ge(s_low, 1)
                dve.wait_ge(s_mcol, 1)
                dve.wait_ge(s_tgate, 1)

                def body(g):
                    def empty(name):
                        dve.wait_ge(s_pj, use.total * (g + 1) + use.index[name] + 1)
                        return PJ[use.index[name] % 2]

                    def reciprocal(n):
                        if n >= 0:
                            dve.wait_ge(s_ex, NS * g + n + 1)
                        col = slice(n % (2 * QT), n % (2 * QT) + 1)
                        ins = dve.reciprocal(rtotal[:, col], total[:, col]) if n >= 0 else dve.memset(scrap[:, 8 + n % 2:9 + n % 2], 0.0)
                        if n >= 0:
                            ins.then_inc(s_rt, 1)

                    def evacuate(n):
                        if n % QT == 0:
                            before = use.index[f"o{n // QT - 1}"] if n >= QT else use.index[f"o{UN - 1}"] - use.total
                            dve.wait_ge(s_pj, use.total * (g + 1) + before + 1)
                        dve.wait_ge(s_tr, 2 * (NS * (g + 1) + n + 1))
                        q = n % QT
                        dve.tensor_copy(pT[:, NK // 2:, q * P:(q + 1) * P],
                                        TR[1][:, :].rearrange("p (k n) -> p k n", n=P)).then_inc(s_td, 1)

                    def add_out(b):
                        for t in range(QT):
                            o = empty(f"w{b}{t}")
                            xt = x3[:, b * QT + t, :]
                            dve.scalar_tensor_tensor(xt, o[:, :], tgate[:, 0:1], xt, ALU.mult, ALU.add).then_inc(s_pjd, 1)

                    for b in range(B):
                        for j in range(2):
                            o = empty(f"v{b}{j}")
                            k0 = b * NK + j * NK // 2
                            dve.tensor_tensor(v[b][:, j * NK // 2:(j + 1) * NK // 2, :],
                                              o[:, :].rearrange("p (k n) -> p k n", n=HD),
                                              mcol[:, k0:k0 + NK // 2].unsqueeze(2).to_broadcast([P, NK // 2, HD]),
                                              ALU.mult).then_inc(s_pjd, 1)
                    for u in range(UN):
                        for q in range(QT):
                            n = u * QT + q
                            dve.wait_ge(s_sc, NS * g + n + 1)
                            dve.wait_ge(s_tr, 2 * (NS * (g + 1) + n - 2 * QT + 1))
                            reciprocal(n - 2)
                            dve.tensor_tensor_reduce(
                                p[u % 2][:, q, :], SC[n % 2][:, :], lower[:, (u // HPG) * S2:(u // HPG + 1) * S2], -SCALE,
                                3.0e38, ALU.add, ALU.min, least[:, n % (2 * QT):n % (2 * QT) + 1]).then_inc(s_sm, 1)
                            if u >= 1:
                                evacuate(n - QT)
                        if u == UN - 1:
                            reciprocal(NS - 2)
                            reciprocal(NS - 1)
                        if u == UN - 1:
                            add_out(0)
                    for q in range(QT):
                        evacuate(NS - QT + q)
                    add_out(1)

                with dve.Fori(0, NKV) as g:
                    body(g)

            def scalar(act):
                act.wait_ge(s_ones, 2)
                act.activation(scrap[:, 4:5], eps[:, 0:1], ACT.Copy).then_inc(s_pja, use.per["A"])
                act.activation(scrap[:, 5:6], eps[:, 0:1], ACT.Copy).then_inc(s_ta, NS)

                def body(g):
                    def empty(name, dst):
                        act.wait_ge(s_pj, use.total * (g + 1) + use.index[name] + 1)
                        act.activation(dst, PJ[use.index[name] % 2][:, :], ACT.Copy).then_inc(s_pja, 1)

                    def evacuate(n):
                        if n % QT == 0:
                            before = use.index[f"o{n // QT - 1}"] if n >= QT else use.index[f"o{UN - 1}"] - use.total
                            act.wait_ge(s_pj, use.total * (g + 1) + before + 1)
                        act.wait_ge(s_tr, 2 * (NS * (g + 1) + n) + 1)
                        q = n % QT
                        act.activation(pT[:, 0:NK // 2, q * P:(q + 1) * P],
                                       TR[0][:, :].rearrange("p (k n) -> p k n", n=P), ACT.Copy).then_inc(s_ta, 1)

                    for b in range(B):
                        for j in range(2):
                            empty(f"k{b}{j}", kT[b][:, j * BANK:(j + 1) * BANK])
                        for h in range(HPG):
                            empty(f"q{b * HPG + h}", qT[b * HPG + h][:, :])
                    for u in range(UN):
                        for q in range(QT):
                            n = u * QT + q
                            w = n % (2 * QT)
                            if u >= 1:
                                evacuate(n - QT)
                            act.wait_ge(s_sm, NS * (g + 1) + n + 1)
                            act.activation(p[u % 2][:, q, :], p[u % 2][:, q, :], ACT.Exp, scale=-1.0,
                                           bias=least[:, w:w + 1],
                                           accum_out=total[:, w:w + 1]).then_inc(s_ex, 1)
                        if u >= 1:
                            empty(f"o{u - 1}", oT[u - 1][:, :])
                    for q in range(QT):
                        evacuate(NS - QT + q)
                    empty(f"o{UN - 1}", oT[UN - 1][:, :])

                with act.Fori(0, NKV) as g:
                    body(g)

            def gpsimd(pool):
                with pool.Fori(0, NKV) as g:
                    for u in range(UN):
                        for q in range(QT):
                            n = u * QT + q
                            w = n % (2 * QT)
                            pool.wait_ge(s_rt, NS * g + n + 1)
                            pool.tensor_tensor(carry[:, w:w + 1], rtotal[:, w:w + 1], rtotal[:, w:w + 1], ALU.mult)
                            pool.tensor_scalar(p[u % 2][:, q, :], p[u % 2][:, q, :], rtotal[:, w:w + 1], 1.0,
                                               ALU.mult, ALU.mult).then_inc(s_pn, 1)

            def tensor(pe):
                pe.wait_ge(s_h0, NT)
                pe.wait_ge(s_ctx, NC_T // 2)
                pe.wait_ge(s_mrow, 1)
                pe.transpose(PJ[0][:, 0:B * NK], mrow[:, :], ident[0:B * NK, 0:B * NK]).then_inc(s_mtr, 1)
                pe.wait_ge(s_mcol, 1)
                pe.wait_ge(s_pja, 1)
                pe.transpose(PJ[0][:, 0:P], ident[:, :], ident[:, :]).then_inc(s_tr, 2 * NS)
                pe.transpose(PJ[0][:, 0:P], ident[:, :], ident[:, :]).then_inc(s_pj, use.total)

                def body(i, s):
                    g = i * 2 + s

                    def bank(name):
                        n = use.index[name]
                        e, count = use.emptied(n - 2, g) if n >= 2 else use.emptied(use.total + n - 2, g - 1)
                        pe.wait_ge(emptied[e], count)
                        return PJ[n % 2]

                    def transposes(n):
                        u, q = n // QT, n % QT
                        pe.wait_ge(s_pn, NS * g + n + 1)
                        for j, s_free in enumerate((s_ta, s_td)):
                            pe.wait_ge(s_free, NS * (g + 1) + n)
                            for k in range(NK // 2):
                                kk = j * NK // 2 + k
                                mm = pe.transpose(TR[j][:, k * P:(k + 1) * P], p[u % 2][:, q, kk * P:(kk + 1) * P], ident[:, :])
                            mm.then_inc(s_tr, 1)

                    def values(u):
                        o = bank(f"o{u}")
                        pe.wait_ge(s_ta, NS * (g + 1) + (u + 1) * QT)
                        pe.wait_ge(s_td, NS * (g + 1) + (u + 1) * QT)
                        for k in range(NK):
                            mm = pe.matmul(o[:, :], v[u // HPG][:, k, :], pT[:, k, :], start=(k == 0), stop=(k == NK - 1))
                        mm.then_inc(s_pj, 1)

                    def project(b):
                        e, count = use.emptied(use.index[f"o{b * HPG + HPG - 1}"], g)
                        for t in range(QT):
                            o = bank(f"w{b}{t}")
                            if t == 0:
                                pe.wait_ge(emptied[e], count)
                            for h in range(HPG):
                                mm = pe.matmul(o[:, :], oT[b * HPG + h][:, t * P:(t + 1) * P], wo[s][:, h, :],
                                               start=(h == 0), stop=(h == HPG - 1))
                            mm.then_inc(s_pj, 1)

                    pe.wait_ge(s_w[s], 16 * LOADS * (i + 1))
                    for b in range(B):
                        for j in range(2):
                            o = bank(f"k{b}{j}")
                            for c in range(VC):
                                mm = pe.matmul(o[:, :], wk[s][:, c, :],
                                               ctxT3[:, c, b * S2 + j * BANK:b * S2 + (j + 1) * BANK],
                                               start=(c == 0), stop=(c == VC - 1))
                            mm.then_inc(s_pj, 1)
                        for j in range(2):
                            o = bank(f"v{b}{j}")
                            for k in range(NK // 2):
                                tok = b * S2 + (j * NK // 2 + k) * P
                                for c in range(VC):
                                    mm = pe.matmul(o[:, k * HD:(k + 1) * HD], ctxT3[:, c, tok:tok + P], wv[s][:, c, :],
                                                   start=(c == 0), stop=(c == VC - 1))
                            mm.then_inc(s_pj, 1)
                        for h in range(HPG):
                            o = bank(f"q{b * HPG + h}")
                            for c in range(KC):
                                mm = pe.matmul(o[:, :], wq[s][:, c, h * HD:(h + 1) * HD], hT3[:, c, b * S:(b + 1) * S],
                                               start=(c == 0), stop=(c == KC - 1))
                            mm.then_inc(s_pj, 1)
                    pe.wait_ge(s_pja, use.per["A"] * (g + 1) + 8)
                    pe.wait_ge(s_pjd, use.per["D"] * (g + 1) + 4)
                    for u in range(UN):
                        for q in range(QT):
                            n = u * QT + q
                            pe.wait_ge(s_sm, NS * (g + 1) + n - 1)
                            for j in range(2):
                                mm = pe.matmul(SC[n % 2][:, j * BANK:(j + 1) * BANK], qT[u][:, q * P:(q + 1) * P],
                                               kT[u // HPG][:, j * BANK:(j + 1) * BANK], start=True, stop=True)
                            mm.then_inc(s_sc, 1)
                            if u >= 1:
                                transposes(n - QT)
                        if u >= 1:
                            values(u - 1)
                        if u == UN - 1:
                            project(0)
                    for q in range(QT):
                        transposes(NS - QT + q)
                    values(UN - 1)
                    project(1)

                with pe.Fori(0, NKV // 2) as i:
                    for s in range(2):
                        body(i, s)

            programs["SP"].append(sync)
            programs["DVE"].append(vector)
            programs["ACT"].append(scalar)
            programs["POOL"].append(gpsimd)
            programs["PE"].append(tensor)
            return s_pjd, use.per["D"] * (NKV + 1)

        x_done = cross_attention_0()

        def layernorm_to_y(tag, before):
            s_stat, s_mv, s_std, s_rstd, s_y = [sem(f"{tag}_{n}") for n in ("stat", "mv", "std", "rstd", "y")]

            def vector(dve):
                dve.wait_ge(*before)
                for t in range(NT):
                    dve.bn_stats(stats[:, 6 * t:6 * t + 6], x3[:, t, :]).then_inc(s_stat, 1)
                for t in range(NT):
                    dve.wait_ge(s_stat, t + 1)
                    dve.bn_aggr(mv[:, 2 * t:2 * t + 2], stats[:, 6 * t:6 * t + 6]).then_inc(s_mv, 1)
                dve.wait_ge(s_std, 1)
                dve.reciprocal(rstd[:, :], std[:, :]).then_inc(s_rstd, 1)
                dve.wait_ge(s_rstd, 1)
                for t in range(NT):
                    dve.tensor_scalar(y3[:, t, :], x3[:, t, :], mv[:, 2 * t:2 * t + 1], rstd[:, t:t + 1],
                                      ALU.subtract, ALU.mult).then_inc(s_y, 1)

            def scalar(act):
                act.wait_ge(s_mv, NT)
                act.activation(std[:, :], mv[:, :].rearrange("p (t k) -> p t k", k=2)[:, :, 1], ACT.Sqrt,
                               bias=eps[:, 0:1]).then_inc(s_std, 1)

            programs["DVE"].append(vector)
            programs["ACT"].append(scalar)
            return s_y

        def rmsnorm(tag, s_y, y_count, weight, hi, lo=None):
            s_w, s_sq, s_std, s_rstd, s_h, s_tr, s_hi, s_lo = [
                sem(f"{tag}_{n}") for n in ("w", "sq", "std", "rstd", "h", "tr", "hi", "lo")]
            wrow = sb(f"{tag}_wrow", [P, D])
            square = sb(f"{tag}_square", [P, 2 * D])
            sumsq = sb(f"{tag}_sumsq", [P, NT])
            rms = sb(f"{tag}_rms", [P, NT])
            rrms = sb(f"{tag}_rrms", [P, NT])
            s_last = s_hi if lo is None else s_lo

            def sync(sp):
                sp.wait_ge(s_y, y_count(0))
                sp.dma_start(wrow[:, :], a[weight].partition_broadcast(P)).then_inc(s_w, 16)

            def scalar(act):
                for t in range(NT):
                    act.wait_ge(s_y, y_count(t))
                    if t >= 2:
                        act.wait_ge(s_sq, t - 1)
                    act.activation(square[:, (t % 2) * D:(t % 2 + 1) * D], y3[:, t, :], ACT.Square,
                                   accum_out=sumsq[:, t:t + 1]).then_inc(s_sq, 1)
                act.wait_ge(s_sq, NT)
                act.activation(rms[:, :], sumsq[:, :], ACT.Sqrt, scale=1.0 / D, bias=eps[:, 0:1]).then_inc(s_std, 1)
                for t in range(NT):
                    act.wait_ge(s_tr, t + 1)
                    act.activation(hi[:, :, t * P:(t + 1) * P], banks[t % 2][:, :].rearrange("p (c n) -> p c n", c=KC),
                                   ACT.Copy).then_inc(s_hi, 1)

            def vector(dve):
                dve.wait_ge(s_std, 1)
                dve.reciprocal(rrms[:, :], rms[:, :]).then_inc(s_rstd, 1)
                dve.wait_ge(s_rstd, 1)
                dve.wait_ge(s_w, 16)

                def low(t):
                    dve.wait_ge(s_hi, t + 1)
                    part = slice(t * P, (t + 1) * P)
                    dve.tensor_tensor(lo[:, :, part], banks[t % 2][:, :].rearrange("p (c n) -> p c n", c=KC),
                                      hi[:, :, part].bitcast(F32), ALU.subtract).then_inc(s_lo, 1)

                for t in range(NT):
                    if t >= 2:
                        dve.wait_ge(s_tr, t - 1)
                    dve.scalar_tensor_tensor(hslot[:, (t % 2) * D:(t % 2 + 1) * D], y3[:, t, :], rrms[:, t:t + 1],
                                             wrow[:, :], ALU.mult, ALU.mult).then_inc(s_h, 1)
                    if lo is not None and t >= 1:
                        low(t - 1)
                if lo is not None:
                    low(NT - 1)

            def tensor(pe):
                for t in range(NT):
                    pe.wait_ge(s_h, t + 1)
                    if t >= 2:
                        pe.wait_ge(s_last, t - 1)
                    for c in range(KC):
                        mm = pe.transpose(banks[t % 2][:, c * P:(c + 1) * P],
                                          hslot[:, (t % 2) * D + c * P:(t % 2) * D + (c + 1) * P], ident[:, :])
                    mm.then_inc(s_tr, 1)

            programs["SP"].append(sync)
            programs["ACT"].append(scalar)
            programs["DVE"].append(vector)
            programs["PE"].append(tensor)
            return s_last

        phase.close()
        phase = ExitStack()
        y = sb("y", [P, NT * D])
        y3 = y[:, :].rearrange("p (t d) -> p t d", t=NT)
        inner = ExitStack()
        phase, outer = inner, phase
        s_y0 = layernorm_to_y("n1", x_done)
        hTa = sb("hT_attn", [P, KC * T])[:, :].rearrange("p (c t) -> p c t", c=KC)
        s_h1 = rmsnorm("n2", s_y0, lambda t: t + 1, "L0_ffn_ln_w", hTa)

        def self_attention():
            NKV, HPG, HD = 8, 4, 64
            UN = B * HPG
            NP = UN // 2
            PPB = HPG // 2
            GW = HPG * HD
            SCALE = 1.0 / float(np.sqrt(HD))
            wk = [sb(f"s_wk{s}", [P, KC, 2 * HD]) for s in range(2)]
            wv = [sb(f"s_wv{s}", [P, KC, HD]) for s in range(2)]
            wq = [sb(f"s_wq{s}", [P, KC, GW]) for s in range(2)]
            wo = [sb(f"s_wo{s}", [P, PPB, D]) for s in range(2)]
            raw = [[sb(f"s_raw{b}{r}", [P, S]) for r in range(1 + PPB)] for b in range(B)]
            rot = [[sb(f"s_rot{b}{r}", [P, S]) for r in range(1 + PPB)] for b in range(B)]
            turn = [sb(f"s_turn{i}", [P, S]) for i in range(2)]
            v = [sb(f"s_v{b}", [P, QT, HD]) for b in range(B)]
            p = [sb(f"s_p{i}", [P, QT, S]) for i in range(2)]
            pT = [sb(f"s_pT{i}", [P, QT, S]) for i in range(2)]
            oT = [sb(f"s_oT{j}", [P, S]) for j in range(NP)]
            least = sb("s_least", [P, 2 * QT])
            total = sb("s_total", [P, 2 * QT])
            rtotal = sb("s_rtotal", [P, 2 * QT])
            carry = sb("s_carry", [P, 2 * QT])
            causal = sb("s_causal", [P, S])
            cos, sin, swap = sb("s_cos", [P, S]), sb("s_sin", [P, S]), sb("s_swap", [P, P])

            plan = []
            for b in range(B):
                plan += [(f"r{b}0", "A"), (f"r{b}1", "A"), (f"r{b}2", "A"), (f"v{b}", "A"),
                         (f"t{b}0", "D"), (f"t{b}1", "D"), (f"t{b}2", "D")]
            out0 = [(f"w0{t}", "D") for t in range(QT)]
            out1 = [(f"w1{t}", "D") for t in range(QT)]
            plan += [("o0", "A"), ("o1", "A")] + out0 + [("o2", "A"), ("o3", "A")] + out1
            use = Use(plan)
            assert use.total % 2 == 0
            PJ, SC, TR = banks[0:2], banks[2:6], banks[6:8]
            NS = UN * QT
            s_c = sem("s_c")
            s_w = [sem(f"s_w{i}") for i in range(2)]
            s_pj, s_pja, s_pjd, s_rc, s_tn, s_sc, s_sm, s_ex, s_rt, s_pn, s_tr, s_ta, s_td = [
                sem(f"s_{n}") for n in ("pj", "pja", "pjd", "rc", "tn", "sc", "sm", "ex", "rt", "pn", "tr", "ta", "td")]
            emptied = {"A": s_pja, "D": s_pjd}
            LOADS = 5
            NR = B * (1 + PPB)

            def load(sp, g, s):
                if isinstance(g, int):
                    c1, c2 = slice(g * HD, (g + 1) * HD), slice(g * GW, (g + 1) * GW)
                else:
                    c1, c2 = bass.ds(g * HD, HD), bass.ds(g * GW, GW)
                wk_d = a["L0_ffn_wk"].rearrange("(c p) n -> p c n", p=P)[:, :, c1]
                sp.dma_start(wk[s][:, :, 0:HD], wk_d).then_inc(s_w[s], 16)
                sp.dma_start(wk[s][:, :, HD:], wk_d).then_inc(s_w[s], 16)
                sp.dma_start(wv[s][:, :, :], a["L0_ffn_wv"].rearrange("(c p) n -> p c n", p=P)[:, :, c1]).then_inc(s_w[s], 16)
                sp.dma_start(wq[s][:, :, :], a["L0_ffn_wq"].rearrange("(c p) n -> p c n", p=P)[:, :, c2]).then_inc(s_w[s], 16)
                sp.dma_start(wo[s][:, :, :], a["L0_ffn_wo"][c2, :].rearrange("(c p) n -> p c n", p=P)).then_inc(s_w[s], 16)

            def sync(sp):
                for dst, name in ((causal, "c_causal"), (cos, "c_cos"), (sin, "c_sin"), (swap, "c_swap")):
                    sp.dma_start(dst[:, :], a[name]).then_inc(s_c, 16)
                load(sp, 0, 0)
                load(sp, 1, 1)
                with sp.Fori(0, NKV // 2 - 1) as i:
                    for s in range(2):
                        sp.wait_ge(s_pjd, (i * 2 + s + 2) * use.per["D"])
                        load(sp, i * 2 + (2 + s), s)

            def vector(dve):
                dve.wait_ge(s_c, 64)
                dve.memset(scrap[:, 10:11], 0.0).then_inc(s_pjd, use.per["D"])
                dve.memset(scrap[:, 11:12], 0.0).then_inc(s_sm, NS)
                dve.memset(scrap[:, 12:13], 0.0).then_inc(s_td, NS // 2)

                def body(g):
                    def empty(name):
                        dve.wait_ge(s_pj, use.total * (g + 1) + use.index[name] + 1)
                        return PJ[use.index[name] % 2]

                    def reciprocal(n):
                        if n < 0:
                            dve.memset(scrap[:, 16 + n % 2:17 + n % 2], 0.0)
                            return
                        dve.wait_ge(s_ex, NS * g + n + 1)
                        col = slice(n % (2 * QT), n % (2 * QT) + 1)
                        dve.reciprocal(rtotal[:, col], total[:, col]).then_inc(s_rt, 1)

                    def evacuate(n):
                        u, q = n // QT, n % QT
                        if n % 2 == 0:
                            return
                        if q == 1:
                            before = use.index[f"o{u // 2 - 1}"] if u >= 2 else use.index[f"o{NP - 1}"] - use.total
                            dve.wait_ge(s_pj, use.total * (g + 1) + before + 1)
                        dve.wait_ge(s_tr, NS * (g + 1) + n + 1)
                        dve.tensor_copy(pT[u % 2][:, 0:q + 1, q * P:(q + 1) * P],
                                        TR[1][:, 0:(q + 1) * P].rearrange("p (k n) -> p k n", n=P)).then_inc(s_td, 1)

                    def add_out(b):
                        for t in range(QT):
                            o = empty(f"w{b}{t}")
                            yt = y3[:, b * QT + t, :]
                            dve.tensor_tensor(yt, o[:, :], yt, ALU.add).then_inc(s_pjd, 1)

                    for b in range(B):
                        for r in range(1 + PPB):
                            k = b * (1 + PPB) + r
                            o = empty(f"t{b}{r}")
                            dve.tensor_tensor(turn[k % 2][:, :], o[:, :], sin[:, :], ALU.mult).then_inc(s_pjd, 1)
                            dve.wait_ge(s_pjd, use.per["D"] * (g + 1) + use.nth[use.index[f"t{b}{r}"]][1])
                            dve.wait_ge(s_rc, NR * g + k + 1)
                            dve.tensor_tensor(rot[b][r][:, :], rot[b][r][:, :], turn[k % 2][:, :], ALU.add).then_inc(s_tn, 1)
                    for u in range(UN):
                        for q in range(QT):
                            n = u * QT + q
                            dve.wait_ge(s_sc, NS * g + n + 1)
                            dve.wait_ge(s_tr, NS * (g + 1) + n - 2 * QT + 1)
                            reciprocal(n - 2)
                            w = (q + 1) * P
                            dve.tensor_tensor_reduce(
                                p[u % 2][:, q, 0:w], SC[n % 4][:, 0:w], causal[:, S - w:S], -SCALE, 3.0e38, ALU.add, ALU.min,
                                least[:, n % (2 * QT):n % (2 * QT) + 1]).then_inc(s_sm, 1)
                            if u >= 1:
                                evacuate(n - QT)
                        if u == UN - 1:
                            reciprocal(NS - 2)
                            reciprocal(NS - 1)
                        if u == HPG + 1:
                            add_out(0)
                    for q in range(QT):
                        evacuate(NS - QT + q)
                    add_out(1)

                with dve.Fori(0, NKV) as g:
                    body(g)

            def scalar(act):
                act.activation(scrap[:, 20:21], eps[:, 0:1], ACT.Copy).then_inc(s_pja, use.per["A"])
                act.activation(scrap[:, 21:22], eps[:, 0:1], ACT.Copy).then_inc(s_ta, NS // 2)

                def body(g):
                    def empty(name, dst, w=BANK):
                        act.wait_ge(s_pj, use.total * (g + 1) + use.index[name] + 1)
                        src = PJ[use.index[name] % 2][:, 0:w]
                        if len(dst.shape) == 3:
                            src = src.rearrange("p (k n) -> p k n", k=dst.shape[1])
                        act.activation(dst, src, ACT.Copy).then_inc(s_pja, 1)

                    def evacuate(n):
                        u, q = n // QT, n % QT
                        if n % 2 == 1:
                            return
                        if q == 0:
                            before = use.index[f"o{u // 2 - 1}"] if u >= 2 else use.index[f"o{NP - 1}"] - use.total
                            act.wait_ge(s_pj, use.total * (g + 1) + before + 1)
                        act.wait_ge(s_tr, NS * (g + 1) + n + 1)
                        act.activation(pT[u % 2][:, 0:q + 1, q * P:(q + 1) * P],
                                       TR[0][:, 0:(q + 1) * P].rearrange("p (k n) -> p k n", n=P), ACT.Copy).then_inc(s_ta, 1)

                    for b in range(B):
                        for r in range(1 + PPB):
                            empty(f"r{b}{r}", raw[b][r][:, :])
                        empty(f"v{b}", v[b][:, :, :], QT * HD)
                    for u in range(UN):
                        for q in range(QT):
                            n = u * QT + q
                            w = n % (2 * QT)
                            if u >= 1:
                                evacuate(n - QT)
                            act.wait_ge(s_sm, NS * (g + 1) + n + 1)
                            part = p[u % 2][:, q, 0:(q + 1) * P]
                            act.activation(part, part, ACT.Exp, scale=-1.0, bias=least[:, w:w + 1],
                                           accum_out=total[:, w:w + 1]).then_inc(s_ex, 1)
                        if u % 2 == 0 and u >= 2:
                            empty(f"o{u // 2 - 1}", oT[u // 2 - 1][:, :])
                    for q in range(QT):
                        evacuate(NS - QT + q)
                    empty(f"o{NP - 1}", oT[NP - 1][:, :])

                with act.Fori(0, NKV) as g:
                    body(g)

            def gpsimd(pool):
                pool.wait_ge(s_c, 64)
                with pool.Fori(0, NKV) as g:
                    for b in range(B):
                        for r in range(1 + PPB):
                            pool.wait_ge(s_pja, use.per["A"] * (g + 1) + use.nth[use.index[f"r{b}{r}"]][1])
                            pool.tensor_tensor(rot[b][r][:, :], raw[b][r][:, :], cos[:, :], ALU.mult).then_inc(s_rc, 1)
                    for u in range(UN):
                        for q in range(QT):
                            n = u * QT + q
                            w = n % (2 * QT)
                            part = p[u % 2][:, q, 0:(q + 1) * P]
                            pool.wait_ge(s_rt, NS * g + n + 1)
                            pool.tensor_tensor(carry[:, w:w + 1], rtotal[:, w:w + 1], rtotal[:, w:w + 1], ALU.mult)
                            pool.tensor_scalar(part, part, rtotal[:, w:w + 1], 1.0, ALU.mult, ALU.mult).then_inc(s_pn, 1)

            def tensor(pe):
                pe.wait_ge(s_h1, NT)
                pe.wait_ge(s_c, 64)
                pe.wait_ge(s_pja, 1)
                pe.transpose(PJ[0][:, 0:P], ident[:, :], ident[:, :]).then_inc(s_tr, NS)
                pe.transpose(PJ[0][:, 0:P], ident[:, :], ident[:, :]).then_inc(s_pj, use.total)

                def body(i, s):
                    g = i * 2 + s

                    def bank(name):
                        n = use.index[name]
                        e, count = use.emptied(n - 2, g) if n >= 2 else use.emptied(use.total + n - 2, g - 1)
                        pe.wait_ge(emptied[e], count)
                        return PJ[n % 2]

                    def transposes(n):
                        u, q = n // QT, n % QT
                        pe.wait_ge(s_pn, NS * g + n + 1)
                        pe.wait_ge((s_ta, s_td)[n % 2], NS // 2 * (g + 1) + n // 2)
                        for k in range(q + 1):
                            mm = pe.transpose(TR[n % 2][:, k * P:(k + 1) * P], p[u % 2][:, q, k * P:(k + 1) * P], ident[:, :])
                        mm.then_inc(s_tr, 1)

                    def values(j):
                        o = bank(f"o{j}")
                        pe.wait_ge(s_ta, NS // 2 * (g + 1) + (j + 1) * QT)
                        pe.wait_ge(s_td, NS // 2 * (g + 1) + (j + 1) * QT)
                        for h in range(2):
                            for k in range(QT):
                                mm = pe.matmul(o[h * HD:(h + 1) * HD, k * P:], v[j // PPB][:, k, :], pT[h][:, k, k * P:],
                                               start=(k == 0), stop=(k == QT - 1))
                        mm.then_inc(s_pj, 1)

                    def project(b):
                        e, count = use.emptied(use.index[f"o{b * PPB + PPB - 1}"], g)
                        for t in range(QT):
                            o = bank(f"w{b}{t}")
                            if t == 0:
                                pe.wait_ge(emptied[e], count)
                            for j in range(PPB):
                                mm = pe.matmul(o[:, :], oT[b * PPB + j][:, t * P:(t + 1) * P], wo[s][:, j, :],
                                               start=(j == 0), stop=(j == PPB - 1))
                            mm.then_inc(s_pj, 1)

                    pe.wait_ge(s_w[s], 16 * LOADS * (i + 1))
                    for b in range(B):
                        for r in range(1 + PPB):
                            o = bank(f"r{b}{r}")
                            w = wk[s][:, :, :] if r == 0 else wq[s][:, :, (r - 1) * P:r * P]
                            for c in range(KC):
                                mm = pe.matmul(o[:, :], w[:, c, :], hTa[:, c, b * S:(b + 1) * S],
                                               start=(c == 0), stop=(c == KC - 1))
                            mm.then_inc(s_pj, 1)
                        o = bank(f"v{b}")
                        for k in range(QT):
                            for c in range(KC):
                                mm = pe.matmul(o[:, k * HD:(k + 1) * HD], hTa[:, c, b * S + k * P:b * S + (k + 1) * P],
                                               wv[s][:, c, :], start=(c == 0), stop=(c == KC - 1))
                        mm.then_inc(s_pj, 1)
                        for r in range(1 + PPB):
                            e, count = use.emptied(use.index[f"r{b}{r}"], g)
                            o = bank(f"t{b}{r}")
                            pe.wait_ge(emptied[e], count)
                            pe.matmul(o[:, :], swap[:, :], raw[b][r][:, :], start=True, stop=True).then_inc(s_pj, 1)
                    pe.wait_ge(s_pja, use.per["A"] * (g + 1) + 2 * (2 + PPB))
                    pe.wait_ge(s_tn, NR * (g + 1))
                    for u in range(UN):
                        b, pair, half = u // HPG, (u % HPG) // 2, u % 2
                        rows = slice(half * HD, (half + 1) * HD)
                        for q in range(QT):
                            n = u * QT + q
                            pe.wait_ge(s_sm, NS * (g + 1) + n - 3)
                            pe.matmul(SC[n % 4][:, 0:(q + 1) * P], rot[b][1 + pair][rows, q * P:(q + 1) * P],
                                      rot[b][0][rows, 0:(q + 1) * P], start=True, stop=True).then_inc(s_sc, 1)
                            if u >= 1:
                                transposes(n - QT)
                        if u % 2 == 0 and u >= 2:
                            values(u // 2 - 1)
                        if u == HPG + 1:
                            project(0)
                    for q in range(QT):
                        transposes(NS - QT + q)
                    values(NP - 1)
                    project(1)

                with pe.Fori(0, NKV // 2) as i:
                    for s in range(2):
                        body(i, s)

            programs["SP"].append(sync)
            programs["DVE"].append(vector)
            programs["ACT"].append(scalar)
            programs["POOL"].append(gpsimd)
            programs["PE"].append(tensor)
            return s_pjd, use.per["D"] * (NKV + 1)

        y_done = self_attention()
        inner.close()
        phase = outer

        ACCURATE = ((0, 0), (1, 0), (0, 1))
        NE, TOPK, HID = 16, 4, 512
        HC = HID // P
        hh = [sb(f"m_h{i}", [P, KC, T], F32R) for i in range(2)]
        gate = sb("m_gate", [P, NE, NT])
        moe_small = ExitStack()
        phase, outer = moe_small, phase
        s_h2 = rmsnorm("n3", y_done[0], lambda t: y_done[1], "L0_ffn_ff_ln_w", hh[0], hh[1])

        def route():
            wg = sb("r_wg", [P, KC, NE])
            wgs = [sb(f"r_wg{i}", [P, KC, NE], F32R) for i in range(2)]
            logit = sb("r_logit", [P, NT, NE])
            top = sb("r_top", [P, NT, 8])
            low = sb("r_low", [P, NT])
            rest = sb("r_rest", [P, NT, NE])
            chosen = sb("r_chosen", [P, NT, NE])
            total = sb("r_total", [P, NT])
            rtotal = sb("r_rtotal", [P, NT])
            s_w, s_hi, s_lo, s_l, s_pick, s_ch, s_ex, s_gate = [
                sem(f"r_{n}") for n in ("w", "hi", "lo", "l", "pick", "ch", "ex", "gate")]

            def sync(sp):
                sp.dma_start(wg[:, :, :], a["L0_ffn_wg"].rearrange("(c p) n -> p c n", p=P)).then_inc(s_w, 16)

            def scalar(act):
                act.wait_ge(s_w, 16)
                act.activation(wgs[0][:, :, :], wg[:, :, :], ACT.Copy).then_inc(s_hi, 1)
                act.wait_ge(s_ch, NT + 3)
                act.activation(logit[:, :, :], logit[:, :, :], ACT.Exp).then_inc(s_ex, 1)

            def tensor(pe):
                pe.wait_ge(s_lo, 1)
                pe.wait_ge(s_h2, NT)
                for t in range(NT):
                    for n, (i, j) in enumerate(ACCURATE):
                        for c in range(KC):
                            mm = pe.matmul(banks[2][:, t * NE:(t + 1) * NE], hh[i][:, c, t * P:(t + 1) * P], wgs[j][:, c, :],
                                           start=(n == 0 and c == 0), stop=(n == 2 and c == KC - 1))
                mm.then_inc(s_l, 1)

            def vector(dve):
                steps = 0

                def step(ins):
                    nonlocal steps
                    steps += 1
                    ins.then_inc(s_ch, 1)
                    dve.wait_ge(s_ch, steps)

                dve.wait_ge(s_hi, 1)
                dve.tensor_tensor(wgs[1][:, :, :], wg[:, :, :], wgs[0][:, :, :].bitcast(F32), ALU.subtract).then_inc(s_lo, 1)
                dve.wait_ge(s_l, 1)
                dve.tensor_copy(logit[:, :, :], banks[2][:, 0:NT * NE].rearrange("p (t e) -> p t e", e=NE)).then_inc(s_pick, 1)
                dve.wait_ge(s_pick, 1)
                for t in range(NT):
                    ins = dve.max(top[:, t, :], logit[:, t, :])
                    ins.then_inc(s_ch, 1)
                steps = NT
                dve.wait_ge(s_ch, NT)
                step(dve.tensor_copy(low[:, :], top[:, :, 0]))
                step(dve.memset(top[:, :, TOPK:], 3.0e38))
                for t in range(NT):
                    dve.match_replace(rest[:, t, :], top[:, t, :], logit[:, t, :], -3.0e38).then_inc(s_pick, 1)
                dve.wait_ge(s_pick, NT + 1)
                dve.tensor_tensor(chosen[:, :, :], logit[:, :, :], rest[:, :, :], ALU.not_equal).then_inc(s_pick, 1)
                dve.wait_ge(s_pick, NT + 2)
                step(dve.tensor_tensor(logit[:, :, :], logit[:, :, :], low[:, :].unsqueeze(2).to_broadcast([P, NT, NE]), ALU.subtract))
                dve.wait_ge(s_ex, 1)
                step(dve.tensor_tensor(logit[:, :, :], logit[:, :, :], chosen[:, :, :], ALU.mult))
                step(dve.tensor_reduce(total[:, :], logit[:, :, :], AX.X, ALU.add))
                step(dve.reciprocal(rtotal[:, :], total[:, :]))
                dve.tensor_tensor(gate[:, :, :].rearrange("p e t -> p t e"), logit[:, :, :],
                                  rtotal[:, :].unsqueeze(2).to_broadcast([P, NT, NE]), ALU.mult).then_inc(s_gate, 1)

            programs["SP"].append(sync)
            programs["ACT"].append(scalar)
            programs["PE"].append(tensor)
            programs["DVE"].append(vector)
            return s_gate

        s_gated = route()
        moe_small.close()
        phase = outer

        def experts():
            NH = T // BANK
            TPH = NT // NH
            NS = NH * HC
            raw = [sb(f"e_raw{i}", [P, KC, HID]) for i in range(2)]
            w1 = [[sb(f"e_w1{s}{i}", [P, KC, HID], F32R) for i in range(2)] for s in range(2)]
            w3 = [[sb(f"e_w3{s}{i}", [P, KC, HID], F32R) for i in range(2)] for s in range(2)]
            w2 = [sb(f"e_w2{i}", [P, HC, D], F32R) for i in range(2)]
            silu = [sb(f"e_silu{i}", [P, BANK]) for i in range(2)]
            act32 = [sb(f"e_act{i}", [P, BANK]) for i in range(2)]
            aT = [[sb(f"e_aT{h}{i}", [P, HC, BANK], F32R) for i in range(2)] for h in range(NH)]
            GU, Y = pairs[0:2], banks[4:6]
            s_in = [sem(f"e_in{i}") for i in range(2)]
            s_hi, s_lo, s_gu, s_sg, s_a, s_ah, s_al, s_y, s_yd = [
                sem(f"e_{n}") for n in ("hi", "lo", "gu", "sg", "a", "ah", "al", "y", "yd")]
            NW = 3 * NE

            def load(sp, n, e, kind):
                if not isinstance(e, int):
                    src = a[f"L0_ffn_{kind}"][bass.ds(e, 1), :, :].rearrange("e (c p) n -> p (e c) n", p=P)
                else:
                    src = a[f"L0_ffn_{kind}"][e].rearrange("(c p) n -> p c n", p=P)
                sp.dma_start(raw[n % 2][:, :, :], src).then_inc(s_in[n % 2], 16)

            def sync(sp):
                sp.wait_ge(s_gated, 1)
                load(sp, 0, 0, "w1")
                load(sp, 1, 0, "w3")

                def body(i, s, last):
                    e = i * 2 + s
                    for k, kind in enumerate(("w2", "w1", "w3")):
                        if last and k:
                            continue
                        sp.wait_ge(s_lo, 3 * e + k + 1)
                        load(sp, 3 * s + k, e + (1 if k else 0), kind)

                with sp.Fori(0, NE // 2 - 1) as i:
                    for s in range(2):
                        body(i, s, False)
                body(NE // 2 - 1, 0, False)
                body(NE // 2 - 1, 1, True)

            def scalar(act):
                def high(dst, n_in, parity):
                    act.wait_ge(s_in[parity], n_in)
                    act.activation(dst[:, :, :], raw[parity][:, :, :], ACT.Copy).then_inc(s_hi, 1)

                act.wait_ge(s_gated, 1)
                high(w1[0][0], 16, 0)
                high(w3[0][0], 16, 1)

                def body(i, s, last):
                    e = i * 2 + s

                    def part_high(k):
                        act.wait_ge(s_a, NS * (e + 1) + k + 1)
                        act.activation(aT[k // HC][0][:, k % HC, :], act32[k % 2][:, :], ACT.Copy).then_inc(s_ah, 1)

                    act.wait_ge(s_y, NS * (e + 1))
                    high(w2[0], 16 * (3 * i + (1 if s == 0 else 3)) + (0 if s else 16), s)
                    for k in range(NS):
                        act.wait_ge(s_gu, NS * (e + 1) + k + 1)
                        act.activation(silu[k % 2][:, :], GU[k % 2][:, 0:BANK], ACT.Silu).then_inc(s_sg, 1)
                        if k >= 1:
                            part_high(k - 1)
                        if not last and k in (2, 5):
                            m = 3 * s + (1 if k == 2 else 2)
                            high((w1 if k == 2 else w3)[1 - s][0], 16 * (3 * i + 1 + m // 2 + 1), m % 2)
                    part_high(NS - 1)

                with act.Fori(0, NE // 2 - 1) as i:
                    for s in range(2):
                        body(i, s, False)
                body(NE // 2 - 1, 0, False)
                body(NE // 2 - 1, 1, True)

            def gpsimd(pool):
                def low(dst, n, parity):
                    pool.wait_ge(s_hi, n)
                    pool.tensor_tensor(dst[1][:, :, :], raw[parity][:, :, :], dst[0][:, :, :].bitcast(F32),
                                       ALU.subtract).then_inc(s_lo, 1)

                low(w1[0], 1, 0)
                low(w3[0], 2, 1)

                def body(i, s, last):
                    e = i * 2 + s
                    low(w2, 3 * e + 3, s)
                    if not last:
                        low(w1[1 - s], 3 * e + 4, (3 * s + 1) % 2)
                        low(w3[1 - s], 3 * e + 5, (3 * s + 2) % 2)

                with pool.Fori(0, NE // 2 - 1) as i:
                    for s in range(2):
                        body(i, s, False)
                body(NE // 2 - 1, 0, False)
                body(NE // 2 - 1, 1, True)

            def vector(dve):
                dve.wait_ge(s_gated, 1)
                dve.memset(scrap[:, 24:25], 0.0).then_inc(s_a, NS)
                dve.memset(scrap[:, 25:26], 0.0).then_inc(s_yd, NT)

                def body(i, s):
                    e = i * 2 + s

                    def part_low(k):
                        dve.wait_ge(s_ah, NS * e + k + 1)
                        dve.tensor_tensor(aT[k // HC][1][:, k % HC, :], act32[k % 2][:, :],
                                          aT[k // HC][0][:, k % HC, :].bitcast(F32), ALU.subtract).then_inc(s_al, 1)

                    for k in range(NS):
                        if k >= 2:
                            dve.wait_ge(s_al, NS * e + k - 1)
                        dve.wait_ge(s_sg, NS * e + k + 1)
                        dve.tensor_tensor(act32[k % 2][:, :], silu[k % 2][:, :], GU[k % 2][:, BANK:], ALU.mult).then_inc(s_a, 1)
                        if k >= 1:
                            part_low(k - 1)
                    part_low(NS - 1)
                    for t in range(NT):
                        dve.wait_ge(s_y, NS * (e + 1) + t + 1)
                        yt = y3[:, t, :]
                        g = gate[:, :, :].rearrange("p e t -> p (e t)")[:, bass.ds(e * NT + t, 1)]
                        dve.scalar_tensor_tensor(yt, Y[t % 2][:, :], g, yt, ALU.mult, ALU.add).then_inc(s_yd, 1)

                with dve.Fori(0, NE // 2) as i:
                    for s in range(2):
                        body(i, s)

            def tensor(pe):
                pe.wait_ge(s_gated, 1)
                pe.transpose(banks[6][:, 0:P], ident[:, :], ident[:, :]).then_inc(s_gu, NS)
                pe.transpose(banks[6][:, 0:P], ident[:, :], ident[:, :]).then_inc(s_y, NS)

                def body(i, s):
                    e = i * 2 + s
                    for k in range(NS):
                        h, m = k // HC, k % HC
                        if k == 0:
                            pe.wait_ge(s_lo, 3 * e + 2)
                        pe.wait_ge(s_a, NS * (e + 1) + k - 1)
                        for j, w in enumerate((w1[s], w3[s])):
                            for n, (x0, x1) in enumerate(ACCURATE):
                                for c in range(KC):
                                    mm = pe.matmul(GU[k % 2][:, j * BANK:(j + 1) * BANK], w[x0][:, c, m * P:(m + 1) * P],
                                                   hh[x1][:, c, h * BANK:(h + 1) * BANK],
                                                   start=(n == 0 and c == 0), stop=(n == 2 and c == KC - 1))
                        mm.then_inc(s_gu, 1)
                    pe.wait_ge(s_lo, 3 * e + 3)
                    for t in range(NT):
                        h = t // TPH
                        if t % TPH == 0:
                            pe.wait_ge(s_al, NS * e + (h + 1) * HC)
                        pe.wait_ge(s_yd, NT * (e + 1) + t - 1)
                        for n, (x0, x1) in enumerate(ACCURATE):
                            for m in range(HC):
                                mm = pe.matmul(Y[t % 2][:, :], aT[h][x0][:, m, (t % TPH) * P:(t % TPH + 1) * P], w2[x1][:, m, :],
                                               start=(n == 0 and m == 0), stop=(n == 2 and m == HC - 1))
                        mm.then_inc(s_y, 1)

                with pe.Fori(0, NE // 2) as i:
                    for s in range(2):
                        body(i, s)

            programs["SP"].append(sync)
            programs["ACT"].append(scalar)
            programs["POOL"].append(gpsimd)
            programs["DVE"].append(vector)
            programs["PE"].append(tensor)
            return s_yd, NT * (NE + 1)

        moe_done = experts()

        s_x1 = sem("s_x1")

        def add_inner(dve):
            dve.wait_ge(*moe_done)
            for t in range(NT):
                dve.scalar_tensor_tensor(x3[:, t, :], y3[:, t, :], tgate[:, 2:3], x3[:, t, :], ALU.mult, ALU.add).then_inc(s_x1, 1)

        programs["DVE"].append(add_inner)
        phase.close()
        phase = ExitStack()

        xT3 = sb("hT_x1", [P, KC * T])[:, :].rearrange("p (c t) -> p c t", c=KC)
        cxT3 = sb("ctxT1", [P, VC * B * S2])[:, :].rearrange("p (c t) -> p c t", c=VC)
        cslot1 = sb("cslot1", [P, 4 * DV])
        s_ctx1 = transpose_context("c1", cxT3, cslot1, (s_x1, 1))
        s_h3 = layernorm("n4", (s_x1, NT), xT3)

        def cross_attention_1():
            HD, HPG, NG = 32, 4, 4
            DCA = 16
            GW = HPG * HD
            UN = B * HPG
            NK = S2 // P
            MAIN = S2 - DCA
            SCALE = 1.0 / float(np.sqrt(HD))
            wq = sb("z_wq", [P, KC, GW])
            wkv = sb("z_wkv", [P, VC, 2 * GW])
            wd = sb("z_wd", [P, VC, 2 * GW])
            wo = sb("z_wo", [P, D])
            bq, bkv, bd = sb("z_bq", [P, GW]), sb("z_bkv", [P, 2 * GW]), sb("z_bd", [P, 2 * GW])
            norms = sb("z_norms", [P, 6])
            qnorm = sb("z_qnorm", [P, 2])
            bo, tbo = sb("z_bo", [P, D]), sb("z_tbo", [P, D])
            part = sb("z_part", [P, 2])
            kv = sb("z_kv", [P, NC_T, HPG, 2 * HD])
            dkv = sb("z_dkv", [P, B, 2 * GW])
            qr = sb("z_qr", [P, NT, GW])
            GQ, GK, GD = NT * HPG, NC_T * HPG, B * HPG
            NB = (GQ + GK + GD) // HPG
            cen = sb("z_cen", [P, GQ + GK + GD, HD])
            sq = sb("z_sq", [P, GQ + GK + GD, HD])
            mean = sb("z_mean", [P, GQ + GK + GD])
            var = sb("z_var", [P, GQ + GK + GD])
            dev = sb("z_dev", [P, GQ + GK + GD])
            rdev = sb("z_rdev", [P, GQ + GK + GD])
            dv = sb("z_dv", [P, B, GW])
            qT = sb("z_qT", [P, T])
            kT = sb("z_kT", [P, B * S2])
            p = [sb(f"z_p{i}", [P, QT, S2]) for i in range(2)]
            pT = sb("z_pT", [P, NK, S])
            oT = [sb(f"z_oT{b}", [P, S]) for b in range(B)]
            most = sb("z_most", [P, 2 * QT, 2])
            total = sb("z_total", [P, 2 * QT, 2])
            rtotal = sb("z_rtotal", [P, 2 * QT, 2])
            carry = sb("z_carry", [P, 2 * QT])

            plan = [(f"kv{n}", "D") for n in range(NC_T // 2)] + [("d", "D"), ("q0", "D"), ("q1", "D")]
            plan += [("tq0", "A"), ("tq1", "A"), ("tk0", "A"), ("tk1", "A"), ("tk2", "A"), ("tk3", "A"), ("td", "A")]
            plan += [("o0", "A")] + [(f"w0{t}", "D") for t in range(QT)] + [("o1", "A")] + [(f"w1{t}", "D") for t in range(QT)]
            use = Use(plan)
            assert use.total % 2 == 0
            PJ, SC, TR = banks[0:2], pairs[1:3], banks[6:8]
            NS = UN * QT
            s_c, s_qn, s_tbo, s_w, s_wo = sem("z_c"), sem("z_qn"), sem("z_tbo"), sem("z_w"), sem("z_wo")
            s_pj, s_pja, s_pjd, s_ch, s_sq, s_dev, s_cen, s_val, s_sc, s_sm, s_ex, s_rt, s_pn, s_tr, s_ta, s_td = [
                sem(f"z_{n}") for n in ("pj", "pja", "pjd", "ch", "sq", "dev", "cen", "val", "sc", "sm", "ex", "rt",
                                        "pn", "tr", "ta", "td")]
            emptied = {"A": s_pja, "D": s_pjd}
            NPROJ = NC_T // 2 + 3
            STEPS = 6

            def read(engine, j, u):
                b, h = u // HPG, u % HPG
                if h == HPG - 1:
                    engine.wait_ge(s_pj, use.total * (j + 1) + use.index[f"o{b}"] + 1)
                else:
                    engine.wait_ge(s_val, (HPG - 1) * (B * j + b) + h + 1)

            def sync(sp):
                sp.wait_ge(s_x1, NT)
                for k, name in enumerate(("qn_w", "qn_b", "kn_w", "kn_b", "kn_dca_w", "kn_dca_b")):
                    for h in range(HPG):
                        sp.dma_start(norms[h * HD:(h + 1) * HD, k:k + 1],
                                     a[f"L1_xattn_{name}"].rearrange("(p o) -> p o", o=1)).then_inc(s_c, 16)
                sp.dma_start(bo[:, :], a["L1_xattn_bo"].partition_broadcast(P)).then_inc(s_c, 16)
                sp.dma_start(part[:, :], a["c_part"]).then_inc(s_c, 16)

                def load(j):
                    one = slice(0, GW) if isinstance(j, int) else bass.ds(j * GW, GW)
                    two = slice(0, 2 * GW) if isinstance(j, int) else bass.ds(j * 2 * GW, 2 * GW)
                    val = slice(D, D + GW) if isinstance(j, int) else bass.ds(j * GW + D, GW)
                    wd_d = a["L1_xattn_Wkv_dca"].rearrange("(c p) n -> p c n", p=P)
                    sp.dma_start(wq[:, :, :], a["L1_xattn_Wq"].rearrange("(c p) n -> p c n", p=P)[:, :, one]).then_inc(s_w, 16)
                    sp.dma_start(wkv[:, :, :], a["wkv"].rearrange("(c p) n -> p c n", p=P)[:, :, two]).then_inc(s_w, 16)
                    sp.dma_start(wd[:, :, 0:GW], wd_d[:, :, one]).then_inc(s_w, 16)
                    sp.dma_start(wd[:, :, GW:], wd_d[:, :, val]).then_inc(s_w, 16)
                    sp.dma_start(bq[:, :], a["L1_xattn_bq"][one].partition_broadcast(P)).then_inc(s_w, 16)
                    sp.dma_start(bkv[:, :], a["bkv"][two].partition_broadcast(P)).then_inc(s_w, 16)
                    sp.dma_start(bd[:, 0:GW], a["L1_xattn_bkv_dca"][one].partition_broadcast(P)).then_inc(s_w, 16)
                    sp.dma_start(bd[:, GW:], a["L1_xattn_bkv_dca"][val].partition_broadcast(P)).then_inc(s_w, 16)

                def load_out(j):
                    one = slice(0, GW) if isinstance(j, int) else bass.ds(j * GW, GW)
                    sp.dma_start(wo[:, :], a["L1_xattn_Wo"][one, :]).then_inc(s_wo, 16)

                load(0)
                load_out(0)
                with sp.Fori(0, NG - 1) as j:
                    sp.wait_ge(s_pjd, use.per["D"] * (j + 1) + NPROJ)
                    load(j + 1)
                    sp.wait_ge(s_pjd, use.per["D"] * (j + 2))
                    load_out(j + 1)

            def vector(dve):
                dve.wait_ge(s_c, 16 * (6 * HPG + 2))
                dve.tensor_scalar(qnorm[:, :], norms[:, 0:2], SCALE, None, ALU.mult).then_inc(s_qn, 1)
                dve.tensor_scalar(tbo[:, :], bo[:, :], tgate[:, 1:2], None, ALU.mult).then_inc(s_tbo, 1)
                dve.memset(scrap[:, 28:29], 0.0).then_inc(s_pjd, use.per["D"])
                dve.memset(scrap[:, 29:30], 0.0).then_inc(s_td, NS)

                def body(j):
                    steps = 0

                    def step(ins):
                        nonlocal steps
                        steps += 1
                        ins.then_inc(s_ch, 1)
                        dve.wait_ge(s_ch, STEPS * j + steps)

                    def empty(name):
                        dve.wait_ge(s_pj, use.total * (j + 1) + use.index[name] + 1)
                        return PJ[use.index[name] % 2]

                    def reciprocal(n):
                        dve.wait_ge(s_ex, 2 * (NS * (j + 1) + n + 1))
                        w = n % (2 * QT)
                        dve.reciprocal(rtotal[:, w, :], total[:, w, :]).then_inc(s_rt, 1)

                    def evacuate(n):
                        if n % QT == 0 and n:
                            read(dve, j, n // QT - 1)
                        dve.wait_ge(s_tr, 2 * (NS * (j + 1) + n + 1))
                        q = n % QT
                        dve.tensor_copy(pT[:, NK // 2:, q * P:(q + 1) * P],
                                        TR[1][:, :].rearrange("p (k n) -> p k n", n=P)).then_inc(s_td, 1)

                    def add_out(b, t):
                        o = empty(f"w{b}{t}")
                        xt = x3[:, b * QT + t, :]
                        dve.scalar_tensor_tensor(xt, o[:, :], tgate[:, 1:2], xt, ALU.mult, ALU.add).then_inc(s_pjd, 1)

                    dve.wait_ge(s_w, 16 * 8 * (j + 1))
                    for n in range(NC_T // 2):
                        o = empty(f"kv{n}")
                        dve.tensor_tensor(kv[:, 2 * n:2 * n + 2, :, :].rearrange("p t h d -> p t (h d)"),
                                          o[:, :].rearrange("p (t d) -> p t d", t=2),
                                          bkv[:, :].unsqueeze(1).to_broadcast([P, 2, 2 * GW]), ALU.add).then_inc(s_pjd, 1)
                    o = empty("d")
                    dve.tensor_tensor(dkv[:, :, :], o[:, :].rearrange("p (t d) -> p t d", t=B),
                                      bd[:, :].unsqueeze(1).to_broadcast([P, B, 2 * GW]), ALU.add).then_inc(s_pjd, 1)
                    for n in range(2):
                        o = empty(f"q{n}")
                        dve.tensor_tensor(qr[:, 4 * n:4 * n + 4, :], o[:, :].rearrange("p (t d) -> p t d", t=4),
                                          bq[:, :].unsqueeze(1).to_broadcast([P, 4, GW]), ALU.add).then_inc(s_pjd, 1)
                    dve.wait_ge(s_pjd, use.per["D"] * (j + 1) + NPROJ)
                    rows = ((qr[:, :, :].rearrange("p t (h d) -> p (t h) d", d=HD), slice(0, GQ)),
                            (kv[:, :, :, 0:HD].rearrange("p t h d -> p (t h) d"), slice(GQ, GQ + GK)),
                            (dkv[:, :, 0:GW].rearrange("p t (h d) -> p t h d", d=HD), slice(GQ + GK, GQ + GK + GD)))
                    for n, (src, g) in enumerate(rows):
                        o = mean[:, g]
                        if n == 2:
                            o = o.rearrange("p (t h) -> p t h", t=B)
                        ins = dve.tensor_reduce(o, src, AX.X, ALU.add)
                        if n < 2:
                            ins.then_inc(s_cen, 1)
                    step(ins)
                    dve.wait_ge(s_cen, 6 * j + 2)
                    step(dve.tensor_scalar(mean[:, :], mean[:, :], 1.0 / HD, None, ALU.mult))
                    for n, (src, g) in enumerate(rows):
                        m, o = mean[:, g], cen[:, g, :]
                        if n == 2:
                            m = m.rearrange("p (t h) -> p t h", t=B).unsqueeze(3).to_broadcast([P, B, HPG, HD])
                            o = o.rearrange("p (t h) d -> p t h d", t=B)
                        else:
                            m = m.unsqueeze(2).to_broadcast(list(src.shape))
                        dve.tensor_tensor(o, src, m, ALU.subtract).then_inc(s_cen, 1)
                    dve.wait_ge(s_sq, j + 1)
                    step(dve.tensor_reduce(var[:, :], sq[:, :, :], AX.X, ALU.add))
                    dve.wait_ge(s_dev, j + 1)
                    step(dve.reciprocal(rdev[:, :], dev[:, :]))
                    dve.tensor_tensor(cen[:, :, :], cen[:, :, :], rdev[:, :].unsqueeze(2).to_broadcast(list(cen[:, :, :].shape)),
                                      ALU.mult).then_inc(s_cen, 1)
                    step(dve.tensor_scalar(dv[:, :, :], dkv[:, :, GW:], part[:, 1:2], None, ALU.mult))
                    for b in range(B):
                        vt = kv[:, (b + 1) * NK - 1, :, HD:]
                        ins = dve.scalar_tensor_tensor(vt, vt, part[:, 0:1], dv[:, b, :].rearrange("p (h d) -> p h d", d=HD),
                                                       ALU.mult, ALU.add)
                    step(ins)
                    assert steps == STEPS
                    for u in range(UN):
                        for q in range(QT):
                            n = u * QT + q
                            w = n % (2 * QT)
                            dve.wait_ge(s_sc, NS * j + n + 1)
                            dve.tensor_reduce(most[:, w, 0:1], SC[n % 2][:, 0:MAIN], AX.X, ALU.max, negate=True)
                            dve.tensor_reduce(most[:, w, 1:2], SC[n % 2][:, MAIN:], AX.X, ALU.max, negate=True).then_inc(s_sm, 1)
                            if n >= 1:
                                reciprocal(n - 1)
                            if u >= 1:
                                evacuate(n - QT)
                            if u == HPG + 1:
                                add_out(0, q)
                    reciprocal(NS - 1)
                    for q in range(QT):
                        evacuate(NS - QT + q)
                    for q in range(QT):
                        add_out(1, q)

                with dve.Fori(0, NG) as j:
                    body(j)
                dve.wait_ge(s_pjd, use.per["D"] * (NG + 1))
                for t in range(NT):
                    dve.tensor_tensor(x3[:, t, :], x3[:, t, :], tbo[:, :], ALU.add).then_inc(s_tbo, 1)

            def scalar(act):
                act.wait_ge(s_qn, 1)
                act.activation(scrap[:, 32:33], eps[:, 0:1], ACT.Copy).then_inc(s_pja, use.per["A"])
                act.activation(scrap[:, 33:34], eps[:, 0:1], ACT.Copy).then_inc(s_ta, NS)
                act.activation(scrap[:, 34:35], eps[:, 0:1], ACT.Copy).then_inc(s_ex, 2 * NS)

                def body(j):
                    def filled(name):
                        act.wait_ge(s_pj, use.total * (j + 1) + use.index[name] + 1)
                        return PJ[use.index[name] % 2]

                    def evacuate(n):
                        if n % QT == 0 and n:
                            read(act, j, n // QT - 1)
                        act.wait_ge(s_tr, 2 * (NS * (j + 1) + n) + 1)
                        q = n % QT
                        act.activation(pT[:, 0:NK // 2, q * P:(q + 1) * P],
                                       TR[0][:, :].rearrange("p (k n) -> p k n", n=P), ACT.Copy).then_inc(s_ta, 1)

                    act.wait_ge(s_cen, 6 * j + 5)
                    act.activation(sq[:, :, :], cen[:, :, :], ACT.Square).then_inc(s_sq, 1)
                    act.wait_ge(s_ch, STEPS * j + 3)
                    act.activation(dev[:, :], var[:, :], ACT.Sqrt, scale=1.0 / HD, bias=eps[:, 1:2]).then_inc(s_dev, 1)
                    for n in range(2):
                        act.activation(qT[:, n * BANK:(n + 1) * BANK], filled(f"tq{n}")[:, :], ACT.Identity,
                                       scale=qnorm[:, 0:1], bias=qnorm[:, 1:2]).then_inc(s_pja, 1)
                    for n in range(4):
                        w = BANK - DCA if n % 2 else BANK
                        act.activation(kT[:, n * BANK:n * BANK + w], filled(f"tk{n}")[:, 0:w], ACT.Identity,
                                       scale=norms[:, 2:3], bias=norms[:, 3:4]).then_inc(s_pja, 1)
                    act.activation(kT[:, :].rearrange("p (b s) -> p b s", b=B)[:, :, MAIN:],
                                   filled("td")[:, 0:B * P].rearrange("p (b s) -> p b s", b=B)[:, :, P - DCA:], ACT.Identity,
                                   scale=norms[:, 4:5], bias=norms[:, 5:6]).then_inc(s_pja, 1)
                    for u in range(UN):
                        for q in range(QT):
                            n = u * QT + q
                            w = n % (2 * QT)
                            if u >= 1:
                                evacuate(n - QT)
                            act.wait_ge(s_sm, NS * j + n + 1)
                            act.wait_ge(s_tr, 2 * (NS * (j + 1) + n - 2 * QT + 1))
                            for k, cols in enumerate((slice(0, MAIN), slice(MAIN, S2))):
                                act.activation(p[u % 2][:, q, cols], SC[n % 2][:, cols], ACT.Exp,
                                               bias=most[:, w, k:k + 1], accum_out=total[:, w, k:k + 1]).then_inc(s_ex, 1)
                        if u == HPG:
                            act.activation(oT[0][:, :], filled("o0")[:, :], ACT.Copy).then_inc(s_pja, 1)
                    for q in range(QT):
                        evacuate(NS - QT + q)
                    act.activation(oT[1][:, :], filled("o1")[:, :], ACT.Copy).then_inc(s_pja, 1)

                with act.Fori(0, NG) as j:
                    body(j)

            def gpsimd(pool):
                with pool.Fori(0, NG) as j:
                    for u in range(UN):
                        for q in range(QT):
                            n = u * QT + q
                            w = n % (2 * QT)
                            pool.wait_ge(s_rt, NS * j + n + 1)
                            pool.tensor_tensor(carry[:, w:w + 1], rtotal[:, w, 0:1], rtotal[:, w, 0:1], ALU.mult)
                            for k, cols in enumerate((slice(0, MAIN), slice(MAIN, S2))):
                                pool.tensor_scalar(p[u % 2][:, q, cols], p[u % 2][:, q, cols], rtotal[:, w, k:k + 1], 1.0,
                                                   ALU.mult, ALU.mult).then_inc(s_pn, 1)

            def tensor(pe):
                pe.wait_ge(s_h3, NT)
                pe.wait_ge(s_ctx1, NC_T // 2)
                pe.transpose(PJ[0][:, 0:P], ident[:, :], ident[:, :]).then_inc(s_tr, 2 * NS)
                pe.transpose(PJ[0][:, 0:P], ident[:, :], ident[:, :]).then_inc(s_pj, use.total)

                def body(j):
                    def bank(name):
                        n = use.index[name]
                        e, count = use.emptied(n - 2, j) if n >= 2 else use.emptied(use.total + n - 2, j - 1)
                        pe.wait_ge(emptied[e], count)
                        return PJ[n % 2]

                    def transposes(n):
                        u, q = n // QT, n % QT
                        pe.wait_ge(s_pn, 2 * (NS * j + n + 1))
                        for i, s_free in enumerate((s_ta, s_td)):
                            pe.wait_ge(s_free, NS * (j + 1) + n)
                            for k in range(NK // 2):
                                kk = i * NK // 2 + k
                                mm = pe.transpose(TR[i][:, k * P:(k + 1) * P], p[u % 2][:, q, kk * P:(kk + 1) * P], ident[:, :])
                            mm.then_inc(s_tr, 1)

                    def values(u):
                        b, h = u // HPG, u % HPG
                        o = bank(f"o{b}") if h == 0 else PJ[use.index[f"o{b}"] % 2]
                        pe.wait_ge(s_ta, NS * (j + 1) + (u + 1) * QT)
                        pe.wait_ge(s_td, NS * (j + 1) + (u + 1) * QT)
                        for k in range(NK):
                            mm = pe.matmul(o[h * HD:(h + 1) * HD, :], kv[:, b * NK + k, h, HD:], pT[:, k, :],
                                           start=(k == 0), stop=(k == NK - 1))
                        mm.then_inc(s_pj if h == HPG - 1 else s_val, 1)

                    def project(b, t):
                        e, count = use.emptied(use.index[f"o{b}"], j)
                        o = bank(f"w{b}{t}")
                        if t == 0:
                            pe.wait_ge(emptied[e], count)
                        pe.matmul(o[:, :], oT[b][:, t * P:(t + 1) * P], wo[:, :], start=True, stop=True).then_inc(s_pj, 1)

                    pe.wait_ge(s_w, 16 * 8 * (j + 1))
                    for n in range(NC_T // 2):
                        o = bank(f"kv{n}")
                        for i in range(2):
                            for c in range(VC):
                                mm = pe.matmul(o[:, i * 2 * GW:(i + 1) * 2 * GW], cxT3[:, c, (2 * n + i) * P:(2 * n + i + 1) * P],
                                               wkv[:, c, :], start=(c == 0), stop=(c == VC - 1))
                        mm.then_inc(s_pj, 1)
                    o = bank("d")
                    for b in range(B):
                        for c in range(VC):
                            mm = pe.matmul(o[:, b * 2 * GW:(b + 1) * 2 * GW], cxT3[:, c, (b + 1) * S2 - P:(b + 1) * S2], wd[:, c, :],
                                           start=(c == 0), stop=(c == VC - 1))
                    mm.then_inc(s_pj, 1)
                    for n in range(2):
                        o = bank(f"q{n}")
                        for i in range(4):
                            for c in range(KC):
                                mm = pe.matmul(o[:, i * GW:(i + 1) * GW], xT3[:, c, (4 * n + i) * P:(4 * n + i + 1) * P], wq[:, c, :],
                                               start=(c == 0), stop=(c == KC - 1))
                        mm.then_inc(s_pj, 1)
                    pe.wait_ge(s_cen, 6 * j + 6)
                    for name, t0, m in (("tq0", 0, 4), ("tq1", 4, 4), ("tk0", 8, 4), ("tk1", 12, 4), ("tk2", 16, 4), ("tk3", 20, 4),
                                        ("td", 24, 2)):
                        o = bank(name)
                        for i in range(m):
                            mm = pe.transpose(o[:, i * P:(i + 1) * P],
                                              cen[:, (t0 + i) * HPG:(t0 + i + 1) * HPG, :].rearrange("p h d -> p (h d)"), ident[:, :])
                        mm.then_inc(s_pj, 1)
                    pe.wait_ge(s_pja, use.per["A"] * (j + 1) + 7)
                    pe.wait_ge(s_ch, STEPS * (j + 1))
                    pe.wait_ge(s_wo, 16 * (j + 1))
                    for u in range(UN):
                        b, h = u // HPG, u % HPG
                        rows = slice(h * HD, (h + 1) * HD)
                        for q in range(QT):
                            n = u * QT + q
                            pe.wait_ge(s_ex, 2 * (NS * (j + 1) + n - 1))
                            for i in range(2):
                                mm = pe.matmul(SC[n % 2][:, i * BANK:(i + 1) * BANK], qT[rows, b * S + q * P:b * S + (q + 1) * P],
                                               kT[rows, b * S2 + i * BANK:b * S2 + (i + 1) * BANK], start=True, stop=True)
                            mm.then_inc(s_sc, 1)
                            if u >= 1:
                                transposes(n - QT)
                            if u == HPG + 1:
                                project(0, q)
                        if u >= 1:
                            values(u - 1)
                    for q in range(QT):
                        transposes(NS - QT + q)
                    values(UN - 1)
                    for q in range(QT):
                        project(1, q)

                with pe.Fori(0, NG) as j:
                    body(j)

            programs["SP"].append(sync)
            programs["DVE"].append(vector)
            programs["ACT"].append(scalar)
            programs["POOL"].append(gpsimd)
            programs["PE"].append(tensor)
            return s_tbo, NT + 1

        x2_done = cross_attention_1()
        phase.close()
        phase = ExitStack()

        def bit_ffn():
            HID = 2048
            HC = HID // P
            HB = HID // BANK
            LEAST = 1e-5
            MAGIC = 1.5 * 2.0 ** 23
            TOP, BOTTOM = 127.0, -128.0
            GROUPS = 8
            raw = [sb("f_raw1", [P, HC, D]), sb("f_raw2", [P, KC, HID])]
            wq = [sb("f_wq1", [P, HC, D], BF16), sb("f_wq2", [P, KC, HID], BF16)]
            w1T, w2T = sb("f_w1T", [P, KC, HID], BF16), sb("f_w2T", [P, HC, D], BF16)
            identb, ones = sb("f_identb", [P, P], BF16), sb("f_ones", [P, P])
            size, wmean, winv = sb("f_size", [P, 2]), sb("f_wmean", [P, 2]), sb("f_winv", [P, 2])
            b1, b2 = sb("f_b1", [P, HID]), sb("f_b2", [P, D])
            h = [sb(f"f_h{s}", [P, D]) for s in range(2)]
            hq = [sb(f"f_hq{s}", [P, D], BF16) for s in range(2)]
            hqT = [sb(f"f_hqT{s}", [P, KC, P], BF16) for s in range(2)]
            z = [sb(f"f_z{s}", [P, HID]) for s in range(2)]
            zq = [sb(f"f_zq{s}", [P, HID], BF16) for s in range(2)]
            zqT = [sb(f"f_zqT{s}", [P, HC, P], BF16) for s in range(2)]
            o = [sb(f"f_o{s}", [P, D]) for s in range(2)]
            most = sb("f_most", [P, 4])
            scale = sb("f_scale", [P, 4])
            unscale = sb("f_unscale", [P, 4])
            HID_B, OUT_B = [banks[k] for k in range(HB)], banks[4:6]
            TRB = [pairs[3][:, i * BANK:(i + 1) * BANK].bitcast(BF16) for i in range(2)]
            WTB = [pairs[2 + i // 2][:, (i % 2) * BANK:(i % 2 + 1) * BANK].bitcast(BF16) for i in range(4)]

            s_w = [sem("f_w1"), sem("f_w2")]
            s_b, s_stat, s_mv, s_std, s_rstd, s_id, s_one = [sem(f"f_{n}") for n in ("b", "stat", "mv", "std", "rstd", "id", "one")]
            s_size, s_sum, s_mean, s_wc, s_wr, s_wq, s_wt, s_wa, s_wd = [
                sem(f"f_{n}") for n in ("size", "sum", "mean", "wc", "wr", "wq", "wt", "wa", "wd")]
            s_ch, s_r, s_q, s_tr, s_te, s_m1, s_z, s_g, s_m2, s_o, s_x2 = [
                sem(f"f_{n}") for n in ("ch", "r", "q", "tr", "te", "m1", "z", "g", "m2", "o", "x2")]
            CH = 4
            STEPS = 26
            TURNS = 6

            def chunk(t3, k):
                n = t3.shape[1] // CH
                return t3[:, k * n:(k + 1) * n, :]

            def sync(sp):
                sp.wait_ge(*x2_done)
                sp.dma_start(raw[0][:, :, :], a["L1_ffn_w1"].rearrange("(t p) d -> p t d", p=P)).then_inc(s_w[0], 16)
                sp.dma_start(raw[1][:, :, :], a["L1_ffn_w2"].rearrange("(t p) d -> p t d", p=P)).then_inc(s_w[1], 16)
                sp.dma_start(b1[:, :], a["L1_ffn_b1"].partition_broadcast(P)).then_inc(s_b, 16)
                sp.dma_start(b2[:, :], a["L1_ffn_b2"].partition_broadcast(P)).then_inc(s_b, 16)
                out3 = out.rearrange("b (t p) d -> p (b t) d", p=P)
                with sp.Fori(0, NT // 2) as i:
                    sp.wait_ge(s_x2, 2 * (i + 1))
                    sp.dma_start(out3[:, bass.ds(i * 2, 2), :], x3[:, bass.ds(i * 2, 2), :]).then_inc(s_out, 16)
                sp.wait_ge(s_out, 16 * (NT // 2))

            def vector(dve):
                dve.wait_ge(*x2_done)
                dve.memset(ones[:, :], 1.0).then_inc(s_one, 1)
                dve.memset(scrap[:, 36:37], 0.0).then_inc(s_z, HB)
                dve.memset(scrap[:, 37:38], 0.0).then_inc(s_o, 2)
                for t in range(NT):
                    dve.bn_stats(stats[:, 6 * t:6 * t + 6], x3[:, t, :]).then_inc(s_stat, 1)
                for t in range(NT):
                    dve.wait_ge(s_stat, t + 1)
                    dve.bn_aggr(mv[:, 2 * t:2 * t + 2], stats[:, 6 * t:6 * t + 6]).then_inc(s_mv, 1)
                dve.wait_ge(s_std, 1)
                dve.reciprocal(rstd[:, :], std[:, :]).then_inc(s_rstd, 1)
                dve.wait_ge(s_sum, 1)
                dve.tensor_scalar(wmean[:, :], HID_B[0][:, 0:2], 1.0 / (HID * D), LEAST, ALU.mult, ALU.max).then_inc(s_mean, 1)
                dve.wait_ge(s_mean, 1)
                dve.reciprocal(winv[:, :], wmean[:, :]).then_inc(s_mean, 1)
                dve.wait_ge(s_mean, 2)
                for w in range(2):
                    for k in range(CH):
                        c = chunk(raw[w], k)
                        dve.tensor_scalar(c, c, winv[:, w:w + 1], 1.0, ALU.mult, ALU.min).then_inc(s_wc, 1)
                        dve.wait_ge(s_wc, w * CH + k + 1)
                        dve.tensor_scalar(c, c, -1.0, MAGIC, ALU.max, ALU.add).then_inc(s_wr, 1)
                for g in range(1, 2 * GROUPS, 2):
                    dve.wait_ge(s_wt, g + 1)
                    turned(dve, g)
                dve.wait_ge(s_rstd, 1)
                dve.wait_ge(s_b, 32)

                def body(i):
                    steps = 0

                    def step(ins):
                        nonlocal steps
                        steps += 1
                        ins.then_inc(s_ch, 1)
                        dve.wait_ge(s_ch, STEPS * i + steps)

                    def quantise(src, n, w):
                        m, q = most[:, n:n + 1], scale[:, n:n + 1]
                        step(dve.tensor_scalar(m, m, LEAST, None, ALU.max))
                        step(dve.reciprocal(q, m))
                        step(dve.tensor_scalar(q, q, TOP, None, ALU.mult))
                        step(dve.tensor_scalar(unscale[:, n:n + 1], m, 1.0 / TOP, wmean[:, w:w + 1], ALU.mult, ALU.mult))
                        step(dve.tensor_scalar(src, src, q, MAGIC, ALU.mult, ALU.add))
                        dve.tensor_scalar(src, src, MAGIC + TOP, MAGIC + BOTTOM, ALU.min, ALU.max).then_inc(s_r, 1)

                    for s in range(2):
                        t = i * 2 + s
                        step(dve.tensor_scalar(h[s][:, :], x3[:, bass.ds(t, 1), :].rearrange("p t d -> p (t d)"),
                                               mv[:, bass.ds(t * 2, 1)], rstd[:, bass.ds(t, 1)], ALU.subtract, ALU.mult))
                        step(dve.tensor_reduce(most[:, s:s + 1], h[s][:, :], AX.X, ALU.max, apply_absolute_value=True))
                        quantise(h[s][:, :], s, 0)
                    for s in range(2):
                        for k in range(HB):
                            dve.wait_ge(s_m1, 2 * HB * i + HB * s + k + 1)
                            cols = slice(k * BANK, (k + 1) * BANK)
                            dve.scalar_tensor_tensor(z[s][:, cols], HID_B[k][:, :], unscale[:, s:s + 1], b1[:, cols],
                                                     ALU.mult, ALU.add).then_inc(s_z, 1)
                    for s in range(2):
                        dve.wait_ge(s_g, 2 * i + s + 1)
                        step(dve.tensor_reduce(most[:, 2 + s:3 + s], z[s][:, :], AX.X, ALU.max, apply_absolute_value=True))
                        quantise(z[s][:, :], 2 + s, 1)
                    for s in range(2):
                        dve.wait_ge(s_m2, 2 * i + s + 1)
                        dve.scalar_tensor_tensor(o[s][:, :], OUT_B[s][:, :], unscale[:, 2 + s:3 + s], b2[:, :],
                                                 ALU.mult, ALU.add).then_inc(s_o, 1)
                        dve.wait_ge(s_o, 2 * i + s + 3)
                        xt = x3[:, bass.ds(i * 2 + s, 1), :].rearrange("p t d -> p (t d)")
                        dve.scalar_tensor_tensor(xt, o[s][:, :], tgate[:, 3:4], xt, ALU.mult, ALU.add).then_inc(s_x2, 1)
                    assert steps == STEPS

                with dve.Fori(0, NT // 2) as i:
                    body(i)

            def turned(engine, g):
                src = WTB[g % 4][:, :]
                if g < GROUPS:
                    dst = w1T[:, g // 2, (g % 2) * 8 * P:(g % 2 + 1) * 8 * P]
                else:
                    m = (g - GROUPS) * 2
                    dst, src = w2T[:, m:m + 2, :], src.rearrange("p (m d) -> p m d", m=2)
                if g % 2:
                    engine.tensor_copy(dst, src).then_inc(s_wd, 1)
                else:
                    engine.activation(dst, src, ACT.Copy).then_inc(s_wa, 1)

            def scalar(act):
                act.wait_ge(*x2_done)
                act.activation(identb[:, :], ident[:, :], ACT.Copy).then_inc(s_id, 1)
                act.activation(scrap[:, 40:41], eps[:, 0:1], ACT.Copy).then_inc(s_te, 2)
                act.wait_ge(s_mv, NT)
                act.activation(std[:, :], mv[:, :].rearrange("p (t k) -> p t k", k=2)[:, :, 1], ACT.Sqrt,
                               bias=eps[:, 0:1]).then_inc(s_std, 1)
                for w in range(2):
                    act.wait_ge(s_w[w], 16)
                    act.activation(wq[w][:, :, :], raw[w][:, :, :], ACT.Abs, accum_out=size[:, w:w + 1]).then_inc(s_size, 1)
                act.wait_ge(s_size, 2)
                for w in range(2):
                    for k in range(CH):
                        act.wait_ge(s_wr, w * CH + k + 1)
                        act.activation(chunk(wq[w], k), chunk(raw[w], k), ACT.Copy, bias=-MAGIC).then_inc(s_wq, 1)
                for g in range(0, 2 * GROUPS, 2):
                    act.wait_ge(s_wt, g + 1)
                    turned(act, g)

                def body(i):
                    def whole(dst, src, n):
                        act.wait_ge(s_r, 4 * i + n + 1)
                        act.activation(dst[:, :], src[:, :], ACT.Copy, bias=-MAGIC).then_inc(s_q, 1)

                    def copy(dst, n, m):
                        act.wait_ge(s_tr, TURNS * i + n + 1)
                        act.activation(dst, TRB[n % 2][:, 0:m * P].rearrange("p (m n) -> p m n", m=m), ACT.Copy).then_inc(s_te, 1)

                    for s in range(2):
                        whole(hq[s], h[s], s)
                    for s in range(2):
                        copy(hqT[s][:, :, :], s, KC)
                    for s in range(2):
                        act.wait_ge(s_z, HB * (2 * i + s + 2))
                        act.activation(z[s][:, :], z[s][:, :], ACT.Gelu).then_inc(s_g, 1)
                    for s in range(2):
                        whole(zq[s], z[s], 2 + s)
                        for k in range(2):
                            copy(zqT[s][:, k * 8:(k + 1) * 8, :], 2 + 2 * s + k, 8)

                with act.Fori(0, NT // 2) as i:
                    body(i)

            def tensor(pe):
                pe.wait_ge(s_one, 1)
                pe.wait_ge(s_size, 2)
                pe.matmul(HID_B[0][:, 0:2], ones[:, :], size[:, :], start=True, stop=True).then_inc(s_sum, 1)
                pe.wait_ge(s_id, 1)
                for g in range(2 * GROUPS):
                    if g < GROUPS:
                        pe.wait_ge(s_wq, CH)
                    else:
                        pe.wait_ge(s_wq, 2 * CH)
                    if g >= 4:
                        pe.wait_ge((s_wa, s_wd)[g % 2], (g - 4) // 2 + 1)
                    for k in range(8):
                        if g < GROUPS:
                            src = wq[0][:, (g % 2) * 8 + k, (g // 2) * P:(g // 2 + 1) * P]
                        else:
                            m = (g - GROUPS) * 2 + k // 4
                            src = wq[1][:, k % 4, m * P:(m + 1) * P]
                        mm = pe.transpose(WTB[g % 4][:, k * P:(k + 1) * P], src, identb[:, :])
                    mm.then_inc(s_wt, 1)
                pe.wait_ge(s_wa, GROUPS)
                pe.wait_ge(s_wd, GROUPS)

                def body(i):
                    def turn(src, n, m):
                        pe.wait_ge(s_te, TURNS * i + n + 1)
                        for k in range(m):
                            mm = pe.transpose(TRB[n % 2][:, k * P:(k + 1) * P], src[:, k * P:(k + 1) * P], identb[:, :])
                        mm.then_inc(s_tr, 1)

                    for s in range(2):
                        pe.wait_ge(s_q, 4 * i + s + 1)
                        turn(hq[s][:, :], s, KC)
                    for s in range(2):
                        pe.wait_ge(s_te, TURNS * i + s + 3)
                        for k in range(HB):
                            pe.wait_ge(s_z, HB * (2 * i + s) + k + 1)
                            for c in range(KC):
                                mm = pe.matmul(HID_B[k][:, :], hqT[s][:, c, :], w1T[:, c, k * BANK:(k + 1) * BANK],
                                               start=(c == 0), stop=(c == KC - 1))
                            mm.then_inc(s_m1, 1)
                    for s in range(2):
                        pe.wait_ge(s_q, 4 * i + 2 + s + 1)
                        for k in range(2):
                            turn(zq[s][:, k * 8 * P:(k + 1) * 8 * P], 2 + 2 * s + k, 8)
                        pe.wait_ge(s_te, TURNS * i + 2 * s + 6)
                        pe.wait_ge(s_o, 2 * i + s + 1)
                        for m in range(HC):
                            mm = pe.matmul(OUT_B[s][:, :], zqT[s][:, m, :], w2T[:, m, :], start=(m == 0), stop=(m == HC - 1))
                        mm.then_inc(s_m2, 1)

                with pe.Fori(0, NT // 2) as i:
                    body(i)

            programs["SP"].append(sync)
            programs["DVE"].append(vector)
            programs["ACT"].append(scalar)
            programs["PE"].append(tensor)

        bit_ffn()
        phase.close()

        block = ctx.enter_context(nc.Block())

        @block.sync
        def _(sp):
            for stage in programs["SP"]:
                stage(sp)

        @block.scalar
        def _(act):
            for stage in programs["ACT"]:
                stage(act)

        @block.tensor
        def _(pe):
            for stage in programs["PE"]:
                stage(pe)

        @block.vector
        def _(dve):
            for stage in programs["DVE"]:
                stage(dve)

        @block.gpsimd
        def _(pool):
            for stage in programs["POOL"]:
                stage(pool)


def constants():
    half = 32
    inv = (np.float32(1.0) / np.float32(150000.0) ** (np.arange(half, dtype=np.float32) / np.float32(half))).astype(np.float32)
    angle = (np.arange(S, dtype=np.float32)[:, None] * inv).astype(np.float32).T
    rows = np.arange(P)
    swap = np.zeros((P, P), np.float32)
    for m in range(P):
        if m % (2 * half) < half:
            swap[m + half, m] = -1.0
        else:
            swap[m - half, m] = 1.0
    causal = np.zeros((P, S), np.float32)
    causal[:, S - P:] = np.where(rows[None, :] <= rows[:, None], 0.0, -BIG)
    part = np.stack([np.arange(P) < P - 16, np.arange(P) >= P - 16], axis=1).astype(np.float32)
    return {"c_part": part, "c_ident": np.eye(P, dtype=np.float32), "c_causal": causal, "c_swap": swap,
            "c_cos": np.tile(np.cos(angle), (4, 1)).astype(np.float32),
            "c_sin": np.tile(np.sin(angle), (4, 1)).astype(np.float32)}


def kernel(**inputs):
    import concourse.bacc as _bacc
    from concourse.bass_utils import run_bass_kernel_spmd as _run

    nc = _bacc.Bacc("TRN2", target_bir_lowering=False, num_devices=1)
    arrays, args = {}, {}
    wkv = np.concatenate([inputs["L1_xattn_Wk"], inputs["L1_xattn_Wv"]], axis=1)
    bkv = np.concatenate([inputs["L1_xattn_bk"], inputs["L1_xattn_bv"]])
    for name, value in {**inputs, **constants(), "wkv": wkv, "bkv": bkv}.items():
        value = np.ascontiguousarray(value)
        if value.dtype == np.bool_:
            value = value.view(np.uint8)
        arrays[f"in_{name}"] = value
        args[name] = nc.dram_tensor(f"in_{name}", value.shape, mybir.dt.from_np(value.dtype), kind="ExternalInput").ap()
    out = nc.dram_tensor("out_x", (B, S, D), F32, kind="ExternalOutput").ap()
    program(nc, args, out)
    r = _run(nc, [arrays], core_ids=[0])
    return r.results[0]["out_x"]
```

```python
from contextlib import ExitStack

import numpy as np

import concourse.bass as bass
from concourse import mybir

P = 128
BANK = 512
F32 = mybir.dt.float32
F32R = mybir.dt.float32r
BF16 = mybir.dt.bfloat16
U8 = mybir.dt.uint8
I32 = mybir.dt.int32
ALU = mybir.AluOpType
ACT = mybir.ActivationFunctionType
AX = mybir.AxisListType

B, S, D = 2, 512, 512
S2, DV = 1024, 256
T = B * S
NT = T // P
QT = S // P
KC = D // P
VC = DV // P
NC_T = B * S2 // P
BIG = 1.0e30


class Use:

    def __init__(self, plan):
        self.plan = plan
        self.total = len(plan)
        self.per = {e: sum(x == e for _, x in plan) for e in "AD"}
        self.index, self.nth, seen = {}, [], {"A": 0, "D": 0}
        for n, (name, e) in enumerate(plan):
            seen[e] += 1
            self.nth.append((e, seen[e]))
            self.index[name] = n

    def emptied(self, n, it):
        e, c = self.nth[n % self.total]
        return e, self.per[e] * (it + 1 + n // self.total) + c


def program(nc, a, out):
    ctx = ExitStack()
    with ctx:
        def sem(name):
            return ctx.enter_context(nc.semaphore(name))

        def keep(name, shape, dt=F32):
            return ctx.enter_context(nc.sbuf_tensor(name, shape, dt))

        pairs = [ctx.enter_context(nc.psum_tensor(f"pair{i}", [P, 2 * BANK], F32)) for i in range(4)]
        banks = [pairs[i // 2][:, (i % 2) * BANK:(i % 2 + 1) * BANK] for i in range(8)]

        x = keep("x", [P, NT * D])
        hslot = keep("hslot", [P, 2 * D])
        ident = keep("ident", [P, P])
        identr = keep("identr", [P, P], F32R)
        gates = keep("gates", [P, 4])
        tgate = keep("tgate", [P, 4])
        stats = keep("stats", [P, NT * 6])
        mv = keep("mv", [P, NT * 2])
        std = keep("std", [P, NT])
        rstd = keep("rstd", [P, NT])
        eps = keep("eps", [P, 2])
        scrap = keep("scrap", [P, 64])
        x3 = x[:, :].rearrange("p (t d) -> p t d", t=NT)

        s_const, s_x, s_gate, s_eps, s_out = sem("s_const"), sem("s_x"), sem("s_gate"), sem("s_eps"), sem("s_out")
        s_tgate, s_idr = sem("s_tgate"), sem("s_idr")

        programs = {"SP": [], "ACT": [], "PE": [], "DVE": [], "POOL": []}

        s_stat, s_mv, s_std, s_rstd = [sem(f"ln_{n}") for n in ("stat", "mv", "std", "rstd")]

        def statistics(n, before):
            def vector(dve):
                dve.wait_ge(*before)
                for t in range(NT):
                    dve.bn_stats(stats[:, 6 * t:6 * t + 6], x3[:, t, :]).then_inc(s_stat, 1)
                for t in range(NT):
                    dve.wait_ge(s_stat, n * NT + t + 1)
                    dve.bn_aggr(mv[:, 2 * t:2 * t + 2], stats[:, 6 * t:6 * t + 6]).then_inc(s_mv, 1)
                dve.wait_ge(s_std, n + 1)
                dve.reciprocal(rstd[:, :], std[:, :]).then_inc(s_rstd, 1)

            def scalar(act):
                act.wait_ge(s_eps, 1)
                act.wait_ge(s_mv, (n + 1) * NT)
                act.activation(std[:, :], mv[:, :].rearrange("p (t k) -> p t k", k=2)[:, :, 1], ACT.Sqrt,
                               bias=eps[:, 0:1]).then_inc(s_std, 1)

            programs["DVE"].append(vector)
            programs["ACT"].append(scalar)

        s_lnh, s_lntr, s_lnev = [sem(f"ln_{n}") for n in ("h", "tr", "ev")]

        def layernorm(n, k, before, hT3):
            statistics(n, before)

            def vector(dve):
                dve.wait_ge(s_rstd, n + 1)
                for t in range(NT):
                    if t >= 2:
                        dve.wait_ge(s_lntr, k * NT + t - 1)
                    dve.tensor_scalar(hslot[:, (t % 2) * D:(t % 2 + 1) * D], x3[:, t, :], mv[:, 2 * t:2 * t + 1],
                                      rstd[:, t:t + 1], ALU.subtract, ALU.mult).then_inc(s_lnh, 1)

            def scalar(act):
                for t in range(NT):
                    act.wait_ge(s_lntr, k * NT + t + 1)
                    act.activation(hT3[:, :, t * P:(t + 1) * P],
                                   banks[t % 2][:, :].rearrange("p (c n) -> p c n", c=KC), ACT.Copy).then_inc(s_lnev, 1)

            def tensor(pe):
                pe.wait_ge(s_const, 16)
                for t in range(NT):
                    pe.wait_ge(s_lnh, k * NT + t + 1)
                    if t >= 2:
                        pe.wait_ge(s_lnev, k * NT + t - 1)
                    for c in range(KC):
                        mm = pe.transpose(banks[t % 2][:, c * P:(c + 1) * P],
                                          hslot[:, (t % 2) * D + c * P:(t % 2) * D + (c + 1) * P], ident[:, :])
                    mm.then_inc(s_lntr, 1)

            programs["DVE"].append(vector)
            programs["ACT"].append(scalar)
            programs["PE"].append(tensor)

        s_ones = sem("s_ones")

        def load_sync(sp):
            sp.dma_start(x3, a["x"].rearrange("b (t p) d -> p (b t) d", p=P)).then_inc(s_x, 16)
            sp.dma_start(ident[:, :], a["c_ident"]).then_inc(s_const, 16)
            sp.dma_start(gates[:, 0:2], a["g_xattn"].partition_broadcast(P)).then_inc(s_gate, 16)
            sp.dma_start(gates[:, 2:4], a["g_ffn"].partition_broadcast(P)).then_inc(s_gate, 16)

        def load_vector(dve):
            dve.memset(eps[:, 0:1], 1e-5).then_inc(s_ones, 1)
            dve.memset(eps[:, 1:2], 1e-6).then_inc(s_eps, 1)
            dve.memset(scrap[:, :], 0.0).then_inc(s_ones, 1)

        def load_scalar(act):
            act.wait_ge(s_gate, 32)
            act.wait_ge(s_ones, 2)
            act.activation(tgate[:, :], gates[:, :], ACT.Tanh).then_inc(s_tgate, 1)
            act.wait_ge(s_const, 16)
            act.activation(identr[:, :], ident[:, :], ACT.Copy).then_inc(s_idr, 1)

        programs["SP"].append(load_sync)
        programs["DVE"].append(load_vector)
        programs["ACT"].append(load_scalar)

        phase = ExitStack()

        def sb(name, shape, dt=F32):
            return phase.enter_context(nc.sbuf_tensor(name, shape, dt))

        hT3 = sb("hT_x0", [P, KC * T])[:, :].rearrange("p (c t) -> p c t", c=KC)
        ctxT = sb("ctxT", [P, VC * B * S2])
        ctxT3 = ctxT[:, :].rearrange("p (c t) -> p c t", c=VC)
        cslot = sb("cslot", [P, 4 * DV])

        PAIRS = NC_T // 2
        s_ctx = [sem(f"ctx_in{i}") for i in range(2)]
        s_ctxtr, s_ctxev = sem("ctx_tr"), sem("ctx_ev")

        def transpose_context(n, ctxT3, cslot, before=None):
            src = a["ctx_1024"].rearrange("b (t p) d -> p (b t) d", p=P)

            def sync(sp):
                if before:
                    sp.wait_ge(*before)
                for t in range(PAIRS):
                    if t >= 2:
                        sp.wait_ge(s_ctxtr, n * PAIRS + t - 1)
                    sp.dma_start(cslot[:, (t % 2) * 2 * DV:(t % 2 + 1) * 2 * DV].rearrange("p (t d) -> p t d", t=2),
                                 src[:, 2 * t:2 * t + 2, :]).then_inc(s_ctx[t % 2], 16)

            def tensor(pe):
                pe.wait_ge(s_const, 16)
                for t in range(PAIRS):
                    pe.wait_ge(s_ctx[t % 2], 16 * (n * PAIRS // 2 + t // 2 + 1))
                    if t >= 2:
                        pe.wait_ge(s_ctxev, n * PAIRS + t - 1)
                    for c in range(VC):
                        for j in range(2):
                            mm = pe.transpose(banks[4 + t % 2][:, (c * 2 + j) * P:(c * 2 + j + 1) * P],
                                              cslot[:, ((t % 2) * 2 + j) * DV + c * P:((t % 2) * 2 + j) * DV + (c + 1) * P],
                                              ident[:, :])
                    mm.then_inc(s_ctxtr, 1)

            def scalar(act):
                for t in range(PAIRS):
                    act.wait_ge(s_ctxtr, n * PAIRS + t + 1)
                    act.activation(ctxT3[:, :, t * 2 * P:(t + 1) * 2 * P],
                                   banks[4 + t % 2][:, :].rearrange("p (c n) -> p c n", c=VC), ACT.Copy).then_inc(s_ctxev, 1)

            programs["SP"].append(sync)
            programs["PE"].append(tensor)
            programs["ACT"].append(scalar)

        transpose_context(0, ctxT3, cslot)
        layernorm(0, 0, (s_x, 16), hT3)

        def cross_attention_0():
            NKV, HPG, HD = 8, 2, 128
            UN = B * HPG
            NK = S2 // P
            GW = HPG * HD
            SCALE = 1.0 / float(np.sqrt(HD))
            wk = [sb(f"x_wk{s}", [P, VC, HD]) for s in range(2)]
            wv = [sb(f"x_wv{s}", [P, VC, HD]) for s in range(2)]
            wq = [sb(f"x_wq{s}", [P, KC, GW]) for s in range(2)]
            wo = [sb(f"x_wo{s}", [P, HPG, D]) for s in range(2)]
            kT = [sb(f"x_kT{b}", [P, S2]) for b in range(B)]
            v = [sb(f"x_v{b}", [P, NK, HD]) for b in range(B)]
            qT = [sb(f"x_qT{u}", [P, S]) for u in range(UN)]
            p = [sb(f"x_p{i}", [P, QT, S2]) for i in range(2)]
            pT = sb("x_pT", [P, NK, S])
            oT = [sb(f"x_oT{u}", [P, S]) for u in range(UN)]
            least = sb("x_least", [P, 2 * QT])
            total = sb("x_total", [P, 2 * QT])
            rtotal = sb("x_rtotal", [P, 2 * QT])
            carry = sb("x_carry", [P, 2 * QT])
            mask8 = sb("x_mask8", [P, B * S2], U8)
            mrow8 = sb("x_mrow8", [B * NK, P], U8)
            mrow = sb("x_mrow", [B * NK, P])
            mcol = sb("x_mcol", [P, B * NK])
            lower = sb("x_lower", [P, B * S2])

            use = Use([(f"k{b}{j}", "A") for b in (0,) for j in range(2)] + [("v00", "D"), ("v01", "D"), ("q0", "A"), ("q1", "A")]
                      + [("k10", "A"), ("k11", "A"), ("v10", "D"), ("v11", "D"), ("q2", "A"), ("q3", "A")]
                      + [("o0", "A"), ("o1", "A"), ("o2", "A")] + [(f"w0{t}", "D") for t in range(QT)]
                      + [("o3", "A")] + [(f"w1{t}", "D") for t in range(QT)])
            assert use.total % 2 == 0
            PJ, SC, TR = banks[0:2], pairs[1:3], banks[6:8]
            NS = UN * QT

            s_mask, s_mrow, s_mtr, s_low, s_mcol = [sem(f"x_{n}") for n in ("mask", "mrow", "mtr", "low", "mcol")]
            s_w = [sem(f"x_w{i}") for i in range(2)]
            s_pj, s_pja, s_pjd, s_sc, s_sm, s_ex, s_rt, s_pn, s_tr, s_ta, s_td = [
                sem(f"x_{n}") for n in ("pj", "pja", "pjd", "sc", "sm", "ex", "rt", "pn", "tr", "ta", "td")]
            emptied = {"A": s_pja, "D": s_pjd}
            LOADS = 4

            def load(sp, g, s):
                if isinstance(g, int):
                    c1, c2 = slice(g * HD, (g + 1) * HD), slice(g * GW, (g + 1) * GW)
                else:
                    c1, c2 = bass.ds(g * HD, HD), bass.ds(g * GW, GW)
                sp.dma_start(wk[s][:, :, :], a["L0_xattn_Wk"].rearrange("(c p) n -> p c n", p=P)[:, :, c1]).then_inc(s_w[s], 16)
                sp.dma_start(wv[s][:, :, :], a["L0_xattn_Wv"].rearrange("(c p) n -> p c n", p=P)[:, :, c1]).then_inc(s_w[s], 16)
                sp.dma_start(wq[s][:, :, :], a["L0_xattn_Wq"].rearrange("(c p) n -> p c n", p=P)[:, :, c2]).then_inc(s_w[s], 16)
                sp.dma_start(wo[s][:, :, :], a["L0_xattn_Wo"][c2, :].rearrange("(c p) n -> p c n", p=P)).then_inc(s_w[s], 16)

            def sync(sp):
                m = a["mask_BxS2_bf1"]
                sp.dma_start(mask8[:, :], m.rearrange("b s -> (b s)").partition_broadcast(P)).then_inc(s_mask, 16)
                sp.dma_start(mrow8[:, :], m.rearrange("b (t p) -> (b t) p", p=P)).then_inc(s_mask, 16)
                load(sp, 0, 0)
                load(sp, 1, 1)
                with sp.Fori(0, NKV // 2 - 1) as i:
                    for s in range(2):
                        sp.wait_ge(s_pjd, (i * 2 + s + 2) * use.per["D"])
                        load(sp, i * 2 + (2 + s), s)

            def vector(dve):
                dve.wait_ge(s_mask, 32)
                dve.tensor_scalar(lower[:, :], mask8[:, :], -1.0, BIG, ALU.add, ALU.mult).then_inc(s_low, 1)
                dve.tensor_copy(mrow[:, :], mrow8[:, :]).then_inc(s_mrow, 1)
                dve.wait_ge(s_mtr, 1)
                dve.tensor_copy(mcol[:, :], PJ[0][:, 0:B * NK]).then_inc(s_mcol, 1)
                dve.wait_ge(s_ones, 2)
                dve.memset(scrap[:, 0:1], 0.0).then_inc(s_pjd, use.per["D"])
                dve.memset(scrap[:, 1:2], 0.0).then_inc(s_sm, NS)
                dve.memset(scrap[:, 2:3], 0.0).then_inc(s_td, NS)
                dve.wait_ge(s_low, 1)
                dve.wait_ge(s_mcol, 1)
                dve.wait_ge(s_tgate, 1)

                def body(g):
                    def empty(name):
                        dve.wait_ge(s_pj, use.total * (g + 1) + use.index[name] + 1)
                        return PJ[use.index[name] % 2]

                    def reciprocal(n):
                        if n >= 0:
                            dve.wait_ge(s_ex, NS * g + n + 1)
                        col = slice(n % (2 * QT), n % (2 * QT) + 1)
                        ins = dve.reciprocal(rtotal[:, col], total[:, col]) if n >= 0 else dve.memset(scrap[:, 8 + n % 2:9 + n % 2], 0.0)
                        if n >= 0:
                            ins.then_inc(s_rt, 1)

                    def evacuate(n):
                        if n % QT == 0:
                            before = use.index[f"o{n // QT - 1}"] if n >= QT else use.index[f"o{UN - 1}"] - use.total
                            dve.wait_ge(s_pj, use.total * (g + 1) + before + 1)
                        dve.wait_ge(s_tr, 2 * (NS * (g + 1) + n + 1))
                        q = n % QT
                        dve.tensor_copy(pT[:, NK // 2:, q * P:(q + 1) * P],
                                        TR[1][:, :].rearrange("p (k n) -> p k n", n=P)).then_inc(s_td, 1)

                    def add_out(b):
                        for t in range(QT):
                            o = empty(f"w{b}{t}")
                            xt = x3[:, b * QT + t, :]
                            dve.scalar_tensor_tensor(xt, o[:, :], tgate[:, 0:1], xt, ALU.mult, ALU.add).then_inc(s_pjd, 1)

                    for b in range(B):
                        for j in range(2):
                            o = empty(f"v{b}{j}")
                            k0 = b * NK + j * NK // 2
                            dve.tensor_tensor(v[b][:, j * NK // 2:(j + 1) * NK // 2, :],
                                              o[:, :].rearrange("p (k n) -> p k n", n=HD),
                                              mcol[:, k0:k0 + NK // 2].unsqueeze(2).to_broadcast([P, NK // 2, HD]),
                                              ALU.mult).then_inc(s_pjd, 1)
                    for u in range(UN):
                        for q in range(QT):
                            n = u * QT + q
                            dve.wait_ge(s_sc, NS * g + n + 1)
                            dve.wait_ge(s_tr, 2 * (NS * (g + 1) + n - 2 * QT + 1))
                            reciprocal(n - 2)
                            dve.tensor_tensor_reduce(
                                p[u % 2][:, q, :], SC[n % 2][:, :], lower[:, (u // HPG) * S2:(u // HPG + 1) * S2], -SCALE,
                                3.0e38, ALU.add, ALU.min, least[:, n % (2 * QT):n % (2 * QT) + 1]).then_inc(s_sm, 1)
                            if u >= 1:
                                evacuate(n - QT)
                        if u == UN - 1:
                            reciprocal(NS - 2)
                            reciprocal(NS - 1)
                        if u == UN - 1:
                            add_out(0)
                    for q in range(QT):
                        evacuate(NS - QT + q)
                    add_out(1)

                with dve.Fori(0, NKV) as g:
                    body(g)

            def scalar(act):
                act.wait_ge(s_ones, 2)
                act.activation(scrap[:, 4:5], eps[:, 0:1], ACT.Copy).then_inc(s_pja, use.per["A"])
                act.activation(scrap[:, 5:6], eps[:, 0:1], ACT.Copy).then_inc(s_ta, NS)

                def body(g):
                    def empty(name, dst):
                        act.wait_ge(s_pj, use.total * (g + 1) + use.index[name] + 1)
                        act.activation(dst, PJ[use.index[name] % 2][:, :], ACT.Copy).then_inc(s_pja, 1)

                    def evacuate(n):
                        if n % QT == 0:
                            before = use.index[f"o{n // QT - 1}"] if n >= QT else use.index[f"o{UN - 1}"] - use.total
                            act.wait_ge(s_pj, use.total * (g + 1) + before + 1)
                        act.wait_ge(s_tr, 2 * (NS * (g + 1) + n) + 1)
                        q = n % QT
                        act.activation(pT[:, 0:NK // 2, q * P:(q + 1) * P],
                                       TR[0][:, :].rearrange("p (k n) -> p k n", n=P), ACT.Copy).then_inc(s_ta, 1)

                    for b in range(B):
                        for j in range(2):
                            empty(f"k{b}{j}", kT[b][:, j * BANK:(j + 1) * BANK])
                        for h in range(HPG):
                            empty(f"q{b * HPG + h}", qT[b * HPG + h][:, :])
                    for u in range(UN):
                        for q in range(QT):
                            n = u * QT + q
                            w = n % (2 * QT)
                            if u >= 1:
                                evacuate(n - QT)
                            act.wait_ge(s_sm, NS * (g + 1) + n + 1)
                            act.activation(p[u % 2][:, q, :], p[u % 2][:, q, :], ACT.Exp, scale=-1.0,
                                           bias=least[:, w:w + 1],
                                           accum_out=total[:, w:w + 1]).then_inc(s_ex, 1)
                        if u >= 1:
                            empty(f"o{u - 1}", oT[u - 1][:, :])
                    for q in range(QT):
                        evacuate(NS - QT + q)
                    empty(f"o{UN - 1}", oT[UN - 1][:, :])

                with act.Fori(0, NKV) as g:
                    body(g)

            def gpsimd(pool):
                with pool.Fori(0, NKV) as g:
                    for u in range(UN):
                        for q in range(QT):
                            n = u * QT + q
                            w = n % (2 * QT)
                            pool.wait_ge(s_rt, NS * g + n + 1)
                            pool.tensor_tensor(carry[:, w:w + 1], rtotal[:, w:w + 1], rtotal[:, w:w + 1], ALU.mult)
                            pool.tensor_scalar(p[u % 2][:, q, :], p[u % 2][:, q, :], rtotal[:, w:w + 1], 1.0,
                                               ALU.mult, ALU.mult).then_inc(s_pn, 1)

            def tensor(pe):
                pe.wait_ge(s_lnev, NT)
                pe.wait_ge(s_ctxev, PAIRS)
                pe.wait_ge(s_mrow, 1)
                pe.transpose(PJ[0][:, 0:B * NK], mrow[:, :], ident[0:B * NK, 0:B * NK]).then_inc(s_mtr, 1)
                pe.wait_ge(s_mcol, 1)
                pe.wait_ge(s_pja, 1)
                pe.transpose(PJ[0][:, 0:P], ident[:, :], ident[:, :]).then_inc(s_tr, 2 * NS)
                pe.transpose(PJ[0][:, 0:P], ident[:, :], ident[:, :]).then_inc(s_pj, use.total)

                def body(i, s):
                    g = i * 2 + s

                    def bank(name):
                        n = use.index[name]
                        e, count = use.emptied(n - 2, g) if n >= 2 else use.emptied(use.total + n - 2, g - 1)
                        pe.wait_ge(emptied[e], count)
                        return PJ[n % 2]

                    def transposes(n):
                        u, q = n // QT, n % QT
                        pe.wait_ge(s_pn, NS * g + n + 1)
                        for j, s_free in enumerate((s_ta, s_td)):
                            pe.wait_ge(s_free, NS * (g + 1) + n)
                            for k in range(NK // 2):
                                kk = j * NK // 2 + k
                                mm = pe.transpose(TR[j][:, k * P:(k + 1) * P], p[u % 2][:, q, kk * P:(kk + 1) * P], ident[:, :])
                            mm.then_inc(s_tr, 1)

                    def values(u):
                        o = bank(f"o{u}")
                        pe.wait_ge(s_ta, NS * (g + 1) + (u + 1) * QT)
                        pe.wait_ge(s_td, NS * (g + 1) + (u + 1) * QT)
                        for k in range(NK):
                            mm = pe.matmul(o[:, :], v[u // HPG][:, k, :], pT[:, k, :], start=(k == 0), stop=(k == NK - 1))
                        mm.then_inc(s_pj, 1)

                    def project(b):
                        e, count = use.emptied(use.index[f"o{b * HPG + HPG - 1}"], g)
                        for t in range(QT):
                            o = bank(f"w{b}{t}")
                            if t == 0:
                                pe.wait_ge(emptied[e], count)
                            for h in range(HPG):
                                mm = pe.matmul(o[:, :], oT[b * HPG + h][:, t * P:(t + 1) * P], wo[s][:, h, :],
                                               start=(h == 0), stop=(h == HPG - 1))
                            mm.then_inc(s_pj, 1)

                    pe.wait_ge(s_w[s], 16 * LOADS * (i + 1))
                    for b in range(B):
                        for j in range(2):
                            o = bank(f"k{b}{j}")
                            for c in range(VC):
                                mm = pe.matmul(o[:, :], wk[s][:, c, :],
                                               ctxT3[:, c, b * S2 + j * BANK:b * S2 + (j + 1) * BANK],
                                               start=(c == 0), stop=(c == VC - 1))
                            mm.then_inc(s_pj, 1)
                        for j in range(2):
                            o = bank(f"v{b}{j}")
                            for k in range(NK // 2):
                                tok = b * S2 + (j * NK // 2 + k) * P
                                for c in range(VC):
                                    mm = pe.matmul(o[:, k * HD:(k + 1) * HD], ctxT3[:, c, tok:tok + P], wv[s][:, c, :],
                                                   start=(c == 0), stop=(c == VC - 1))
                            mm.then_inc(s_pj, 1)
                        for h in range(HPG):
                            o = bank(f"q{b * HPG + h}")
                            for c in range(KC):
                                mm = pe.matmul(o[:, :], wq[s][:, c, h * HD:(h + 1) * HD], hT3[:, c, b * S:(b + 1) * S],
                                               start=(c == 0), stop=(c == KC - 1))
                            mm.then_inc(s_pj, 1)
                    pe.wait_ge(s_pja, use.per["A"] * (g + 1) + 8)
                    pe.wait_ge(s_pjd, use.per["D"] * (g + 1) + 4)
                    for u in range(UN):
                        for q in range(QT):
                            n = u * QT + q
                            pe.wait_ge(s_sm, NS * (g + 1) + n - 1)
                            for j in range(2):
                                mm = pe.matmul(SC[n % 2][:, j * BANK:(j + 1) * BANK], qT[u][:, q * P:(q + 1) * P],
                                               kT[u // HPG][:, j * BANK:(j + 1) * BANK], start=True, stop=True)
                            mm.then_inc(s_sc, 1)
                            if u >= 1:
                                transposes(n - QT)
                        if u >= 1:
                            values(u - 1)
                        if u == UN - 1:
                            project(0)
                    for q in range(QT):
                        transposes(NS - QT + q)
                    values(UN - 1)
                    project(1)

                with pe.Fori(0, NKV // 2) as i:
                    for s in range(2):
                        body(i, s)

            programs["SP"].append(sync)
            programs["DVE"].append(vector)
            programs["ACT"].append(scalar)
            programs["POOL"].append(gpsimd)
            programs["PE"].append(tensor)
            return s_pjd, use.per["D"] * (NKV + 1)

        x_done = cross_attention_0()

        def layernorm_to_y(n, before):
            s_y = sem("s_y")
            statistics(n, before)

            def vector(dve):
                dve.wait_ge(s_rstd, n + 1)
                for t in range(NT):
                    dve.tensor_scalar(y3[:, t, :], x3[:, t, :], mv[:, 2 * t:2 * t + 1], rstd[:, t:t + 1],
                                      ALU.subtract, ALU.mult).then_inc(s_y, 1)

            programs["DVE"].append(vector)
            return s_y

        s_rnw, s_rnsq, s_rnstd, s_rnrstd, s_rnh, s_rntr, s_rnhi, s_rnlo = [
            sem(f"rn_{n}") for n in ("w", "sq", "std", "rstd", "h", "tr", "hi", "lo")]

        def rmsnorm(k, s_y, y_count, weight, hi, lo=None, rows=None):
            wrow = sb(f"rn{k}_wrow", [P, D])
            square = sb(f"rn{k}_square", [P, 2 * D])
            sumsq = sb(f"rn{k}_sumsq", [P, NT])
            rms = sb(f"rn{k}_rms", [P, NT])
            rrms = sb(f"rn{k}_rrms", [P, NT])
            s_last = s_rnhi if lo is None else s_rnlo
            k0 = k * NT if lo is None else 0

            def sync(sp):
                sp.wait_ge(s_y, y_count(0))
                sp.dma_start(wrow[:, :], a[weight].partition_broadcast(P)).then_inc(s_rnw, 16)
                if rows:
                    for t in range(NT):
                        sp.wait_ge(s_rnh, k * NT + t + 1)
                        sp.dma_start(rows[0][t * P:(t + 1) * P, :], hslot[:, (t % 2) * D:(t % 2 + 1) * D]).then_inc(rows[1][t % 2], 16)

            def scalar(act):
                for t in range(NT):
                    act.wait_ge(s_y, y_count(t))
                    if t >= 2:
                        act.wait_ge(s_rnsq, k * NT + t - 1)
                    act.activation(square[:, (t % 2) * D:(t % 2 + 1) * D], y3[:, t, :], ACT.Square,
                                   accum_out=sumsq[:, t:t + 1]).then_inc(s_rnsq, 1)
                act.wait_ge(s_rnsq, (k + 1) * NT)
                act.activation(rms[:, :], sumsq[:, :], ACT.Sqrt, scale=1.0 / D, bias=eps[:, 0:1]).then_inc(s_rnstd, 1)
                for t in range(NT):
                    act.wait_ge(s_rntr, k * NT + t + 1)
                    act.activation(hi[:, :, t * P:(t + 1) * P], banks[t % 2][:, :].rearrange("p (c n) -> p c n", c=KC),
                                   ACT.Copy).then_inc(s_rnhi, 1)

            def vector(dve):
                dve.wait_ge(s_rnstd, k + 1)
                dve.reciprocal(rrms[:, :], rms[:, :]).then_inc(s_rnrstd, 1)
                dve.wait_ge(s_rnrstd, k + 1)
                dve.wait_ge(s_rnw, 16 * (k + 1))

                def low(t):
                    dve.wait_ge(s_rnhi, k * NT + t + 1)
                    part = slice(t * P, (t + 1) * P)
                    dve.tensor_tensor(lo[:, :, part], banks[t % 2][:, :].rearrange("p (c n) -> p c n", c=KC),
                                      hi[:, :, part].bitcast(F32), ALU.subtract).then_inc(s_rnlo, 1)

                for t in range(NT):
                    if t >= 2:
                        dve.wait_ge(s_rntr, k * NT + t - 1)
                        if rows:
                            dve.wait_ge(rows[1][t % 2], 16 * (t // 2))
                    dve.scalar_tensor_tensor(hslot[:, (t % 2) * D:(t % 2 + 1) * D], y3[:, t, :], rrms[:, t:t + 1],
                                             wrow[:, :], ALU.mult, ALU.mult).then_inc(s_rnh, 1)
                    if lo is not None and t >= 1:
                        low(t - 1)
                if lo is not None:
                    low(NT - 1)

            def tensor(pe):
                for t in range(NT):
                    pe.wait_ge(s_rnh, k * NT + t + 1)
                    if t >= 2:
                        pe.wait_ge(s_last, k0 + t - 1)
                    for c in range(KC):
                        mm = pe.transpose(banks[t % 2][:, c * P:(c + 1) * P],
                                          hslot[:, (t % 2) * D + c * P:(t % 2) * D + (c + 1) * P], ident[:, :])
                    mm.then_inc(s_rntr, 1)

            programs["SP"].append(sync)
            programs["ACT"].append(scalar)
            programs["DVE"].append(vector)
            programs["PE"].append(tensor)

        phase.close()
        phase = ExitStack()
        y = sb("y", [P, NT * D])
        y3 = y[:, :].rearrange("p (t d) -> p t d", t=NT)
        inner = ExitStack()
        phase, outer = inner, phase
        s_y0 = layernorm_to_y(1, x_done)
        hTa = sb("hT_attn", [P, KC * T])[:, :].rearrange("p (c t) -> p c t", c=KC)
        rmsnorm(0, s_y0, lambda t: t + 1, "L0_ffn_ln_w", hTa)

        def self_attention():
            NKV, HPG, HD = 8, 4, 64
            UN = B * HPG
            NP = UN // 2
            PPB = HPG // 2
            GW = HPG * HD
            SCALE = 1.0 / float(np.sqrt(HD))
            wk = [sb(f"s_wk{s}", [P, KC, 2 * HD]) for s in range(2)]
            wv = [sb(f"s_wv{s}", [P, KC, HD]) for s in range(2)]
            wq = [sb(f"s_wq{s}", [P, KC, GW]) for s in range(2)]
            wo = [sb(f"s_wo{s}", [P, PPB, D]) for s in range(2)]
            raw = [[sb(f"s_raw{b}{r}", [P, S]) for r in range(1 + PPB)] for b in range(B)]
            rot = [[sb(f"s_rot{b}{r}", [P, S]) for r in range(1 + PPB)] for b in range(B)]
            turn = [sb(f"s_turn{i}", [P, S]) for i in range(2)]
            v = [sb(f"s_v{b}", [P, QT, HD]) for b in range(B)]
            p = [sb(f"s_p{i}", [P, QT, S]) for i in range(2)]
            pT = [sb(f"s_pT{i}", [P, QT, S]) for i in range(2)]
            oT = [sb(f"s_oT{j}", [P, S]) for j in range(NP)]
            least = sb("s_least", [P, 2 * QT])
            total = sb("s_total", [P, 2 * QT])
            rtotal = sb("s_rtotal", [P, 2 * QT])
            carry = sb("s_carry", [P, 2 * QT])
            causal = sb("s_causal", [P, S])
            cos, sin, swap = sb("s_cos", [P, S]), sb("s_sin", [P, S]), sb("s_swap", [P, P])

            plan = []
            for b in range(B):
                plan += [(f"r{b}0", "A"), (f"r{b}1", "A"), (f"r{b}2", "A"), (f"v{b}", "A"),
                         (f"t{b}0", "D"), (f"t{b}1", "D"), (f"t{b}2", "D")]
            out0 = [(f"w0{t}", "D") for t in range(QT)]
            out1 = [(f"w1{t}", "D") for t in range(QT)]
            plan += [("o0", "A"), ("o1", "A")] + out0 + [("o2", "A"), ("o3", "A")] + out1
            use = Use(plan)
            assert use.total % 2 == 0
            PJ, SC, TR = banks[0:2], banks[2:6], banks[6:8]
            NS = UN * QT
            s_c = sem("s_c")
            s_w = [sem(f"s_w{i}") for i in range(2)]
            s_pj, s_pja, s_pjd, s_rc, s_tn, s_sc, s_sm, s_ex, s_rt, s_pn, s_tr, s_ta, s_td = [
                sem(f"s_{n}") for n in ("pj", "pja", "pjd", "rc", "tn", "sc", "sm", "ex", "rt", "pn", "tr", "ta", "td")]
            emptied = {"A": s_pja, "D": s_pjd}
            LOADS = 5
            NR = B * (1 + PPB)

            def load(sp, g, s):
                if isinstance(g, int):
                    c1, c2 = slice(g * HD, (g + 1) * HD), slice(g * GW, (g + 1) * GW)
                else:
                    c1, c2 = bass.ds(g * HD, HD), bass.ds(g * GW, GW)
                wk_d = a["L0_ffn_wk"].rearrange("(c p) n -> p c n", p=P)[:, :, c1]
                sp.dma_start(wk[s][:, :, 0:HD], wk_d).then_inc(s_w[s], 16)
                sp.dma_start(wk[s][:, :, HD:], wk_d).then_inc(s_w[s], 16)
                sp.dma_start(wv[s][:, :, :], a["L0_ffn_wv"].rearrange("(c p) n -> p c n", p=P)[:, :, c1]).then_inc(s_w[s], 16)
                sp.dma_start(wq[s][:, :, :], a["L0_ffn_wq"].rearrange("(c p) n -> p c n", p=P)[:, :, c2]).then_inc(s_w[s], 16)
                sp.dma_start(wo[s][:, :, :], a["L0_ffn_wo"][c2, :].rearrange("(c p) n -> p c n", p=P)).then_inc(s_w[s], 16)

            def sync(sp):
                for dst, name in ((causal, "c_causal"), (cos, "c_cos"), (sin, "c_sin"), (swap, "c_swap")):
                    sp.dma_start(dst[:, :], a[name]).then_inc(s_c, 16)
                load(sp, 0, 0)
                load(sp, 1, 1)
                with sp.Fori(0, NKV // 2 - 1) as i:
                    for s in range(2):
                        sp.wait_ge(s_pjd, (i * 2 + s + 2) * use.per["D"])
                        load(sp, i * 2 + (2 + s), s)

            def vector(dve):
                dve.wait_ge(s_c, 64)
                dve.memset(scrap[:, 10:11], 0.0).then_inc(s_pjd, use.per["D"])
                dve.memset(scrap[:, 11:12], 0.0).then_inc(s_sm, NS)
                dve.memset(scrap[:, 12:13], 0.0).then_inc(s_td, NS // 2)

                def body(g):
                    def empty(name):
                        dve.wait_ge(s_pj, use.total * (g + 1) + use.index[name] + 1)
                        return PJ[use.index[name] % 2]

                    def reciprocal(n):
                        if n < 0:
                            dve.memset(scrap[:, 16 + n % 2:17 + n % 2], 0.0)
                            return
                        dve.wait_ge(s_ex, NS * g + n + 1)
                        col = slice(n % (2 * QT), n % (2 * QT) + 1)
                        dve.reciprocal(rtotal[:, col], total[:, col]).then_inc(s_rt, 1)

                    def evacuate(n):
                        u, q = n // QT, n % QT
                        if n % 2 == 0:
                            return
                        if q == 1:
                            before = use.index[f"o{u // 2 - 1}"] if u >= 2 else use.index[f"o{NP - 1}"] - use.total
                            dve.wait_ge(s_pj, use.total * (g + 1) + before + 1)
                        dve.wait_ge(s_tr, NS * (g + 1) + n + 1)
                        dve.tensor_copy(pT[u % 2][:, 0:q + 1, q * P:(q + 1) * P],
                                        TR[1][:, 0:(q + 1) * P].rearrange("p (k n) -> p k n", n=P)).then_inc(s_td, 1)

                    def add_out(b):
                        for t in range(QT):
                            o = empty(f"w{b}{t}")
                            yt = y3[:, b * QT + t, :]
                            dve.tensor_tensor(yt, o[:, :], yt, ALU.add).then_inc(s_pjd, 1)

                    for b in range(B):
                        for r in range(1 + PPB):
                            k = b * (1 + PPB) + r
                            o = empty(f"t{b}{r}")
                            dve.tensor_tensor(turn[k % 2][:, :], o[:, :], sin[:, :], ALU.mult).then_inc(s_pjd, 1)
                            dve.wait_ge(s_pjd, use.per["D"] * (g + 1) + use.nth[use.index[f"t{b}{r}"]][1])
                            dve.wait_ge(s_rc, NR * g + k + 1)
                            dve.tensor_tensor(rot[b][r][:, :], rot[b][r][:, :], turn[k % 2][:, :], ALU.add).then_inc(s_tn, 1)
                    for u in range(UN):
                        for q in range(QT):
                            n = u * QT + q
                            dve.wait_ge(s_sc, NS * g + n + 1)
                            dve.wait_ge(s_tr, NS * (g + 1) + n - 2 * QT + 1)
                            reciprocal(n - 2)
                            w = (q + 1) * P
                            dve.tensor_tensor_reduce(
                                p[u % 2][:, q, 0:w], SC[n % 4][:, 0:w], causal[:, S - w:S], -SCALE, 3.0e38, ALU.add, ALU.min,
                                least[:, n % (2 * QT):n % (2 * QT) + 1]).then_inc(s_sm, 1)
                            if u >= 1:
                                evacuate(n - QT)
                        if u == UN - 1:
                            reciprocal(NS - 2)
                            reciprocal(NS - 1)
                        if u == HPG + 1:
                            add_out(0)
                    for q in range(QT):
                        evacuate(NS - QT + q)
                    add_out(1)

                with dve.Fori(0, NKV) as g:
                    body(g)

            def scalar(act):
                act.activation(scrap[:, 20:21], eps[:, 0:1], ACT.Copy).then_inc(s_pja, use.per["A"])
                act.activation(scrap[:, 21:22], eps[:, 0:1], ACT.Copy).then_inc(s_ta, NS // 2)

                def body(g):
                    def empty(name, dst, w=BANK):
                        act.wait_ge(s_pj, use.total * (g + 1) + use.index[name] + 1)
                        src = PJ[use.index[name] % 2][:, 0:w]
                        if len(dst.shape) == 3:
                            src = src.rearrange("p (k n) -> p k n", k=dst.shape[1])
                        act.activation(dst, src, ACT.Copy).then_inc(s_pja, 1)

                    def evacuate(n):
                        u, q = n // QT, n % QT
                        if n % 2 == 1:
                            return
                        if q == 0:
                            before = use.index[f"o{u // 2 - 1}"] if u >= 2 else use.index[f"o{NP - 1}"] - use.total
                            act.wait_ge(s_pj, use.total * (g + 1) + before + 1)
                        act.wait_ge(s_tr, NS * (g + 1) + n + 1)
                        act.activation(pT[u % 2][:, 0:q + 1, q * P:(q + 1) * P],
                                       TR[0][:, 0:(q + 1) * P].rearrange("p (k n) -> p k n", n=P), ACT.Copy).then_inc(s_ta, 1)

                    for b in range(B):
                        for r in range(1 + PPB):
                            empty(f"r{b}{r}", raw[b][r][:, :])
                        empty(f"v{b}", v[b][:, :, :], QT * HD)
                    for u in range(UN):
                        for q in range(QT):
                            n = u * QT + q
                            w = n % (2 * QT)
                            if u >= 1:
                                evacuate(n - QT)
                            act.wait_ge(s_sm, NS * (g + 1) + n + 1)
                            part = p[u % 2][:, q, 0:(q + 1) * P]
                            act.activation(part, part, ACT.Exp, scale=-1.0, bias=least[:, w:w + 1],
                                           accum_out=total[:, w:w + 1]).then_inc(s_ex, 1)
                        if u % 2 == 0 and u >= 2:
                            empty(f"o{u // 2 - 1}", oT[u // 2 - 1][:, :])
                    for q in range(QT):
                        evacuate(NS - QT + q)
                    empty(f"o{NP - 1}", oT[NP - 1][:, :])

                with act.Fori(0, NKV) as g:
                    body(g)

            def gpsimd(pool):
                pool.wait_ge(s_c, 64)
                with pool.Fori(0, NKV) as g:
                    for b in range(B):
                        for r in range(1 + PPB):
                            pool.wait_ge(s_pja, use.per["A"] * (g + 1) + use.nth[use.index[f"r{b}{r}"]][1])
                            pool.tensor_tensor(rot[b][r][:, :], raw[b][r][:, :], cos[:, :], ALU.mult).then_inc(s_rc, 1)
                    for u in range(UN):
                        for q in range(QT):
                            n = u * QT + q
                            w = n % (2 * QT)
                            part = p[u % 2][:, q, 0:(q + 1) * P]
                            pool.wait_ge(s_rt, NS * g + n + 1)
                            pool.tensor_tensor(carry[:, w:w + 1], rtotal[:, w:w + 1], rtotal[:, w:w + 1], ALU.mult)
                            pool.tensor_scalar(part, part, rtotal[:, w:w + 1], 1.0, ALU.mult, ALU.mult).then_inc(s_pn, 1)

            def tensor(pe):
                pe.wait_ge(s_rnhi, NT)
                pe.wait_ge(s_c, 64)
                pe.wait_ge(s_pja, 1)
                pe.transpose(PJ[0][:, 0:P], ident[:, :], ident[:, :]).then_inc(s_tr, NS)
                pe.transpose(PJ[0][:, 0:P], ident[:, :], ident[:, :]).then_inc(s_pj, use.total)

                def body(i, s):
                    g = i * 2 + s

                    def bank(name):
                        n = use.index[name]
                        e, count = use.emptied(n - 2, g) if n >= 2 else use.emptied(use.total + n - 2, g - 1)
                        pe.wait_ge(emptied[e], count)
                        return PJ[n % 2]

                    def transposes(n):
                        u, q = n // QT, n % QT
                        pe.wait_ge(s_pn, NS * g + n + 1)
                        pe.wait_ge((s_ta, s_td)[n % 2], NS // 2 * (g + 1) + n // 2)
                        for k in range(q + 1):
                            mm = pe.transpose(TR[n % 2][:, k * P:(k + 1) * P], p[u % 2][:, q, k * P:(k + 1) * P], ident[:, :])
                        mm.then_inc(s_tr, 1)

                    def values(j):
                        o = bank(f"o{j}")
                        pe.wait_ge(s_ta, NS // 2 * (g + 1) + (j + 1) * QT)
                        pe.wait_ge(s_td, NS // 2 * (g + 1) + (j + 1) * QT)
                        for h in range(2):
                            for k in range(QT):
                                mm = pe.matmul(o[h * HD:(h + 1) * HD, k * P:], v[j // PPB][:, k, :], pT[h][:, k, k * P:],
                                               start=(k == 0), stop=(k == QT - 1))
                        mm.then_inc(s_pj, 1)

                    def project(b):
                        e, count = use.emptied(use.index[f"o{b * PPB + PPB - 1}"], g)
                        for t in range(QT):
                            o = bank(f"w{b}{t}")
                            if t == 0:
                                pe.wait_ge(emptied[e], count)
                            for j in range(PPB):
                                mm = pe.matmul(o[:, :], oT[b * PPB + j][:, t * P:(t + 1) * P], wo[s][:, j, :],
                                               start=(j == 0), stop=(j == PPB - 1))
                            mm.then_inc(s_pj, 1)

                    pe.wait_ge(s_w[s], 16 * LOADS * (i + 1))
                    for b in range(B):
                        for r in range(1 + PPB):
                            o = bank(f"r{b}{r}")
                            w = wk[s][:, :, :] if r == 0 else wq[s][:, :, (r - 1) * P:r * P]
                            for c in range(KC):
                                mm = pe.matmul(o[:, :], w[:, c, :], hTa[:, c, b * S:(b + 1) * S],
                                               start=(c == 0), stop=(c == KC - 1))
                            mm.then_inc(s_pj, 1)
                        o = bank(f"v{b}")
                        for k in range(QT):
                            for c in range(KC):
                                mm = pe.matmul(o[:, k * HD:(k + 1) * HD], hTa[:, c, b * S + k * P:b * S + (k + 1) * P],
                                               wv[s][:, c, :], start=(c == 0), stop=(c == KC - 1))
                        mm.then_inc(s_pj, 1)
                        for r in range(1 + PPB):
                            e, count = use.emptied(use.index[f"r{b}{r}"], g)
                            o = bank(f"t{b}{r}")
                            pe.wait_ge(emptied[e], count)
                            pe.matmul(o[:, :], swap[:, :], raw[b][r][:, :], start=True, stop=True).then_inc(s_pj, 1)
                    pe.wait_ge(s_pja, use.per["A"] * (g + 1) + 2 * (2 + PPB))
                    pe.wait_ge(s_tn, NR * (g + 1))
                    for u in range(UN):
                        b, pair, half = u // HPG, (u % HPG) // 2, u % 2
                        rows = slice(half * HD, (half + 1) * HD)
                        for q in range(QT):
                            n = u * QT + q
                            pe.wait_ge(s_sm, NS * (g + 1) + n - 3)
                            pe.matmul(SC[n % 4][:, 0:(q + 1) * P], rot[b][1 + pair][rows, q * P:(q + 1) * P],
                                      rot[b][0][rows, 0:(q + 1) * P], start=True, stop=True).then_inc(s_sc, 1)
                            if u >= 1:
                                transposes(n - QT)
                        if u % 2 == 0 and u >= 2:
                            values(u // 2 - 1)
                        if u == HPG + 1:
                            project(0)
                    for q in range(QT):
                        transposes(NS - QT + q)
                    values(NP - 1)
                    project(1)

                with pe.Fori(0, NKV // 2) as i:
                    for s in range(2):
                        body(i, s)

            programs["SP"].append(sync)
            programs["DVE"].append(vector)
            programs["ACT"].append(scalar)
            programs["POOL"].append(gpsimd)
            programs["PE"].append(tensor)
            return s_pjd, use.per["D"] * (NKV + 1)

        y_done = self_attention()
        inner.close()
        phase = outer

        ACCURATE = ((0, 0), (1, 0), (0, 1))
        NE, TOPK, HID = 16, 4, 512
        HC = HID // P
        hh = [sb(f"m_h{i}", [P, KC, T], F32R) for i in range(2)]
        gate = sb("m_gate", [P, NE, NT])
        CAP = T * TOPK // NE * 3 // 2
        CT = CAP // P
        place = sb("m_place", [P, NE + 2, NT])
        where = sb("m_where", [P, TOPK, NT], I32)
        share = sb("m_share", [P, TOPK, NT])
        crowded = sb("m_crowded", [P, 1], I32)
        token = sb("m_token", [P, NT, 2], BF16)
        h_rows = nc.dram_tensor("h_rows", (T, D), F32, kind="Internal").ap()
        y_rows = nc.dram_tensor("y_rows", (NE * CAP, D), F32, kind="Internal").ap()
        s_hrow = [sem(f"m_hrow{i}") for i in range(2)]
        moe_small = ExitStack()
        phase, outer = moe_small, phase
        rmsnorm(1, y_done[0], lambda t: y_done[1], "L0_ffn_ff_ln_w", hh[0], hh[1], (h_rows, s_hrow))

        def route():
            wg = sb("r_wg", [P, KC, NE])
            wgs = [sb(f"r_wg{i}", [P, KC, NE], F32R) for i in range(2)]
            logit = sb("r_logit", [P, NT, NE])
            top = sb("r_top", [P, NT, 8])
            low = sb("r_low", [P, NT])
            rest = sb("r_rest", [P, NT, NE])
            chosen = sb("r_chosen", [P, NT, NE])
            total = sb("r_total", [P, NT])
            rtotal = sb("r_rtotal", [P, NT])
            before = sb("r_before", [P, P])
            ones = sb("r_ones", [P, P])
            first = sb("r_first", [P, NE])
            token32 = sb("r_token", [P, NT, 2])
            run = sb("r_run", [P, NT + 1, NE])
            pos = sb("r_pos", [P, NT, NE])
            row = sb("r_row", [P, NT, NE])
            rank = [sb(f"r_rank{i}", [P, NT, NE]) for i in range(2)]
            pick = sb("r_pickm", [P, NT, NE])
            row_k = sb("r_row_k", [P, TOPK, NT])
            most = sb("r_most", [P, 1])
            s_const2, s_cnt = sem("r_const"), sem("r_cnt")
            s_w, s_hi, s_lo, s_l, s_pick, s_ch, s_ex, s_gate = [
                sem(f"r_{n}") for n in ("w", "hi", "lo", "l", "pick", "ch", "ex", "gate")]

            def sync(sp):
                sp.dma_start(wg[:, :, :], a["L0_ffn_wg"].rearrange("(c p) n -> p c n", p=P)).then_inc(s_w, 16)
                for dst, name in ((before, "c_before"), (ones, "c_ones")):
                    sp.dma_start(dst[:, :], a[name]).then_inc(s_const2, 16)
                sp.dma_start(first[:, :], a["c_first"].partition_broadcast(P)).then_inc(s_const2, 16)
                sp.dma_start(token32[:, :, :], a["c_token"]).then_inc(s_const2, 16)

            def scalar(act):
                act.wait_ge(s_w, 16)
                act.activation(wgs[0][:, :, :], wg[:, :, :], ACT.Copy).then_inc(s_hi, 1)
                act.wait_ge(s_ch, NT + 3)
                act.activation(logit[:, :, :], logit[:, :, :], ACT.Exp).then_inc(s_ex, 1)

            def tensor(pe):
                pe.wait_ge(s_lo, 1)
                pe.wait_ge(s_rnlo, NT)
                for t in range(NT):
                    for n, (i, j) in enumerate(ACCURATE):
                        for c in range(KC):
                            mm = pe.matmul(banks[2][:, t * NE:(t + 1) * NE], hh[i][:, c, t * P:(t + 1) * P], wgs[j][:, c, :],
                                           start=(n == 0 and c == 0), stop=(n == 2 and c == KC - 1))
                mm.then_inc(s_l, 1)
                pe.wait_ge(s_const2, 64)
                pe.wait_ge(s_pick, NT + 2)
                flat = chosen[:, :, :].rearrange("p t e -> p (t e)")
                pe.matmul(banks[3][:, 0:NT * NE], before[:, :], flat, start=True, stop=True)
                pe.matmul(banks[3][:, NT * NE:2 * NT * NE], ones[:, :], flat, start=True, stop=True).then_inc(s_cnt, 1)

            def vector(dve):
                steps = 0

                def step(ins):
                    nonlocal steps
                    steps += 1
                    ins.then_inc(s_ch, 1)
                    dve.wait_ge(s_ch, steps)

                dve.wait_ge(s_hi, 1)
                dve.tensor_tensor(wgs[1][:, :, :], wg[:, :, :], wgs[0][:, :, :].bitcast(F32), ALU.subtract).then_inc(s_lo, 1)
                dve.wait_ge(s_l, 1)
                dve.tensor_copy(logit[:, :, :], banks[2][:, 0:NT * NE].rearrange("p (t e) -> p t e", e=NE)).then_inc(s_pick, 1)
                dve.wait_ge(s_pick, 1)
                for t in range(NT):
                    ins = dve.max(top[:, t, :], logit[:, t, :])
                    ins.then_inc(s_ch, 1)
                steps = NT
                dve.wait_ge(s_ch, NT)
                step(dve.tensor_copy(low[:, :], top[:, :, 0]))
                step(dve.memset(top[:, :, TOPK:], 3.0e38))
                for t in range(NT):
                    dve.match_replace(rest[:, t, :], top[:, t, :], logit[:, t, :], -3.0e38).then_inc(s_pick, 1)
                dve.wait_ge(s_pick, NT + 1)
                dve.tensor_tensor(chosen[:, :, :], logit[:, :, :], rest[:, :, :], ALU.not_equal).then_inc(s_pick, 1)
                dve.wait_ge(s_pick, NT + 2)
                step(dve.tensor_tensor(logit[:, :, :], logit[:, :, :], low[:, :].unsqueeze(2).to_broadcast([P, NT, NE]), ALU.subtract))
                dve.wait_ge(s_ex, 1)
                step(dve.tensor_tensor(logit[:, :, :], logit[:, :, :], chosen[:, :, :], ALU.mult))
                step(dve.tensor_reduce(total[:, :], logit[:, :, :], AX.X, ALU.add))
                step(dve.reciprocal(rtotal[:, :], total[:, :]))
                by_token = gate[:, :, :].rearrange("p e t -> p t e")
                step(dve.tensor_tensor(by_token, logit[:, :, :], rtotal[:, :].unsqueeze(2).to_broadcast([P, NT, NE]), ALU.mult))
                dve.wait_ge(s_const2, 64)
                dve.wait_ge(s_cnt, 1)
                step(dve.tensor_copy(token[:, :, :], token32[:, :, :]))
                step(dve.memset(place[:, :, :], 0.0))
                step(dve.memset(run[:, 0, :], 0.0))
                counts = banks[3][:, 0:2 * NT * NE].rearrange("p (n t e) -> p n t e", n=2, e=NE)
                for t in range(NT):
                    step(dve.tensor_tensor(run[:, t + 1, :], run[:, t, :], counts[:, 1, t, :], ALU.add))
                step(dve.tensor_tensor(pos[:, :, :], run[:, 0:NT, :], counts[:, 0, :, :], ALU.add))
                placed = place[:, 0:NE, :].rearrange("p e t -> p t e")
                step(dve.scalar_tensor_tensor(placed, pos[:, :, :], 1.0, chosen[:, :, :], ALU.add, ALU.mult))
                step(dve.tensor_tensor(row[:, :, :], placed, first[:, :].unsqueeze(1).to_broadcast([P, NT, NE]), ALU.add))
                src = chosen
                for k in range(4):
                    n, dst = 1 << k, rank[k % 2]
                    step(dve.tensor_copy(dst[:, :, 0:n], src[:, :, 0:n]))
                    step(dve.tensor_tensor(dst[:, :, n:], src[:, :, n:], src[:, :, 0:NE - n], ALU.add))
                    src = dst
                step(dve.tensor_tensor(rank[0][:, :, :], src[:, :, :], chosen[:, :, :], ALU.mult))
                for k in range(TOPK):
                    for value, dst in ((row[:, :, :], row_k), (by_token, share)):
                        step(dve.scalar_tensor_tensor(pick[:, :, :], rank[0][:, :, :], k + 1.0, value, ALU.is_equal, ALU.mult))
                        step(dve.tensor_reduce(dst[:, k, :], pick[:, :, :], AX.X, ALU.add))
                step(dve.tensor_copy(where[:, :, :], row_k[:, :, :]))
                step(dve.tensor_reduce(most[:, :], run[:, NT, :], AX.X, ALU.max))
                dve.tensor_scalar(crowded[:, :], most[:, :], float(CAP), None, ALU.is_gt).then_inc(s_gate, 1)

            programs["SP"].append(sync)
            programs["ACT"].append(scalar)
            programs["PE"].append(tensor)
            programs["DVE"].append(vector)
            return s_gate

        s_gated = route()
        moe_small.close()
        phase = outer

        def experts():
            NH = T // BANK
            TPH = NT // NH
            NS = NH * HC
            raw = [sb(f"e_raw{i}", [P, KC, HID]) for i in range(2)]
            w1 = [[sb(f"e_w1{s}{i}", [P, KC, HID], F32R) for i in range(2)] for s in range(2)]
            w3 = [[sb(f"e_w3{s}{i}", [P, KC, HID], F32R) for i in range(2)] for s in range(2)]
            w2 = [sb(f"e_w2{i}", [P, HC, D], F32R) for i in range(2)]
            silu = [sb(f"e_silu{i}", [P, BANK]) for i in range(2)]
            act32 = [sb(f"e_act{i}", [P, BANK]) for i in range(2)]
            carry = sb("e_carry", [P, 2])
            aT0 = [sb(f"e_aT0{i}", [P, HC, BANK], F32R) for i in range(2)]
            with ExitStack() as every_only:
                aT = [aT0, [every_only.enter_context(nc.sbuf_tensor(f"e_aT1{i}", [P, HC, BANK], F32R)) for i in range(2)]]
            with ExitStack() as few_only:
                rows = few_only.enter_context(nc.sbuf_tensor("e_rows", [P, CT, D], F32))
                mine = few_only.enter_context(nc.sbuf_tensor("e_mine", [P, NT, CAP], BF16))
                count_up = few_only.enter_context(nc.sbuf_tensor("e_count_up", [P, CAP], F32))
                ids32 = few_only.enter_context(nc.sbuf_tensor("e_ids32", [P, CT], F32))
                ids = [few_only.enter_context(nc.sbuf_tensor(f"e_ids{i}", [P, CT], I32)) for i in range(2)]
            GU, Y = pairs[0:2], banks[4:6]
            s_in = [sem(f"e_in{i}") for i in range(2)]
            s_mine, s_list, s_id, s_xt, s_xh, s_xl, s_got, s_add, s_done = [
                sem(f"e_{n}") for n in ("mine", "list", "id", "xt", "xh", "xl", "got", "add", "done")]
            s_up = sem("e_up")
            s_back = [sem(f"e_back{i}") for i in range(2)]
            s_st = [sem(f"e_st{i}") for i in range(2)]
            s_hi, s_lo, s_gu, s_sg, s_a, s_ah, s_al, s_y, s_yd = [
                sem(f"e_{n}") for n in ("hi", "lo", "gu", "sg", "a", "ah", "al", "y", "yd")]
            NW = 3 * NE

            def load(sp, n, e, kind):
                if not isinstance(e, int):
                    src = a[f"L0_ffn_{kind}"][bass.ds(e, 1), :, :].rearrange("e (c p) n -> p (e c) n", p=P)
                else:
                    src = a[f"L0_ffn_{kind}"][e].rearrange("(c p) n -> p c n", p=P)
                sp.dma_start(raw[n % 2][:, :, :], src).then_inc(s_in[n % 2], 16)

            def every_sync(sp):
                load(sp, 0, 0, "w1")
                load(sp, 1, 0, "w3")

                def body(i, s, last):
                    e = i * 2 + s
                    for k, kind in enumerate(("w2", "w1", "w3")):
                        if last and k:
                            continue
                        sp.wait_ge(s_lo, 3 * e + k + 1)
                        load(sp, 3 * s + k, e + (1 if k else 0), kind)

                with sp.Fori(0, NE // 2 - 1) as i:
                    for s in range(2):
                        body(i, s, False)
                body(NE // 2 - 1, 0, False)
                body(NE // 2 - 1, 1, True)

            def high(act, dst, n_in, parity):
                act.wait_ge(s_in[parity], n_in)
                act.activation(dst[:, :, :], raw[parity][:, :, :], ACT.Copy).then_inc(s_hi, 1)

            def every_scalar(act):
                high(act, w1[0][0], 16, 0)
                high(act, w3[0][0], 16, 1)

                def body(i, s, last):
                    e = i * 2 + s

                    def part_high(k):
                        act.wait_ge(s_a, NS * (e + 1) + k + 1)
                        act.activation(aT[k // HC][0][:, k % HC, :], act32[k % 2][:, :], ACT.Copy).then_inc(s_ah, 1)

                    act.wait_ge(s_y, NS * (e + 1))
                    high(act, w2[0], 16 * (3 * i + (1 if s == 0 else 3)) + (0 if s else 16), s)
                    for k in range(NS):
                        act.wait_ge(s_gu, NS * (e + 1) + k + 1)
                        act.activation(silu[k % 2][:, :], GU[k % 2][:, 0:BANK], ACT.Silu).then_inc(s_sg, 1)
                        if k >= 1:
                            part_high(k - 1)
                        if not last and k in (2, 5):
                            m = 3 * s + (1 if k == 2 else 2)
                            high(act, (w1 if k == 2 else w3)[1 - s][0], 16 * (3 * i + 1 + m // 2 + 1), m % 2)
                    part_high(NS - 1)

                with act.Fori(0, NE // 2 - 1) as i:
                    for s in range(2):
                        body(i, s, False)
                body(NE // 2 - 1, 0, False)
                body(NE // 2 - 1, 1, True)

            def low(pool, dst, n, parity):
                pool.wait_ge(s_hi, n)
                pool.tensor_tensor(dst[1][:, :, :], raw[parity][:, :, :], dst[0][:, :, :].bitcast(F32),
                                   ALU.subtract).then_inc(s_lo, 1)

            def every_gpsimd(pool):
                low(pool, w1[0], 1, 0)
                low(pool, w3[0], 2, 1)

                def body(i, s, last):
                    e = i * 2 + s
                    low(pool, w2, 3 * e + 3, s)
                    if not last:
                        low(pool, w1[1 - s], 3 * e + 4, (3 * s + 1) % 2)
                        low(pool, w3[1 - s], 3 * e + 5, (3 * s + 2) % 2)

                with pool.Fori(0, NE // 2 - 1) as i:
                    for s in range(2):
                        body(i, s, False)
                body(NE // 2 - 1, 0, False)
                body(NE // 2 - 1, 1, True)

            def every_vector(dve):
                dve.memset(scrap[:, 24:25], 0.0).then_inc(s_a, NS)
                dve.memset(scrap[:, 25:26], 0.0).then_inc(s_yd, NT)

                def body(i, s):
                    e = i * 2 + s

                    def part_low(k):
                        dve.wait_ge(s_ah, NS * e + k + 1)
                        dve.tensor_tensor(aT[k // HC][1][:, k % HC, :], act32[k % 2][:, :],
                                          aT[k // HC][0][:, k % HC, :].bitcast(F32), ALU.subtract).then_inc(s_al, 1)

                    for k in range(NS):
                        if k >= 2:
                            dve.wait_ge(s_al, NS * e + k - 1)
                        dve.wait_ge(s_sg, NS * e + k + 1)
                        dve.tensor_tensor(act32[k % 2][:, :], silu[k % 2][:, :], GU[k % 2][:, BANK:], ALU.mult).then_inc(s_a, 1)
                        if k >= 1:
                            part_low(k - 1)
                    part_low(NS - 1)
                    for t in range(NT):
                        dve.wait_ge(s_y, NS * (e + 1) + t + 1)
                        yt = y3[:, t, :]
                        g = gate[:, :, :].rearrange("p e t -> p (e t)")[:, bass.ds(e * NT + t, 1)]
                        dve.scalar_tensor_tensor(yt, Y[t % 2][:, :], g, yt, ALU.mult, ALU.add).then_inc(s_yd, 1)

                with dve.Fori(0, NE // 2) as i:
                    for s in range(2):
                        body(i, s)
                dve.wait_ge(s_yd, NT * (NE + 1))
                dve.memset(scrap[:, 26:27], 0.0).then_inc(s_done, 1)

            def every_tensor(pe):
                pe.transpose(banks[6][:, 0:P], ident[:, :], ident[:, :]).then_inc(s_gu, NS)
                pe.transpose(banks[6][:, 0:P], ident[:, :], ident[:, :]).then_inc(s_y, NS)

                def body(i, s):
                    e = i * 2 + s
                    for k in range(NS):
                        h, m = k // HC, k % HC
                        if k == 0:
                            pe.wait_ge(s_lo, 3 * e + 2)
                        pe.wait_ge(s_a, NS * (e + 1) + k - 1)
                        for j, w in enumerate((w1[s], w3[s])):
                            for n, (x0, x1) in enumerate(ACCURATE):
                                for c in range(KC):
                                    mm = pe.matmul(GU[k % 2][:, j * BANK:(j + 1) * BANK], w[x0][:, c, m * P:(m + 1) * P],
                                                   hh[x1][:, c, h * BANK:(h + 1) * BANK],
                                                   start=(n == 0 and c == 0), stop=(n == 2 and c == KC - 1))
                        mm.then_inc(s_gu, 1)
                    pe.wait_ge(s_lo, 3 * e + 3)
                    for t in range(NT):
                        h = t // TPH
                        if t % TPH == 0:
                            pe.wait_ge(s_al, NS * e + (h + 1) * HC)
                        pe.wait_ge(s_yd, NT * (e + 1) + t - 1)
                        for n, (x0, x1) in enumerate(ACCURATE):
                            for m in range(HC):
                                mm = pe.matmul(Y[t % 2][:, :], aT[h][x0][:, m, (t % TPH) * P:(t % TPH + 1) * P], w2[x1][:, m, :],
                                               start=(n == 0 and m == 0), stop=(n == 2 and m == HC - 1))
                        mm.then_inc(s_y, 1)

                with pe.Fori(0, NE // 2) as i:
                    for s in range(2):
                        body(i, s)

            TR = banks[6:8]
            XS = [[hh[i][:, :, s * CAP:(s + 1) * CAP] for i in range(2)] for s in range(2)]

            def few_sync(sp):
                def store(e, s):
                    for r in range(CT):
                        sp.wait_ge(s_yd, CT * (e + 1) + r + 1)
                        k = (CT * s + r) % 2
                        row = e * CAP + r * P
                        dst = y_rows[row:row + P, :] if isinstance(e, int) else y_rows[bass.ds(row, P), :]
                        sp.dma_start(dst, hslot[:, k * D:(k + 1) * D]).then_inc(s_st[k], 16)

                def body(i, s, first, last):
                    e = i * 2 + s
                    for k, kind in enumerate(("w2", "w1", "w3")):
                        if not (last and k):
                            sp.wait_ge(s_lo, 3 * e + k + 1)
                            load(sp, 3 * s + k, e + (1 if k else 0), kind)
                        if k == 1 and not first:
                            store(e - 1, 1 - s)

                sp.dma_start(count_up[:, :], a["c_count_up"].partition_broadcast(P)).then_inc(s_up, 16)
                load(sp, 0, 0, "w1")
                load(sp, 1, 0, "w3")
                body(0, 0, True, False)
                body(0, 1, False, False)
                with sp.Fori(1, NE // 2 - 1) as i:
                    for s in range(2):
                        body(i, s, False, False)
                body(NE // 2 - 1, 0, False, False)
                body(NE // 2 - 1, 1, False, True)
                store(NE - 1, 1)

            def few_scalar(act):
                high(act, w1[0][0], 16, 0)
                high(act, w3[0][0], 16, 1)

                def tokens(e, s):
                    for c in range(KC):
                        act.wait_ge(s_xt, KC * e + c + 1)
                        act.activation(XS[s][0][:, c, :], TR[c % 2][:, 0:CAP], ACT.Copy).then_inc(s_xh, 1)

                tokens(0, 0)

                def body(i, s, last):
                    e = i * 2 + s

                    def part_high(m):
                        act.wait_ge(s_a, HC * (e + 1) + m + 1)
                        act.activation(aT0[0][:, m, 0:CAP], act32[m % 2][:, 0:CAP], ACT.Copy).then_inc(s_ah, 1)

                    act.wait_ge(s_y, CT * (e + 1))
                    high(act, w2[0], 16 * (3 * i + (1 if s == 0 else 3)) + (0 if s else 16), s)
                    for m in range(HC):
                        act.wait_ge(s_gu, HC * (e + 1) + m + 1)
                        act.activation(silu[m % 2][:, 0:CAP], GU[m % 2][:, 0:CAP], ACT.Silu).then_inc(s_sg, 1)
                        if m >= 1:
                            part_high(m - 1)
                        if not last and m in (1, 2):
                            n = 3 * s + m
                            high(act, (w1 if m == 1 else w3)[1 - s][0], 16 * (3 * i + 1 + n // 2 + 1), n % 2)
                    part_high(HC - 1)
                    tokens(e + 1, 1 - s)

                with act.Fori(0, NE // 2 - 1) as i:
                    for s in range(2):
                        body(i, s, False)
                body(NE // 2 - 1, 0, False)
                body(NE // 2 - 1, 1, True)

            def few_gpsimd(pool):
                pool.wait_ge(s_hrow[0], 16 * NT // 2)
                pool.wait_ge(s_hrow[1], 16 * NT // 2)

                def gather(e, s):
                    pool.wait_ge(s_id, 2 * e + 2)
                    if not (isinstance(e, int) and e == 0):
                        pool.wait_ge(s_xt, KC * e)
                    pool.tensor_tensor(carry[:, s:s + 1], eps[:, 0:1], eps[:, 0:1], ALU.mult)
                    for r in range(CT):
                        pool.indirect_dma_start(rows[:, r, :], None, h_rows,
                                                bass.IndirectOffsetOnAxis(ap=ids[s][:, r:r + 1], axis=0)).then_inc(s_got, 16)

                gather(0, 0)
                low(pool, w1[0], 1, 0)
                low(pool, w3[0], 2, 1)

                def body(i, s, last):
                    e = i * 2 + s
                    gather(e + 1, 1 - s)
                    low(pool, w2, 3 * e + 3, s)
                    if not last:
                        low(pool, w1[1 - s], 3 * e + 4, (3 * s + 1) % 2)
                        low(pool, w3[1 - s], 3 * e + 5, (3 * s + 2) % 2)

                with pool.Fori(0, NE // 2 - 1) as i:
                    for s in range(2):
                        body(i, s, False)
                body(NE // 2 - 1, 0, False)
                body(NE // 2 - 1, 1, True)
                for k in range(2):
                    pool.wait_ge(s_st[k], 16 * (NE * CT // 2 + 1))
                pool.wait_ge(s_lo, 3 * NE)
                for t in range(NT):
                    if t >= 2:
                        pool.wait_ge(s_add, TOPK * (t - 1))
                    for k in range(TOPK):
                        pool.indirect_dma_start(raw[t % 2][:, k, :], None, y_rows,
                                                bass.IndirectOffsetOnAxis(ap=where[:, k, t:t + 1], axis=0)).then_inc(s_back[t % 2], 16)

            def few_vector(dve):
                dve.memset(scrap[:, 44:45], 0.0).then_inc(s_a, HC)
                dve.memset(scrap[:, 45:46], 0.0).then_inc(s_yd, CT)
                dve.memset(scrap[:, 46:47], 0.0).then_inc(s_al, 2)
                dve.memset(scrap[:, 47:48], 0.0).then_inc(s_st[0], 16)
                dve.memset(scrap[:, 48:49], 0.0).then_inc(s_st[1], 16)
                flat = place[:, :, :].rearrange("p e t -> p (e t)")

                def mark(e):
                    if not (isinstance(e, int) and e == 0):
                        dve.wait_ge(s_list, e)
                    for t in range(NT):
                        col = flat[:, t + e * NT:t + e * NT + 1] if isinstance(e, int) else flat[:, bass.ds(e * NT + t, 1)]
                        dve.tensor_scalar(mine[:, t, :], count_up[:, :], col, None, ALU.is_equal).then_inc(s_mine, 1)

                def listed(e, s):
                    dve.wait_ge(s_list, e + 1)
                    lists = Y[0][:, 0:2 * CT].rearrange("p (r k) -> p r k", k=2)
                    dve.tensor_reduce(ids32[:, :], lists, AX.X, ALU.add).then_inc(s_id, 1)
                    dve.wait_ge(s_id, 2 * e + 1)
                    dve.tensor_copy(ids[s][:, :], ids32[:, :]).then_inc(s_id, 1)

                def tokens(e, s):
                    for c in range(KC):
                        dve.wait_ge(s_xh, KC * e + c + 1)
                        dve.tensor_tensor(XS[s][1][:, c, :], TR[c % 2][:, 0:CAP], XS[s][0][:, c, :].bitcast(F32),
                                          ALU.subtract).then_inc(s_xl, 1)

                dve.wait_ge(s_up, 16)
                mark(0)
                listed(0, 0)
                mark(1)
                listed(1, 1)
                tokens(0, 0)

                def body(i, s):
                    e = i * 2 + s

                    def part_low(m):
                        dve.wait_ge(s_ah, HC * e + m + 1)
                        dve.tensor_tensor(aT0[1][:, m, 0:CAP], act32[m % 2][:, 0:CAP], aT0[0][:, m, 0:CAP].bitcast(F32),
                                          ALU.subtract).then_inc(s_al, 1)

                    mark(e + 2)
                    for m in range(HC):
                        dve.wait_ge(s_al, HC * e + m + 1)
                        dve.wait_ge(s_sg, HC * e + m + 1)
                        dve.tensor_tensor(act32[m % 2][:, 0:CAP], silu[m % 2][:, 0:CAP], GU[m % 2][:, BANK:BANK + CAP],
                                          ALU.mult).then_inc(s_a, 1)
                        if m >= 1:
                            part_low(m - 1)
                    part_low(HC - 1)
                    listed(e + 2, s)
                    tokens(e + 1, 1 - s)
                    for r in range(CT):
                        k = (CT * s + r) % 2
                        dve.wait_ge(s_y, CT * (e + 1) + r + 1)
                        dve.wait_ge(s_st[k], (CT * 16) * i + 16 * ((CT * s + r) // 2 + (0 if k == (CT * s + r) % 2 else 1)) + 16)
                        dve.tensor_copy(hslot[:, k * D:(k + 1) * D], Y[(r + 1) % 2][:, :]).then_inc(s_yd, 1)

                with dve.Fori(0, NE // 2) as i:
                    for s in range(2):
                        body(i, s)
                for t in range(NT):
                    dve.wait_ge(s_back[t % 2], 16 * TOPK * (t // 2 + 1))
                    for k in range(TOPK):
                        yt = y3[:, t, :]
                        dve.scalar_tensor_tensor(yt, raw[t % 2][:, k, :], share[:, k, t:t + 1], yt, ALU.mult, ALU.add).then_inc(s_add, 1)
                        dve.wait_ge(s_add, TOPK * t + k + 1)
                dve.memset(scrap[:, 49:50], 0.0).then_inc(s_done, 1)

            def few_tensor(pe):
                pe.transpose(banks[6][:, 0:P], ident[:, :], ident[:, :]).then_inc(s_gu, HC)
                pe.transpose(banks[6][:, 0:P], ident[:, :], ident[:, :]).then_inc(s_y, CT)

                def order(e):
                    pe.wait_ge(s_mine, NT * (e + 1))
                    for r in range(CT):
                        for t in range(NT):
                            mm = pe.matmul(Y[0][:, 2 * r:2 * r + 2], mine[:, t, r * P:(r + 1) * P], token[:, t, :],
                                           start=(t == 0), stop=(t == NT - 1))
                    mm.then_inc(s_list, 1)

                def turn(e):
                    pe.wait_ge(s_got, 16 * CT * (e + 1))
                    for c in range(KC):
                        if not (isinstance(e, int) and e == 0 and c < 2):
                            pe.wait_ge(s_xl, KC * e + c - 1)
                        for r in range(CT):
                            mm = pe.transpose(TR[c % 2][:, r * P:(r + 1) * P], rows[:, r, c * P:(c + 1) * P], ident[:, :])
                        mm.then_inc(s_xt, 1)

                order(0)
                pe.wait_ge(s_id, 1)
                order(1)
                turn(0)

                def body(i, s):
                    e = i * 2 + s
                    pe.wait_ge(s_lo, 3 * e + 2)
                    pe.wait_ge(s_xl, KC * (e + 1))
                    for m in range(HC):
                        pe.wait_ge(s_a, HC * (e + 1) + m - 1)
                        for j, w in enumerate((w1[s], w3[s])):
                            for n, (x0, x1) in enumerate(ACCURATE):
                                for c in range(KC):
                                    mm = pe.matmul(GU[m % 2][:, j * BANK:j * BANK + CAP], w[x0][:, c, m * P:(m + 1) * P],
                                                   XS[s][x1][:, c, :], start=(n == 0 and c == 0), stop=(n == 2 and c == KC - 1))
                        mm.then_inc(s_gu, 1)
                    pe.wait_ge(s_yd, CT * (e + 1) - 1)
                    order(e + 2)
                    turn(e + 1)
                    pe.wait_ge(s_lo, 3 * e + 3)
                    pe.wait_ge(s_al, HC * (e + 1) + 2)
                    for r in range(CT):
                        pe.wait_ge(s_yd, CT * (e + 1) + max(r - 1, 0))
                        if r == 1:
                            pe.wait_ge(s_id, 2 * e + 5)
                        for n, (x0, x1) in enumerate(ACCURATE):
                            for m in range(HC):
                                mm = pe.matmul(Y[(r + 1) % 2][:, :], aT0[x0][:, m, r * P:(r + 1) * P], w2[x1][:, m, :],
                                               start=(n == 0 and m == 0), stop=(n == 2 and m == HC - 1))
                        mm.then_inc(s_y, 1)

                with pe.Fori(0, NE // 2) as i:
                    for s in range(2):
                        body(i, s)

            def either(every, few):
                def stage(engine):
                    engine.wait_ge(s_gated, 1)
                    flag = engine.value_load(crowded[0:1, 0:1], min_val=0, max_val=1)
                    with engine.If(flag > 0):
                        every(engine)
                    with engine.Else():
                        few(engine)
                return stage

            programs["SP"].append(either(every_sync, few_sync))
            programs["ACT"].append(either(every_scalar, few_scalar))
            programs["POOL"].append(either(every_gpsimd, few_gpsimd))
            programs["DVE"].append(either(every_vector, few_vector))
            programs["PE"].append(either(every_tensor, few_tensor))
            return s_done, 1


        moe_done = experts()

        s_x1 = sem("s_x1")

        def add_inner(dve):
            dve.wait_ge(*moe_done)
            for t in range(NT):
                dve.scalar_tensor_tensor(x3[:, t, :], y3[:, t, :], tgate[:, 2:3], x3[:, t, :], ALU.mult, ALU.add).then_inc(s_x1, 1)

        programs["DVE"].append(add_inner)
        phase.close()
        phase = ExitStack()

        xT3 = sb("hT_x1", [P, KC * T])[:, :].rearrange("p (c t) -> p c t", c=KC)
        cxT3 = sb("ctxT1", [P, VC * B * S2])[:, :].rearrange("p (c t) -> p c t", c=VC)
        cslot1 = sb("cslot1", [P, 4 * DV])
        transpose_context(1, cxT3, cslot1, (s_x1, NT))
        layernorm(2, 1, (s_x1, NT), xT3)

        def cross_attention_1():
            HD, HPG, NG = 32, 4, 4
            DCA = 16
            GW = HPG * HD
            UN = B * HPG
            NK = S2 // P
            MAIN = S2 - DCA
            SCALE = 1.0 / float(np.sqrt(HD))
            HALF = S // 2
            LAG, RING = 3, 4
            STACK = 3 * HD
            PAIR = HPG // 2
            wq = sb("z_wq", [P, KC, GW])
            wkv = sb("z_wkv", [P, VC, HPG, 2 * HD])
            wd = sb("z_wd", [P, VC, 2, GW])
            wo = sb("z_wo", [P, PAIR, D])
            bq, bkv, bd = sb("z_bq", [P, GW]), sb("z_bkv", [P, HPG, 2 * HD]), sb("z_bd", [P, 2, GW])
            GM = (KC + 2 * VC + 3) * HPG
            wmean = sb("z_wmean", [P, GM])
            norms = sb("z_norms", [P, 6, HD])
            qnorm = sb("z_qnorm", [P, 2, HD])
            tbo = sb("z_tbo", [P, D])
            part = sb("z_part", [P, 2])
            RQ, RK = NT * HPG, NK * HPG
            RD = B * HPG
            var = sb("z_var", [P, RQ + RD + B * RK])
            dev = sb("z_dev", [P, RQ + RD + B * RK])
            rdev = sb("z_rdev", [P, RQ + RD + B * RK])
            qS = sb("z_qS", [STACK, HPG, T], F32R)
            kS = sb("z_kS", [STACK, HPG, B * S2], F32R)
            vS = sb("z_vS", [P, NC_T, PAIR, 6 * HD], F32R)
            oT = [sb(f"z_oT{b}", [P, PAIR, S]) for b in range(B)]
            most = sb("z_most", [P, RING, 2])
            total = sb("z_total", [P, RING, 2])
            rtotal = sb("z_rtotal", [P, RING, 2])
            carry = sb("z_carry", [P, RING])
            with ExitStack() as front:
                def fb(name, shape, dt=F32):
                    return front.enter_context(nc.sbuf_tensor(name, shape, dt))
                kv = fb("z_kv", [P, NC_T, HPG, 2 * HD])
                cq = fb("z_cq", [P, NT + B, GW])
                dv = fb("z_dv", [P, B, GW])
                dk = fb("z_dk", [P, B, GW])
                sq = fb("z_sq", [P, RQ + RD, HD])
                split = [fb(f"z_split{i}", [P, RK, 3, HD], F32R) for i in range(2)]
            with ExitStack() as back:
                p = [back.enter_context(nc.sbuf_tensor(f"z_p{i}", [P, S2], F32)) for i in range(RING)]
                pT = [back.enter_context(nc.sbuf_tensor(f"z_pT{i}", [P, NK, S], F32R)) for i in range(2)]

            plan = [(f"d{b}", "D") for b in range(B)] + [("q0", "D"), ("q1", "D")] + [(f"kv{n}", "D") for n in range(PAIRS)]
            plan += [(f"tq{h}{i}", "A") for h in range(HPG) for i in range(2)]
            plan += [(f"tk{b}{h}{i}", "A") for b in range(B) for h in range(HPG) for i in range(2)]
            for b in range(B):
                plan += [(f"o{b}{i}", "A") for i in range(PAIR)] + [(f"w{b}{t}", "D") for t in range(QT)]
            use = Use(plan)
            assert use.total % 2 == 0
            PJ, SC, TR = banks[0:2], pairs[1:3], banks[6:8]
            NS = UN * QT
            OUT = HPG * QT + LAG + 2
            assert LAG % 2
            s_c, s_qn, s_tbo, s_w, s_wo = sem("z_c"), sem("z_qn"), sem("z_tbo"), sem("z_w"), sem("z_wo")
            s_pj, s_pja, s_pjd, s_cw, s_ch, s_sq, s_dev, s_nrm, s_aff, s_hi, s_lo, s_sc, s_sm, s_ex, s_rt, s_pn, s_tr, s_th, s_tl = [
                sem(f"z_{n}") for n in ("pj", "pja", "pjd", "cw", "ch", "sq", "dev", "nrm", "aff", "hi", "lo", "sc", "sm", "ex",
                                        "rt", "pn", "tr", "th", "tl")]
            emptied = {"A": s_pja, "D": s_pjd}
            LOADS = 8
            STEPS = 16
            rows = [slice(0, RQ + RD)] + [slice(RQ + RD + b * RK, RQ + RD + (b + 1) * RK) for b in range(B)]

            def headrows(b):
                r = kv[:, b * NK:(b + 1) * NK, :, :].rearrange("p t h d -> p (t h) d")
                return r[:, :, 0:HD], r[:, :, HD:]

            cqrows = cq[:, :, :].rearrange("p t (h d) -> p (t h) d", d=HD)
            centred = [wq[:, :, :].rearrange("p c (h d) -> p (c h) d", d=HD),
                       wkv[:, :, :, :].rearrange("p c h d -> p (c h) d")[:, :, 0:HD],
                       wd[:, 0, 0, :].rearrange("p (h d) -> p h d", d=HD), wd[:, 1, 0, :].rearrange("p (h d) -> p h d", d=HD),
                       bq[:, :].rearrange("p (h d) -> p h d", d=HD), bkv[:, :, 0:HD],
                       bd[:, 0, :].rearrange("p (h d) -> p h d", d=HD)]
            assert VC == 2 and sum(w.shape[1] for w in centred) == GM
            NCW = 2 * len(centred) + 1

            def done(engine, j, name):
                e, count = use.emptied(use.index[name], j)
                engine.wait_ge(emptied[e], count)

            def sync(sp):
                sp.wait_ge(s_x1, NT)
                for k, name in enumerate(("qn_w", "qn_b", "kn_w", "kn_b", "kn_dca_w", "kn_dca_b")):
                    sp.dma_start(norms[:, k, :], a[f"L1_xattn_{name}"].partition_broadcast(P)).then_inc(s_c, 16)
                sp.dma_start(tbo[:, :], a["L1_xattn_bo"].partition_broadcast(P)).then_inc(s_c, 16)
                sp.dma_start(part[:, :], a["c_part"]).then_inc(s_c, 16)

                def load(j):
                    one = slice(0, GW) if isinstance(j, int) else bass.ds(j * GW, GW)
                    two = slice(0, 2 * GW) if isinstance(j, int) else bass.ds(j * 2 * GW, 2 * GW)
                    val = slice(D, D + GW) if isinstance(j, int) else bass.ds(j * GW + D, GW)
                    wd_d = a["L1_xattn_Wkv_dca"].rearrange("(c p) n -> p c n", p=P)
                    sp.dma_start(wq[:, :, :], a["L1_xattn_Wq"].rearrange("(c p) n -> p c n", p=P)[:, :, one]).then_inc(s_w, 16)
                    sp.dma_start(wkv[:, :, :, :].rearrange("p c h d -> p c (h d)"),
                                 a["wkv"].rearrange("(c p) n -> p c n", p=P)[:, :, two]).then_inc(s_w, 16)
                    sp.dma_start(wd[:, :, 0, :], wd_d[:, :, one]).then_inc(s_w, 16)
                    sp.dma_start(wd[:, :, 1, :], wd_d[:, :, val]).then_inc(s_w, 16)
                    sp.dma_start(bq[:, :], a["L1_xattn_bq"][one].partition_broadcast(P)).then_inc(s_w, 16)
                    sp.dma_start(bkv[:, :, :].rearrange("p h d -> p (h d)"), a["bkv"][two].partition_broadcast(P)).then_inc(s_w, 16)
                    sp.dma_start(bd[:, 0, :], a["L1_xattn_bkv_dca"][one].partition_broadcast(P)).then_inc(s_w, 16)
                    sp.dma_start(bd[:, 1, :], a["L1_xattn_bkv_dca"][val].partition_broadcast(P)).then_inc(s_w, 16)

                def load_out(j):
                    for i in range(PAIR):
                        for h in range(2):
                            first = (i * 2 + h) * HD
                            src = a["L1_xattn_Wo"][(slice(first, first + HD) if isinstance(j, int) else bass.ds(j * GW + first, HD)), :]
                            for n in range(2):
                                sp.dma_start(wo[(2 * h + n) * HD:(2 * h + n + 1) * HD, i, :], src).then_inc(s_wo, 16)

                load(0)
                load_out(0)
                with sp.Fori(0, NG - 1) as j:
                    sp.wait_ge(s_pjd, use.per["D"] * (j + 1) + use.nth[use.index[f"kv{PAIRS - 1}"]][1])
                    load(j + 1)
                    sp.wait_ge(s_pjd, use.per["D"] * (j + 2))
                    load_out(j + 1)
                sp.wait_ge(s_pjd, use.per["D"] * NG + use.nth[use.index[f"kv{PAIRS - 1}"]][1])
                load(0)

            def vector(dve):
                dve.wait_ge(s_c, 16 * 8)
                dve.tensor_scalar(qnorm[:, :, :], norms[:, 0:2, :], SCALE, None, ALU.mult).then_inc(s_qn, 1)
                dve.tensor_scalar(tbo[:, :], tbo[:, :], tgate[:, 1:2], None, ALU.mult).then_inc(s_tbo, 1)
                dve.memset(scrap[:, 28:29], 0.0).then_inc(s_pjd, use.per["D"])
                dve.memset(scrap[:, 29:30], 0.0).then_inc(s_tl, 2 * NS)
                dve.wait_ge(s_qn, 2)

                def centre(j):
                    dve.wait_ge(s_w, 16 * LOADS * (j + 1))
                    at = 0
                    for w in centred:
                        dve.tensor_reduce(wmean[:, at:at + w.shape[1]], w, AX.X, ALU.add).then_inc(s_cw, 1)
                        at += w.shape[1]
                    dve.wait_ge(s_cw, NCW * j + NCW // 2)
                    dve.tensor_scalar(wmean[:, :], wmean[:, :], 1.0 / HD, None, ALU.mult).then_inc(s_cw, 1)
                    dve.wait_ge(s_cw, NCW * j + NCW // 2 + 1)
                    at = 0
                    for w in centred:
                        dve.tensor_tensor(w, w, wmean[:, at:at + w.shape[1]].unsqueeze(2).to_broadcast(list(w.shape)),
                                          ALU.subtract).then_inc(s_cw, 1)
                        at += w.shape[1]
                    dve.wait_ge(s_cw, NCW * (j + 1))

                def body(j):
                    steps = 0

                    def step(ins):
                        nonlocal steps
                        steps += 1
                        ins.then_inc(s_ch, 1)
                        dve.wait_ge(s_ch, STEPS * j + steps)

                    def empty(name):
                        dve.wait_ge(s_pj, use.total * (j + 1) + use.index[name] + 1)
                        return PJ[use.index[name] % 2]

                    def keys_values(n):
                        o = empty(f"kv{n}")
                        dve.tensor_tensor(kv[:, 2 * n:2 * n + 2, :, :].rearrange("p t h d -> p t (h d)"),
                                          o[:, :].rearrange("p (t d) -> p t d", t=2),
                                          bkv[:, :, :].rearrange("p h d -> p (h d)").unsqueeze(1).to_broadcast([P, 2, 2 * GW]),
                                          ALU.add).then_inc(s_pjd, 1)

                    def spread(k):
                        g = rows[k]
                        dve.wait_ge(s_sq, 3 * j + k + 1)
                        step(dve.tensor_reduce(var[:, g], sq[:, 0:g.stop - g.start, :], AX.X, ALU.add))

                    def normalise(k, x):
                        g = rows[k]
                        dve.wait_ge(s_dev, 3 * j + k + 1)
                        step(dve.reciprocal(rdev[:, g], dev[:, g]))
                        return dve.tensor_tensor(x, x, rdev[:, g].unsqueeze(2).to_broadcast(list(x.shape)), ALU.mult)

                    def row(w, x):
                        return w.unsqueeze(1).to_broadcast(list(x.shape))

                    for b in range(B):
                        o = empty(f"d{b}")
                        dve.tensor_tensor(cq[:, NT + b, :], o[:, 0:GW], bd[:, 0, :], ALU.add)
                        dve.tensor_tensor(dv[:, b, :], o[:, GW:2 * GW], bd[:, 1, :], ALU.add).then_inc(s_pjd, 1)
                    for n in range(2):
                        o = empty(f"q{n}")
                        dve.tensor_tensor(cq[:, 4 * n:4 * n + 4, :], o[:, :].rearrange("p (t d) -> p t d", t=4),
                                          bq[:, :].unsqueeze(1).to_broadcast([P, 4, GW]), ALU.add).then_inc(s_pjd, 1)
                    q, d = cqrows[:, 0:RQ, :], cqrows[:, RQ:, :]
                    keys_values(0)
                    spread(0)
                    keys_values(1)
                    step(normalise(0, cqrows))
                    keys_values(2)
                    dve.tensor_tensor(q, q, row(qnorm[:, 0, :], q), ALU.mult)
                    step(dve.tensor_tensor(d, d, row(norms[:, 4, :], d), ALU.mult))
                    keys_values(3)
                    dve.tensor_tensor(q, q, row(qnorm[:, 1, :], q), ALU.add).then_inc(s_nrm, 1)
                    step(dve.tensor_tensor(d, d, row(norms[:, 5, :], d), ALU.add))
                    keys_values(4)
                    dve.tensor_scalar(dk[:, :, :], cq[:, NT:, :], part[:, 1:2], None, ALU.mult)
                    step(dve.tensor_scalar(dv[:, :, :], dv[:, :, :], part[:, 1:2], None, ALU.mult))
                    spread(1)
                    keys_values(5)
                    normalise(1, headrows(0)[0]).then_inc(s_nrm, 1)
                    keys_values(6)
                    dve.wait_ge(s_hi, 5 * j + 1)
                    dve.tensor_tensor(split[0][:, :, 1, :], q, split[0][:, :, 0, :].bitcast(F32), ALU.subtract).then_inc(s_lo, 1)
                    keys_values(7)
                    done(dve, j, f"kv{PAIRS - 1}")
                    for b in range(B):
                        vt = kv[:, (b + 1) * NK - 1, :, HD:]
                        ins = dve.scalar_tensor_tensor(vt, vt, part[:, 0:1], dv[:, b, :].rearrange("p (h d) -> p h d", d=HD),
                                                       ALU.mult, ALU.add)
                    step(ins)

                    def last_keys(b):
                        kt = kv[:, (b + 1) * NK - 1, :, 0:HD]
                        return dve.scalar_tensor_tensor(kt, kt, part[:, 0:1], dk[:, b, :].rearrange("p (h d) -> p h d", d=HD),
                                                        ALU.mult, ALU.add)

                    def low_keys(b):
                        part_k = split[(1 + b) % 2]
                        dve.wait_ge(s_hi, 5 * j + 2 * b + 2)
                        dve.tensor_tensor(part_k[:, :, 2, :], headrows(b)[0], part_k[:, :, 0, :].bitcast(F32),
                                          ALU.subtract).then_inc(s_lo, 1)

                    def low_values(b):
                        dve.wait_ge(s_hi, 5 * j + 2 * b + 3)
                        v_hi, v_lo, v = values_of(b)
                        dve.tensor_tensor(v_lo, v, v_hi.bitcast(F32), ALU.subtract).then_inc(s_lo, 1)

                    dve.wait_ge(s_aff, 2 * (j + 1))
                    step(last_keys(0))
                    spread(2)
                    low_keys(0)
                    k = headrows(1)[0]
                    step(normalise(2, k))
                    low_values(0)
                    step(dve.tensor_tensor(k, k, row(norms[:, 2, :], k), ALU.mult))
                    step(dve.tensor_tensor(k, k, row(norms[:, 3, :], k), ALU.add))
                    step(last_keys(1))
                    low_keys(1)
                    low_values(1)
                    assert steps == STEPS, steps

                    def reciprocal(n):
                        dve.wait_ge(s_ex, 2 * (NS * (j + 1) + n + 1))
                        dve.reciprocal(rtotal[:, n % RING, :], total[:, n % RING, :]).then_inc(s_rt, 1)

                    def low(n):
                        u, q = n // QT, n % QT
                        for i in range(2):
                            dve.wait_ge(s_th, 2 * (NS * j + n) + i + 1)
                            k = slice(i * NK // 2, (i + 1) * NK // 2)
                            cols = slice(q * P, (q + 1) * P)
                            dve.tensor_tensor(pT[1][:, k, cols], TR[i][:, :].rearrange("p (k n) -> p k n", n=P),
                                              pT[0][:, k, cols].bitcast(F32), ALU.subtract).then_inc(s_tl, 1)

                    def add_out(b, t):
                        o = empty(f"w{b}{t}")
                        xt = x3[:, b * QT + t, :]
                        dve.scalar_tensor_tensor(xt, o[:, :], tgate[:, 1:2], xt, ALU.mult, ALU.add).then_inc(s_pjd, 1)

                    for n in range(NS):
                        w = n % RING
                        dve.wait_ge(s_sc, NS * j + n + 1)
                        dve.tensor_reduce(most[:, w, 0:1], SC[n % 2][:, 0:MAIN], AX.X, ALU.max, negate=True)
                        dve.tensor_reduce(most[:, w, 1:2], SC[n % 2][:, MAIN:], AX.X, ALU.max, negate=True).then_inc(s_sm, 1)
                        if n >= 1:
                            reciprocal(n - 1)
                        if n >= LAG:
                            low(n - LAG)
                        if OUT <= n <= OUT + 1:
                            for t in (2 * (n - OUT), 2 * (n - OUT) + 1):
                                add_out(0, t)
                    reciprocal(NS - 1)
                    for n in range(NS - LAG, NS):
                        low(n)
                    centre(j + 1)
                    for t in range(QT):
                        add_out(1, t)

                centre(0)
                with dve.Fori(0, NG) as j:
                    body(j)
                dve.wait_ge(s_pjd, use.per["D"] * (NG + 1))
                for t in range(NT):
                    dve.tensor_tensor(x3[:, t, :], x3[:, t, :], tbo[:, :], ALU.add).then_inc(s_tbo, 1)

            def values_of(b):
                t = vS[:, b * NK:(b + 1) * NK, :, :].rearrange("p t i (k d) -> p (t i) k d", d=HD)
                v = kv[:, b * NK:(b + 1) * NK, :, HD:].rearrange("p t (i h) d -> p (t i) h d", h=2)
                return t[:, :, 0:5:4, :], t[:, :, 1:6:4, :], v

            def scalar(act):
                act.wait_ge(s_qn, 1)
                flat = vS[:, :, :, :].rearrange("p t i d -> p (t i d)")
                act.activation(flat, scrap[:, 63:64].to_broadcast(list(flat.shape)), ACT.Copy).then_inc(s_qn, 1)
                act.wait_ge(s_qn, 2)
                act.activation(scrap[:, 32:33], eps[:, 0:1], ACT.Copy).then_inc(s_pja, use.per["A"])
                act.activation(scrap[:, 34:35], eps[:, 0:1], ACT.Copy).then_inc(s_ex, 2 * NS)

                def body(j):
                    def filled(name):
                        act.wait_ge(s_pj, use.total * (j + 1) + use.index[name] + 1)
                        return PJ[use.index[name] % 2]

                    def square(k, x, name):
                        done(act, j, name)
                        act.activation(sq[:, 0:x.shape[1], :], x, ACT.Square).then_inc(s_sq, 1)

                    def root(k, steps):
                        act.wait_ge(s_ch, STEPS * j + steps)
                        act.activation(dev[:, rows[k]], var[:, rows[k]], ACT.Sqrt, scale=1.0 / HD, bias=eps[:, 1:2]).then_inc(s_dev, 1)

                    def stacked(b, h, i):
                        first = b * S2 + i * BANK
                        act.activation(kS[:, h, first:first + BANK], filled(f"tk{b}{h}{i}")[0:STACK, :].bitcast(F32R),
                                       ACT.Copy).then_inc(s_pja, 1)

                    def high_keys_values(b):
                        act.activation(split[(1 + b) % 2][:, :, 0:2, :], headrows(b)[0].unsqueeze(2).to_broadcast([P, RK, 2, HD]),
                                       ACT.Copy).then_inc(s_hi, 1)
                        v_hi, _, v = values_of(b)
                        act.activation(v_hi, v, ACT.Copy).then_inc(s_hi, 1)

                    square(0, cqrows, "q1")
                    root(0, 1)
                    square(1, headrows(0)[0], f"kv{PAIRS // 2 - 1}")
                    act.wait_ge(s_nrm, 2 * j + 1)
                    act.activation(split[0][:, :, 0:3:2, :], cqrows[:, 0:RQ, :].unsqueeze(2).to_broadcast([P, RQ, 2, HD]),
                                   ACT.Copy).then_inc(s_hi, 1)
                    root(1, 7)
                    square(2, headrows(1)[0], f"kv{PAIRS - 1}")
                    act.wait_ge(s_ch, STEPS * j + 10)
                    high_keys_values(0)
                    root(2, 11)
                    for h in range(HPG):
                        for i in range(2):
                            act.activation(qS[:, h, i * BANK:(i + 1) * BANK], filled(f"tq{h}{i}")[0:STACK, :].bitcast(F32R),
                                           ACT.Copy).then_inc(s_pja, 1)
                    for h in range(HPG):
                        for i in range(2):
                            stacked(0, h, i)
                    act.wait_ge(s_ch, STEPS * j + 16)
                    high_keys_values(1)

                    def high(n):
                        q = n % QT
                        for i in range(2):
                            act.wait_ge(s_tr, 2 * (NS * j + n) + i + 1)
                            act.activation(pT[0][:, i * NK // 2:(i + 1) * NK // 2, q * P:(q + 1) * P],
                                           TR[i][:, :].rearrange("p (k n) -> p k n", n=P), ACT.Copy).then_inc(s_th, 1)

                    def outputs(b, i):
                        act.activation(oT[b][:, i, :], filled(f"o{b}{i}")[:, :], ACT.Copy).then_inc(s_pja, 1)

                    for n in range(NS):
                        u, q = n // QT, n % QT
                        w = n % RING
                        if n >= LAG:
                            high(n - LAG)
                        act.wait_ge(s_sm, NS * j + n + 1)
                        for k, cols in enumerate((slice(0, MAIN), slice(MAIN, S2))):
                            act.activation(p[w][:, cols], SC[n % 2][:, cols], ACT.Exp,
                                           bias=most[:, w, k:k + 1], accum_out=total[:, w, k:k + 1]).then_inc(s_ex, 1)
                        if n < HPG:
                            for i in range(2):
                                stacked(1, n, i)
                        i = (n - LAG - 1) // (2 * QT) - 1
                        if i >= 0 and (n - LAG - 1) % (2 * QT) == 0:
                            outputs(i // PAIR, i % PAIR)
                    for n in range(NS - LAG, NS):
                        high(n)
                    outputs(B - 1, PAIR - 1)

                with act.Fori(0, NG) as j:
                    body(j)

            def gpsimd(pool):
                pool.wait_ge(s_c, 16 * 8)
                with pool.Fori(0, NG) as j:
                    k = headrows(0)[0]
                    pool.wait_ge(s_nrm, 2 * (j + 1))
                    pool.tensor_tensor(k, k, norms[:, 2, :].unsqueeze(1).to_broadcast(list(k.shape)), ALU.mult).then_inc(s_aff, 1)
                    pool.wait_ge(s_aff, 2 * j + 1)
                    pool.tensor_tensor(k, k, norms[:, 3, :].unsqueeze(1).to_broadcast(list(k.shape)), ALU.add).then_inc(s_aff, 1)
                    for n in range(NS):
                        w = n % RING
                        pool.wait_ge(s_rt, NS * j + n + 1)
                        pool.tensor_tensor(carry[:, w:w + 1], rtotal[:, w, 0:1], rtotal[:, w, 0:1], ALU.mult)
                        for k, cols in enumerate((slice(0, MAIN), slice(MAIN, S2))):
                            pool.tensor_scalar(p[w][:, cols], p[w][:, cols], rtotal[:, w, k:k + 1], 1.0,
                                               ALU.mult, ALU.mult).then_inc(s_pn, 1)

            def tensor(pe):
                pe.wait_ge(s_lnev, 2 * NT)
                pe.wait_ge(s_ctxev, 2 * PAIRS)
                pe.transpose(PJ[0][:, 0:P], ident[:, :], ident[:, :]).then_inc(s_pj, use.total)
                pe.wait_ge(s_idr, 1)

                def body(j):
                    def bank(name):
                        n = use.index[name]
                        e, count = use.emptied(n - 2, j) if n >= 2 else use.emptied(use.total + n - 2, j - 1)
                        pe.wait_ge(emptied[e], count)
                        return PJ[n % 2]

                    pe.wait_ge(s_cw, NCW * (j + 1))
                    for b in range(B):
                        o = bank(f"d{b}")
                        for c in range(VC):
                            mm = pe.matmul(o[:, 0:2 * GW], cxT3[:, c, (b + 1) * S2 - P:(b + 1) * S2],
                                           wd[:, c, :, :].rearrange("p k d -> p (k d)"), start=(c == 0), stop=(c == VC - 1))
                        mm.then_inc(s_pj, 1)
                    for n in range(2):
                        o = bank(f"q{n}")
                        for i in range(4):
                            for c in range(KC):
                                mm = pe.matmul(o[:, i * GW:(i + 1) * GW], xT3[:, c, (4 * n + i) * P:(4 * n + i + 1) * P], wq[:, c, :],
                                               start=(c == 0), stop=(c == KC - 1))
                        mm.then_inc(s_pj, 1)
                    for n in range(PAIRS):
                        o = bank(f"kv{n}")
                        for i in range(2):
                            for c in range(VC):
                                mm = pe.matmul(o[:, i * 2 * GW:(i + 1) * 2 * GW], cxT3[:, c, (2 * n + i) * P:(2 * n + i + 1) * P],
                                               wkv[:, c, :, :].rearrange("p h d -> p (h d)"), start=(c == 0), stop=(c == VC - 1))
                        mm.then_inc(s_pj, 1)

                    def stack(name, parts, row0):
                        o = bank(name)
                        for i in range(4):
                            mm = pe.transpose(o[0:STACK, i * P:(i + 1) * P].bitcast(F32R),
                                              parts[:, row0 + i * HPG, :, :].rearrange("p k d -> p (k d)"), identr[:, :])
                        mm.then_inc(s_pj, 1)

                    pe.wait_ge(s_lo, 5 * j + 1)
                    for h in range(HPG):
                        for i in range(2):
                            stack(f"tq{h}{i}", split[0], i * 4 * HPG + h)
                    pe.wait_ge(s_lo, 5 * j + 2)
                    for h in range(HPG):
                        for i in range(2):
                            stack(f"tk0{h}{i}", split[1], i * 4 * HPG + h)
                    done(pe, j, f"tk0{HPG - 1}1")
                    pe.wait_ge(s_wo, 16 * 8 * (j + 1))

                    def transposes(n):
                        pe.wait_ge(s_pn, 2 * (NS * j + n + 1))
                        for i in range(2):
                            pe.wait_ge(s_tl, 2 * (NS * (j + 1) + n - 1) + i + 1)
                            for k in range(NK // 2):
                                kk = i * NK // 2 + k
                                mm = pe.transpose(TR[i][:, k * P:(k + 1) * P], p[n % RING][:, kk * P:(kk + 1) * P], ident[:, :])
                            mm.then_inc(s_tr, 1)

                    def values(m):
                        u, half = m // 2, m % 2
                        b, h = u // HPG, u % HPG
                        cols = slice(half * HALF, (half + 1) * HALF)
                        name = f"o{b}{h // 2}"
                        o = bank(name) if h % 2 == 0 and half == 0 else PJ[use.index[name] % 2]
                        if half == 0 and u % HPG == 0:
                            pe.wait_ge(s_lo, 5 * j + 2 * b + 3)
                        pe.wait_ge(s_tl, 2 * (NS * (j + 1) + 2 * (m + 1)))
                        for k in range(NK):
                            v = vS[:, b * NK + k, h // 2, (h % 2) * 2 * HD:(h % 2) * 2 * HD + P]
                            for i in range(2):
                                mm = pe.matmul(o[:, cols], v, pT[i][:, k, cols], start=(h % 2 == 0 and half == 0 and k == 0 and i == 0),
                                               stop=(h % 2 == 1 and half == 1 and k == NK - 1 and i == 1))
                        if h % 2 and half:
                            mm.then_inc(s_pj, 1)

                    def project(b, t):
                        o = bank(f"w{b}{t}")
                        if t == 0:
                            done(pe, j, f"o{b}{PAIR - 1}")
                        for i in range(PAIR):
                            mm = pe.matmul(o[:, :], oT[b][:, i, t * P:(t + 1) * P], wo[:, i, :], start=(i == 0), stop=(i == PAIR - 1))
                        mm.then_inc(s_pj, 1)

                    for n in range(NS):
                        u, q = n // QT, n % QT
                        b, h = u // HPG, u % HPG
                        if n == HPG * QT:
                            done(pe, j, f"tk1{HPG - 1}1")
                        pe.wait_ge(s_ex, 2 * (NS * (j + 1) + n - 1))
                        for i in range(2):
                            mm = pe.matmul(SC[n % 2][:, i * BANK:(i + 1) * BANK], qS[:, h, b * S + q * P:b * S + (q + 1) * P],
                                           kS[:, h, b * S2 + i * BANK:b * S2 + (i + 1) * BANK], start=True, stop=True)
                        mm.then_inc(s_sc, 1)
                        if n == 0:
                            pe.wait_ge(s_lo, 5 * j + 4)
                        if n < HPG:
                            for i in range(2):
                                stack(f"tk1{n}{i}", split[0], i * 4 * HPG + n)
                        if n >= LAG:
                            transposes(n - LAG)
                        if OUT <= n <= OUT + 1:
                            for t in (2 * (n - OUT), 2 * (n - OUT) + 1):
                                project(0, t)
                        m = (n - LAG - 2) // 2
                        if n == OUT + 1:
                            values(m)
                        elif m >= 0 and (n - LAG) % 2 == 0 and n != OUT:
                            values(m)
                    for n in range(NS - LAG, NS):
                        transposes(n)
                        if n % 2 and n < NS - 1:
                            values(n // 2)
                    values(NS // 2 - 1)
                    for t in range(QT):
                        project(B - 1, t)

                with pe.Fori(0, NG) as j:
                    body(j)

            programs["SP"].append(sync)
            programs["DVE"].append(vector)
            programs["ACT"].append(scalar)
            programs["POOL"].append(gpsimd)
            programs["PE"].append(tensor)
            return s_tbo, NT + 1

        x2_done = cross_attention_1()
        phase.close()
        phase = ExitStack()

        statistics(3, x2_done)

        def bit_ffn():
            HID = 2048
            HC = HID // P
            HB = HID // BANK
            LEAST = 1e-5
            MAGIC = 1.5 * 2.0 ** 23
            TOP, BOTTOM = 127.0, -128.0
            GROUPS = 8
            raw = [sb("f_raw1", [P, HC, D]), sb("f_raw2", [P, KC, HID])]
            wq = [sb("f_wq1", [P, HC, D], BF16), sb("f_wq2", [P, KC, HID], BF16)]
            w1T, w2T = sb("f_w1T", [P, KC, HID], BF16), sb("f_w2T", [P, HC, D], BF16)
            identb, ones = sb("f_identb", [P, P], BF16), sb("f_ones", [P, P])
            size, wmean, winv = sb("f_size", [P, 2]), sb("f_wmean", [P, 2]), sb("f_winv", [P, 2])
            b1, b2 = sb("f_b1", [P, HID]), sb("f_b2", [P, D])
            h = [sb(f"f_h{s}", [P, D]) for s in range(2)]
            hq = [sb(f"f_hq{s}", [P, D], BF16) for s in range(2)]
            hqT = [sb(f"f_hqT{s}", [P, KC, P], BF16) for s in range(2)]
            z = [sb(f"f_z{s}", [P, HID]) for s in range(2)]
            zq = [sb(f"f_zq{s}", [P, HID], BF16) for s in range(2)]
            zqT = [sb(f"f_zqT{s}", [P, HC, P], BF16) for s in range(2)]
            o = [sb(f"f_o{s}", [P, D]) for s in range(2)]
            most = sb("f_most", [P, 4])
            scale = sb("f_scale", [P, 4])
            unscale = sb("f_unscale", [P, 4])
            HID_B, OUT_B = [banks[k] for k in range(HB)], banks[4:6]
            TRB = [pairs[3][:, i * BANK:(i + 1) * BANK].bitcast(BF16) for i in range(2)]
            WTB = [pairs[2 + i // 2][:, (i % 2) * BANK:(i % 2 + 1) * BANK].bitcast(BF16) for i in range(4)]

            s_w = [sem("f_w1"), sem("f_w2")]
            s_b, s_id, s_one = [sem(f"f_{n}") for n in ("b", "id", "one")]
            s_size, s_sum, s_mean, s_wc, s_wr, s_wq, s_wt, s_wa, s_wd = [
                sem(f"f_{n}") for n in ("size", "sum", "mean", "wc", "wr", "wq", "wt", "wa", "wd")]
            s_ch, s_r, s_q, s_tr, s_te, s_m1, s_z, s_g, s_m2, s_o, s_x2 = [
                sem(f"f_{n}") for n in ("ch", "r", "q", "tr", "te", "m1", "z", "g", "m2", "o", "x2")]
            CH = 4
            STEPS = 26
            TURNS = 6

            def chunk(t3, k):
                n = t3.shape[1] // CH
                return t3[:, k * n:(k + 1) * n, :]

            def sync(sp):
                sp.wait_ge(*x2_done)
                sp.dma_start(raw[0][:, :, :], a["L1_ffn_w1"].rearrange("(t p) d -> p t d", p=P)).then_inc(s_w[0], 16)
                sp.dma_start(raw[1][:, :, :], a["L1_ffn_w2"].rearrange("(t p) d -> p t d", p=P)).then_inc(s_w[1], 16)
                sp.dma_start(b1[:, :], a["L1_ffn_b1"].partition_broadcast(P)).then_inc(s_b, 16)
                sp.dma_start(b2[:, :], a["L1_ffn_b2"].partition_broadcast(P)).then_inc(s_b, 16)
                out3 = out.rearrange("b (t p) d -> p (b t) d", p=P)
                with sp.Fori(0, NT // 2) as i:
                    sp.wait_ge(s_x2, 2 * (i + 1))
                    sp.dma_start(out3[:, bass.ds(i * 2, 2), :], x3[:, bass.ds(i * 2, 2), :]).then_inc(s_out, 16)
                sp.wait_ge(s_out, 16 * (NT // 2))

            def vector(dve):
                dve.wait_ge(*x2_done)
                dve.memset(ones[:, :], 1.0).then_inc(s_one, 1)
                dve.memset(scrap[:, 36:37], 0.0).then_inc(s_z, HB)
                dve.memset(scrap[:, 37:38], 0.0).then_inc(s_o, 2)
                dve.wait_ge(s_sum, 1)
                dve.tensor_scalar(wmean[:, :], HID_B[0][:, 0:2], 1.0 / (HID * D), LEAST, ALU.mult, ALU.max).then_inc(s_mean, 1)
                dve.wait_ge(s_mean, 1)
                dve.reciprocal(winv[:, :], wmean[:, :]).then_inc(s_mean, 1)
                dve.wait_ge(s_mean, 2)
                for w in range(2):
                    for k in range(CH):
                        c = chunk(raw[w], k)
                        dve.tensor_scalar(c, c, winv[:, w:w + 1], 1.0, ALU.mult, ALU.min).then_inc(s_wc, 1)
                        dve.wait_ge(s_wc, w * CH + k + 1)
                        dve.tensor_scalar(c, c, -1.0, MAGIC, ALU.max, ALU.add).then_inc(s_wr, 1)
                for g in range(1, 2 * GROUPS, 2):
                    dve.wait_ge(s_wt, g + 1)
                    turned(dve, g)
                dve.wait_ge(s_rstd, 4)
                dve.wait_ge(s_b, 32)

                def body(i):
                    steps = 0

                    def step(ins):
                        nonlocal steps
                        steps += 1
                        ins.then_inc(s_ch, 1)
                        dve.wait_ge(s_ch, STEPS * i + steps)

                    def quantise(src, n, w):
                        m, q = most[:, n:n + 1], scale[:, n:n + 1]
                        step(dve.tensor_scalar(m, m, LEAST, None, ALU.max))
                        step(dve.reciprocal(q, m))
                        step(dve.tensor_scalar(q, q, TOP, None, ALU.mult))
                        step(dve.tensor_scalar(unscale[:, n:n + 1], m, 1.0 / TOP, wmean[:, w:w + 1], ALU.mult, ALU.mult))
                        step(dve.tensor_scalar(src, src, q, MAGIC, ALU.mult, ALU.add))
                        dve.tensor_scalar(src, src, MAGIC + TOP, MAGIC + BOTTOM, ALU.min, ALU.max).then_inc(s_r, 1)

                    for s in range(2):
                        t = i * 2 + s
                        step(dve.tensor_scalar(h[s][:, :], x3[:, bass.ds(t, 1), :].rearrange("p t d -> p (t d)"),
                                               mv[:, bass.ds(t * 2, 1)], rstd[:, bass.ds(t, 1)], ALU.subtract, ALU.mult))
                        step(dve.tensor_reduce(most[:, s:s + 1], h[s][:, :], AX.X, ALU.max, apply_absolute_value=True))
                        quantise(h[s][:, :], s, 0)
                    for s in range(2):
                        for k in range(HB):
                            dve.wait_ge(s_m1, 2 * HB * i + HB * s + k + 1)
                            cols = slice(k * BANK, (k + 1) * BANK)
                            dve.scalar_tensor_tensor(z[s][:, cols], HID_B[k][:, :], unscale[:, s:s + 1], b1[:, cols],
                                                     ALU.mult, ALU.add).then_inc(s_z, 1)
                    for s in range(2):
                        dve.wait_ge(s_g, 2 * i + s + 1)
                        step(dve.tensor_reduce(most[:, 2 + s:3 + s], z[s][:, :], AX.X, ALU.max, apply_absolute_value=True))
                        quantise(z[s][:, :], 2 + s, 1)
                    for s in range(2):
                        dve.wait_ge(s_m2, 2 * i + s + 1)
                        dve.scalar_tensor_tensor(o[s][:, :], OUT_B[s][:, :], unscale[:, 2 + s:3 + s], b2[:, :],
                                                 ALU.mult, ALU.add).then_inc(s_o, 1)
                        dve.wait_ge(s_o, 2 * i + s + 3)
                        xt = x3[:, bass.ds(i * 2 + s, 1), :].rearrange("p t d -> p (t d)")
                        dve.scalar_tensor_tensor(xt, o[s][:, :], tgate[:, 3:4], xt, ALU.mult, ALU.add).then_inc(s_x2, 1)
                    assert steps == STEPS

                with dve.Fori(0, NT // 2) as i:
                    body(i)

            def turned(engine, g):
                src = WTB[g % 4][:, :]
                if g < GROUPS:
                    dst = w1T[:, g // 2, (g % 2) * 8 * P:(g % 2 + 1) * 8 * P]
                else:
                    m = (g - GROUPS) * 2
                    dst, src = w2T[:, m:m + 2, :], src.rearrange("p (m d) -> p m d", m=2)
                if g % 2:
                    engine.tensor_copy(dst, src).then_inc(s_wd, 1)
                else:
                    engine.activation(dst, src, ACT.Copy).then_inc(s_wa, 1)

            def scalar(act):
                act.wait_ge(*x2_done)
                act.activation(identb[:, :], ident[:, :], ACT.Copy).then_inc(s_id, 1)
                act.activation(scrap[:, 40:41], eps[:, 0:1], ACT.Copy).then_inc(s_te, 2)
                for w in range(2):
                    act.wait_ge(s_w[w], 16)
                    act.activation(wq[w][:, :, :], raw[w][:, :, :], ACT.Abs, accum_out=size[:, w:w + 1]).then_inc(s_size, 1)
                act.wait_ge(s_size, 2)
                for w in range(2):
                    for k in range(CH):
                        act.wait_ge(s_wr, w * CH + k + 1)
                        act.activation(chunk(wq[w], k), chunk(raw[w], k), ACT.Copy, bias=-MAGIC).then_inc(s_wq, 1)
                for g in range(0, 2 * GROUPS, 2):
                    act.wait_ge(s_wt, g + 1)
                    turned(act, g)

                def body(i):
                    def whole(dst, src, n):
                        act.wait_ge(s_r, 4 * i + n + 1)
                        act.activation(dst[:, :], src[:, :], ACT.Copy, bias=-MAGIC).then_inc(s_q, 1)

                    def copy(dst, n, m):
                        act.wait_ge(s_tr, TURNS * i + n + 1)
                        act.activation(dst, TRB[n % 2][:, 0:m * P].rearrange("p (m n) -> p m n", m=m), ACT.Copy).then_inc(s_te, 1)

                    for s in range(2):
                        whole(hq[s], h[s], s)
                    for s in range(2):
                        copy(hqT[s][:, :, :], s, KC)
                    for s in range(2):
                        act.wait_ge(s_z, HB * (2 * i + s + 2))
                        act.activation(z[s][:, :], z[s][:, :], ACT.Gelu).then_inc(s_g, 1)
                    for s in range(2):
                        whole(zq[s], z[s], 2 + s)
                        for k in range(2):
                            copy(zqT[s][:, k * 8:(k + 1) * 8, :], 2 + 2 * s + k, 8)

                with act.Fori(0, NT // 2) as i:
                    body(i)

            def tensor(pe):
                pe.wait_ge(s_one, 1)
                pe.wait_ge(s_size, 2)
                pe.matmul(HID_B[0][:, 0:2], ones[:, :], size[:, :], start=True, stop=True).then_inc(s_sum, 1)
                pe.wait_ge(s_id, 1)
                for g in range(2 * GROUPS):
                    if g < GROUPS:
                        pe.wait_ge(s_wq, CH)
                    else:
                        pe.wait_ge(s_wq, 2 * CH)
                    if g >= 4:
                        pe.wait_ge((s_wa, s_wd)[g % 2], (g - 4) // 2 + 1)
                    for k in range(8):
                        if g < GROUPS:
                            src = wq[0][:, (g % 2) * 8 + k, (g // 2) * P:(g // 2 + 1) * P]
                        else:
                            m = (g - GROUPS) * 2 + k // 4
                            src = wq[1][:, k % 4, m * P:(m + 1) * P]
                        mm = pe.transpose(WTB[g % 4][:, k * P:(k + 1) * P], src, identb[:, :])
                    mm.then_inc(s_wt, 1)
                pe.wait_ge(s_wa, GROUPS)
                pe.wait_ge(s_wd, GROUPS)

                def body(i):
                    def turn(src, n, m):
                        pe.wait_ge(s_te, TURNS * i + n + 1)
                        for k in range(m):
                            mm = pe.transpose(TRB[n % 2][:, k * P:(k + 1) * P], src[:, k * P:(k + 1) * P], identb[:, :])
                        mm.then_inc(s_tr, 1)

                    for s in range(2):
                        pe.wait_ge(s_q, 4 * i + s + 1)
                        turn(hq[s][:, :], s, KC)
                    for s in range(2):
                        pe.wait_ge(s_te, TURNS * i + s + 3)
                        for k in range(HB):
                            pe.wait_ge(s_z, HB * (2 * i + s) + k + 1)
                            for c in range(KC):
                                mm = pe.matmul(HID_B[k][:, :], hqT[s][:, c, :], w1T[:, c, k * BANK:(k + 1) * BANK],
                                               start=(c == 0), stop=(c == KC - 1))
                            mm.then_inc(s_m1, 1)
                    for s in range(2):
                        pe.wait_ge(s_q, 4 * i + 2 + s + 1)
                        for k in range(2):
                            turn(zq[s][:, k * 8 * P:(k + 1) * 8 * P], 2 + 2 * s + k, 8)
                        pe.wait_ge(s_te, TURNS * i + 2 * s + 6)
                        pe.wait_ge(s_o, 2 * i + s + 1)
                        for m in range(HC):
                            mm = pe.matmul(OUT_B[s][:, :], zqT[s][:, m, :], w2T[:, m, :], start=(m == 0), stop=(m == HC - 1))
                        mm.then_inc(s_m2, 1)

                with pe.Fori(0, NT // 2) as i:
                    body(i)

            programs["SP"].append(sync)
            programs["DVE"].append(vector)
            programs["ACT"].append(scalar)
            programs["PE"].append(tensor)

        bit_ffn()
        phase.close()

        block = ctx.enter_context(nc.Block())

        @block.sync
        def _(sp):
            for stage in programs["SP"]:
                stage(sp)

        @block.scalar
        def _(act):
            for stage in programs["ACT"]:
                stage(act)

        @block.tensor
        def _(pe):
            for stage in programs["PE"]:
                stage(pe)

        @block.vector
        def _(dve):
            for stage in programs["DVE"]:
                stage(dve)

        @block.gpsimd
        def _(pool):
            for stage in programs["POOL"]:
                stage(pool)


def constants():
    half = 32
    inv = (np.float32(1.0) / np.float32(150000.0) ** (np.arange(half, dtype=np.float32) / np.float32(half))).astype(np.float32)
    angle = (np.arange(S, dtype=np.float32)[:, None] * inv).astype(np.float32).T
    rows = np.arange(P)
    swap = np.zeros((P, P), np.float32)
    for m in range(P):
        if m % (2 * half) < half:
            swap[m + half, m] = -1.0
        else:
            swap[m - half, m] = 1.0
    causal = np.zeros((P, S), np.float32)
    causal[:, S - P:] = np.where(rows[None, :] <= rows[:, None], 0.0, -BIG)
    part = np.stack([np.arange(P) < P - 16, np.arange(P) >= P - 16], axis=1).astype(np.float32)
    ne, cap = 16, T * 4 // 16 * 3 // 2
    token = np.stack(np.broadcast_arrays(rows[:, None], P * np.arange(NT)[None, :]), axis=2).astype(np.float32)
    return {"c_before": np.triu(np.ones((P, P), np.float32), 1), "c_ones": np.ones((P, P), np.float32),
            "c_first": (np.arange(ne) * cap - 1).astype(np.float32), "c_count_up": np.arange(1, cap + 1).astype(np.float32),
            "c_token": token, "c_part": part, "c_ident": np.eye(P, dtype=np.float32), "c_causal": causal, "c_swap": swap,
            "c_cos": np.tile(np.cos(angle), (4, 1)).astype(np.float32),
            "c_sin": np.tile(np.sin(angle), (4, 1)).astype(np.float32)}


def kernel(**inputs):
    import concourse.bacc as _bacc
    from concourse.bass_utils import run_bass_kernel_spmd as _run

    nc = _bacc.Bacc("TRN2", target_bir_lowering=False, num_devices=1)
    arrays, args = {}, {}
    wkv = np.concatenate([inputs["L1_xattn_Wk"], inputs["L1_xattn_Wv"]], axis=1)
    bkv = np.concatenate([inputs["L1_xattn_bk"], inputs["L1_xattn_bv"]])
    for name, value in {**inputs, **constants(), "wkv": wkv, "bkv": bkv}.items():
        value = np.ascontiguousarray(value)
        if value.dtype == np.bool_:
            value = value.view(np.uint8)
        arrays[f"in_{name}"] = value
        args[name] = nc.dram_tensor(f"in_{name}", value.shape, mybir.dt.from_np(value.dtype), kind="ExternalInput").ap()
    out = nc.dram_tensor("out_x", (B, S, D), F32, kind="ExternalOutput").ap()
    program(nc, args, out)
    r = _run(nc, [arrays], core_ids=[0])
    return r.results[0]["out_x"]
```

```python
from contextlib import ExitStack

import numpy as np

import concourse.bass as bass
from concourse import mybir

P = 128
BANK = 512
F32 = mybir.dt.float32
F32R = mybir.dt.float32r
BF16 = mybir.dt.bfloat16
U8 = mybir.dt.uint8
I32 = mybir.dt.int32
ALU = mybir.AluOpType
ACT = mybir.ActivationFunctionType
AX = mybir.AxisListType

B, S, D = 2, 512, 512
S2, DV = 1024, 256
T = B * S
NT = T // P
QT = S // P
KC = D // P
VC = DV // P
NC_T = B * S2 // P
BIG = 1.0e30


class Use:

    def __init__(self, plan):
        self.plan = plan
        self.total = len(plan)
        self.per = {e: sum(x == e for _, x in plan) for e in "AD"}
        self.index, self.nth, seen = {}, [], {"A": 0, "D": 0}
        for n, (name, e) in enumerate(plan):
            seen[e] += 1
            self.nth.append((e, seen[e]))
            self.index[name] = n

    def emptied(self, n, it):
        e, c = self.nth[n % self.total]
        return e, self.per[e] * (it + 1 + n // self.total) + c


def program(nc, a, out):
    ctx = ExitStack()
    with ctx:
        def sem(name):
            return ctx.enter_context(nc.semaphore(name))

        def keep(name, shape, dt=F32):
            return ctx.enter_context(nc.sbuf_tensor(name, shape, dt))

        pairs = [ctx.enter_context(nc.psum_tensor(f"pair{i}", [P, 2 * BANK], F32)) for i in range(4)]
        banks = [pairs[i // 2][:, (i % 2) * BANK:(i % 2 + 1) * BANK] for i in range(8)]

        x = keep("x", [P, NT * D])
        hslot = keep("hslot", [P, 2 * D])
        ident = keep("ident", [P, P])
        identr = keep("identr", [P, P], F32R)
        gates = keep("gates", [P, 4])
        tgate = keep("tgate", [P, 4])
        stats = keep("stats", [P, NT * 6])
        mv = keep("mv", [P, NT * 2])
        std = keep("std", [P, NT])
        rstd = keep("rstd", [P, NT])
        eps = keep("eps", [P, 2])
        scrap = keep("scrap", [P, 64])
        x3 = x[:, :].rearrange("p (t d) -> p t d", t=NT)

        s_const, s_x, s_gate, s_eps, s_out = sem("s_const"), sem("s_x"), sem("s_gate"), sem("s_eps"), sem("s_out")
        s_tgate, s_idr = sem("s_tgate"), sem("s_idr")

        programs = {"SP": [], "ACT": [], "PE": [], "DVE": [], "POOL": []}

        s_stat, s_mv, s_std, s_rstd = [sem(f"ln_{n}") for n in ("stat", "mv", "std", "rstd")]

        def statistics(n, before):
            def vector(dve):
                dve.wait_ge(*before)
                for t in range(NT):
                    dve.bn_stats(stats[:, 6 * t:6 * t + 6], x3[:, t, :]).then_inc(s_stat, 1)
                for t in range(NT):
                    dve.wait_ge(s_stat, n * NT + t + 1)
                    dve.bn_aggr(mv[:, 2 * t:2 * t + 2], stats[:, 6 * t:6 * t + 6]).then_inc(s_mv, 1)
                dve.wait_ge(s_std, n + 1)
                dve.reciprocal(rstd[:, :], std[:, :]).then_inc(s_rstd, 1)

            def scalar(act):
                act.wait_ge(s_eps, 1)
                act.wait_ge(s_mv, (n + 1) * NT)
                act.activation(std[:, :], mv[:, :].rearrange("p (t k) -> p t k", k=2)[:, :, 1], ACT.Sqrt,
                               bias=eps[:, 0:1]).then_inc(s_std, 1)

            programs["DVE"].append(vector)
            programs["ACT"].append(scalar)

        s_lnh, s_lntr, s_lnev = [sem(f"ln_{n}") for n in ("h", "tr", "ev")]

        def layernorm(n, k, before, hT3):
            statistics(n, before)

            def vector(dve):
                dve.wait_ge(s_rstd, n + 1)
                for t in range(NT):
                    if t >= 2:
                        dve.wait_ge(s_lntr, k * NT + t - 1)
                    dve.tensor_scalar(hslot[:, (t % 2) * D:(t % 2 + 1) * D], x3[:, t, :], mv[:, 2 * t:2 * t + 1],
                                      rstd[:, t:t + 1], ALU.subtract, ALU.mult).then_inc(s_lnh, 1)

            def scalar(act):
                for t in range(NT):
                    act.wait_ge(s_lntr, k * NT + t + 1)
                    act.activation(hT3[:, :, t * P:(t + 1) * P],
                                   banks[t % 2][:, :].rearrange("p (c n) -> p c n", c=KC), ACT.Copy).then_inc(s_lnev, 1)

            def tensor(pe):
                pe.wait_ge(s_const, 16)
                for t in range(NT):
                    pe.wait_ge(s_lnh, k * NT + t + 1)
                    if t >= 2:
                        pe.wait_ge(s_lnev, k * NT + t - 1)
                    for c in range(KC):
                        mm = pe.transpose(banks[t % 2][:, c * P:(c + 1) * P],
                                          hslot[:, (t % 2) * D + c * P:(t % 2) * D + (c + 1) * P], ident[:, :])
                    mm.then_inc(s_lntr, 1)

            programs["DVE"].append(vector)
            programs["ACT"].append(scalar)
            programs["PE"].append(tensor)

        s_ones = sem("s_ones")

        def load_sync(sp):
            sp.dma_start(x3, a["x"].rearrange("b (t p) d -> p (b t) d", p=P)).then_inc(s_x, 16)
            sp.dma_start(ident[:, :], a["c_ident"]).then_inc(s_const, 16)
            sp.dma_start(gates[:, 0:2], a["g_xattn"].partition_broadcast(P)).then_inc(s_gate, 16)
            sp.dma_start(gates[:, 2:4], a["g_ffn"].partition_broadcast(P)).then_inc(s_gate, 16)

        def load_vector(dve):
            dve.memset(eps[:, 0:1], 1e-5).then_inc(s_ones, 1)
            dve.memset(eps[:, 1:2], 1e-6).then_inc(s_eps, 1)
            dve.memset(scrap[:, :], 0.0).then_inc(s_ones, 1)

        def load_scalar(act):
            act.wait_ge(s_gate, 32)
            act.wait_ge(s_ones, 2)
            act.activation(tgate[:, :], gates[:, :], ACT.Tanh).then_inc(s_tgate, 1)
            act.wait_ge(s_const, 16)
            act.activation(identr[:, :], ident[:, :], ACT.Copy).then_inc(s_idr, 1)

        programs["SP"].append(load_sync)
        programs["DVE"].append(load_vector)
        programs["ACT"].append(load_scalar)

        phase = ExitStack()

        def sb(name, shape, dt=F32):
            return phase.enter_context(nc.sbuf_tensor(name, shape, dt))

        hT3 = sb("hT_x0", [P, KC * T])[:, :].rearrange("p (c t) -> p c t", c=KC)
        ctxT = sb("ctxT", [P, VC * B * S2])
        ctxT3 = ctxT[:, :].rearrange("p (c t) -> p c t", c=VC)
        cslot = sb("cslot", [P, 4 * DV])

        PAIRS = NC_T // 2
        s_ctx = [sem(f"ctx_in{i}") for i in range(2)]
        s_ctxtr, s_ctxev = sem("ctx_tr"), sem("ctx_ev")

        def transpose_context(n, ctxT3, cslot, before=None):
            src = a["ctx_1024"].rearrange("b (t p) d -> p (b t) d", p=P)

            def sync(sp):
                if before:
                    sp.wait_ge(*before)
                for t in range(PAIRS):
                    if t >= 2:
                        sp.wait_ge(s_ctxtr, n * PAIRS + t - 1)
                    sp.dma_start(cslot[:, (t % 2) * 2 * DV:(t % 2 + 1) * 2 * DV].rearrange("p (t d) -> p t d", t=2),
                                 src[:, 2 * t:2 * t + 2, :]).then_inc(s_ctx[t % 2], 16)

            def tensor(pe):
                pe.wait_ge(s_const, 16)
                for t in range(PAIRS):
                    pe.wait_ge(s_ctx[t % 2], 16 * (n * PAIRS // 2 + t // 2 + 1))
                    if t >= 2:
                        pe.wait_ge(s_ctxev, n * PAIRS + t - 1)
                    for c in range(VC):
                        for j in range(2):
                            mm = pe.transpose(banks[4 + t % 2][:, (c * 2 + j) * P:(c * 2 + j + 1) * P],
                                              cslot[:, ((t % 2) * 2 + j) * DV + c * P:((t % 2) * 2 + j) * DV + (c + 1) * P],
                                              ident[:, :])
                    mm.then_inc(s_ctxtr, 1)

            def scalar(act):
                for t in range(PAIRS):
                    act.wait_ge(s_ctxtr, n * PAIRS + t + 1)
                    act.activation(ctxT3[:, :, t * 2 * P:(t + 1) * 2 * P],
                                   banks[4 + t % 2][:, :].rearrange("p (c n) -> p c n", c=VC), ACT.Copy).then_inc(s_ctxev, 1)

            programs["SP"].append(sync)
            programs["PE"].append(tensor)
            programs["ACT"].append(scalar)

        transpose_context(0, ctxT3, cslot)
        layernorm(0, 0, (s_x, 16), hT3)

        ACCURATE = ((0, 0), (1, 0), (0, 1))

        def cross_attention_0():
            NKV, HPG, HD = 8, 2, 128
            TURNS = B * NKV
            NK = S2 // P
            GW = HPG * HD
            SCALE = 1.0 / float(np.sqrt(HD))
            NS = HPG * QT
            LAG = QT
            HALF = S // 2
            VALUES = LAG + 2
            READY = [VALUES + 2 * (2 * u + 1) - NS for u in range(HPG)]
            FRONT = ("k0", "q0", "k1", "q1", "v0", "v1")
            PROJECT = {n: name for n, name in enumerate(FRONT)}
            SPLIT = 6
            OUT_BEFORE, OUT_BEHIND = {6: 1, 7: 2}, {5: 0, 7: 3}
            NF = len(FRONT)
            NO = HPG + QT
            HI = len(FRONT) - 1
            assert READY[0] >= 0 and READY[-1] < min(OUT_BEHIND) and READY[-1] < SPLIT
            wk, wv = sb("x_wk", [P, VC, HD]), sb("x_wv", [P, VC, HD])
            wq = sb("x_wq", [P, KC, GW])
            wo = sb("x_wo", [P, HPG, D])
            kT = [[sb(f"x_kT{i}{b}", [P, S2], F32R) for b in range(B)] for i in range(2)]
            vraw = cslot[:, :].rearrange("p (k n) -> p k n", n=HD)
            v = [[sb(f"x_v{i}{b}", [P, NK, HD], F32R) for b in range(B)] for i in range(2)]
            qT = [[[sb(f"x_qT{i}{b}{u}", [P, S], F32R) for u in range(HPG)] for b in range(B)] for i in range(2)]
            with ExitStack() as front:
                mask8 = front.enter_context(nc.sbuf_tensor("x_mask8", [P, B * S2], U8))
                mrow8 = front.enter_context(nc.sbuf_tensor("x_mrow8", [B * NK, P], U8))
                mrow = front.enter_context(nc.sbuf_tensor("x_mrow", [B * NK, P], F32))
            p = [sb(f"x_p{i}", [P, S2]) for i in range(NS)]
            pT = [sb(f"x_pT{i}", [P, NK, S], F32R) for i in range(2)]
            oT = [sb(f"x_oT{u}", [P, S]) for u in range(HPG)]
            least = sb("x_least", [P, NS])
            total = sb("x_total", [P, NS])
            rtotal = sb("x_rtotal", [P, NS])
            carry = sb("x_carry", [P, NS])
            mcol = sb("x_mcol", [P, B * NK])
            lower = sb("x_lower", [P, B * S2])

            PJ, OB, SC, TR = banks[0], banks[1], pairs[1:3], banks[6:8]

            s_mask, s_mtr, s_low = [sem(f"x_{n}") for n in ("mask", "mtr", "low")]
            s_w, s_wo = [sem(f"x_{n}") for n in ("w", "wo")]
            s_pj, s_pjd, s_hi, s_of, s_oa, s_wd, s_sc, s_sm, s_ex, s_rt, s_pn, s_tr, s_ta, s_td = [
                sem(f"x_{n}") for n in ("pj", "pjd", "hi", "of", "oa", "wd", "sc", "sm", "ex", "rt", "pn", "tr", "ta", "td")]
            LOADS = 3
            POOL = 1 + NS

            def until(engine, s, count):
                if not isinstance(count, int) or count > 0:
                    engine.wait_ge(s, count)

            def turns(engine, body):
                body(0, 0, "first")
                with engine.Fori(0, NKV - 1) as g:
                    body(g, 1, "")
                    body(g + 1, 0, "")
                body(NKV - 1, 1, "last")
                body(NKV, 0, "after")

            def sync(sp):
                m = a["mask_BxS2_bf1"]
                sp.dma_start(mask8[:, :], m.rearrange("b s -> (b s)").partition_broadcast(P)).then_inc(s_mask, 16)
                sp.dma_start(mrow8[:, :], m.rearrange("b (t p) -> (b t) p", p=P)).then_inc(s_mask, 16)

                def load(g):
                    c1, c2 = (slice(g * HD, (g + 1) * HD), slice(g * GW, (g + 1) * GW)) if isinstance(g, int) else (
                        bass.ds(g * HD, HD), bass.ds(g * GW, GW))
                    for name, cols, dst in (("Wk", c1, wk), ("Wq", c2, wq), ("Wv", c1, wv)):
                        sp.dma_start(dst[:, :, :], a[f"L0_xattn_{name}"].rearrange("(c p) n -> p c n", p=P)[:, :, cols]).then_inc(s_w, 16)

                def load_out(g):
                    rows = slice(g * GW, (g + 1) * GW) if isinstance(g, int) else bass.ds(g * GW, GW)
                    sp.dma_start(wo[:, :, :], a["L0_xattn_Wo"][rows, :].rearrange("(c p) n -> p c n", p=P)).then_inc(s_wo, 16)

                load(0)
                load_out(0)
                with sp.Fori(0, NKV - 1) as g:
                    sp.wait_ge(s_pj, NF * (B * g + 2))
                    load(g + 1)
                    sp.wait_ge(s_of, NO * (B * g + 2))
                    load_out(g + 1)

            def vector(dve):
                dve.wait_ge(s_mask, 32)
                dve.tensor_scalar(lower[:, :], mask8[:, :], -1.0, BIG, ALU.add, ALU.mult).then_inc(s_low, 1)
                dve.tensor_copy(mrow[:, :], mrow8[:, :]).then_inc(s_low, 1)
                dve.wait_ge(s_mtr, 1)
                dve.tensor_copy(mcol[:, :], PJ[:, 0:B * NK]).then_inc(s_low, 1)
                dve.wait_ge(s_ones, 2)
                dve.memset(scrap[:, 0:1], 0.0).then_inc(s_wd, QT)
                dve.wait_ge(s_low, 3)
                dve.wait_ge(s_tgate, 1)

                def front(h, b, name):
                    i = FRONT.index(name)
                    if name[0] == "v":
                        j = int(name[1])
                        k0 = b * NK + j * NK // 2
                        dve.wait_ge(s_pj, NF * h + i + 1)
                        if j == 0:
                            until(dve, s_pn, POOL * (h - 1) + 1)
                        ins = dve.tensor_tensor(vraw[:, j * NK // 2:(j + 1) * NK // 2, :], PJ[:, :].rearrange("p (k n) -> p k n", n=HD),
                                                mcol[:, k0:k0 + NK // 2].unsqueeze(2).to_broadcast([P, NK // 2, HD]), ALU.mult)
                    else:
                        dst = parts(b, name)
                        dve.wait_ge(s_hi, HI * h + i + 1)
                        ins = dve.tensor_tensor(dst[1], PJ[:, :], dst[0].bitcast(F32), ALU.subtract)
                    ins.then_inc(s_pjd, 1)

                for name in FRONT:
                    front(0, 0, name)

                def body(g, b, part):
                    h, before, own, ahead = B * g + b, part != "first", part != "after", part in ("first", "")

                    def reciprocal(n):
                        if n < 0 and not before:
                            dve.memset(scrap[:, 8 + n % 2:9 + n % 2], 0.0)
                            return
                        dve.wait_ge(s_ex, NS * h + n + 1)
                        col = slice(n % NS, n % NS + 1)
                        dve.reciprocal(rtotal[:, col], total[:, col]).then_inc(s_rt, 1)

                    def evacuate(n):
                        q = n % QT
                        for j in range(2):
                            keys = slice(j * NK // 2, (j + 1) * NK // 2)
                            dve.wait_ge(s_ta, 2 * (NS * h + n) + j + 1)
                            dve.tensor_tensor(pT[1][:, keys, q * P:(q + 1) * P], TR[j][:, :].rearrange("p (k n) -> p k n", n=P),
                                              pT[0][:, keys, q * P:(q + 1) * P].bitcast(F32), ALU.subtract).then_inc(s_td, 1)

                    def add_out(t):
                        dve.wait_ge(s_of, NO * (h - 1) + HPG + t + 1)
                        xt = x3[:, (1 - b) * QT + t, :]
                        dve.scalar_tensor_tensor(xt, PJ[:, :], tgate[:, 0:1], xt, ALU.mult, ALU.add).then_inc(s_wd, 1)

                    for n in range(NS):
                        if own:
                            dve.wait_ge(s_sc, NS * h + n + 1)
                            until(dve, s_tr, 2 * (NS * (h - 1) + n + 1))
                        if own or n < 2:
                            reciprocal(n - 2)
                        if own:
                            dve.tensor_tensor_reduce(
                                p[n][:, :], SC[n % 2][:, :], lower[:, b * S2:(b + 1) * S2], -SCALE,
                                3.0e38, ALU.add, ALU.min, least[:, n:n + 1]).then_inc(s_sm, 1)
                        if ahead and n in PROJECT:
                            front(h + 1, 1 - b, PROJECT[n])
                        if before and n in OUT_BEFORE:
                            add_out(OUT_BEFORE[n])
                        if own if n >= LAG else before:
                            evacuate(n - LAG)
                        if before and n in OUT_BEHIND:
                            add_out(OUT_BEHIND[n])

                turns(dve, body)

            def parts(b, name):
                i = int(name[1])
                return [kT[x][b][:, i * BANK:(i + 1) * BANK] if name[0] == "k" else qT[x][b][i][:, :] for x in range(2)]

            def scalar(act):
                act.wait_ge(s_ones, 2)

                def front(h, b, name):
                    act.wait_ge(s_pj, NF * h + FRONT.index(name) + 1)
                    act.activation(parts(b, name)[0], PJ[:, :], ACT.Copy).then_inc(s_hi, 1)

                def high_values(h, b):
                    act.wait_ge(s_pjd, NF * (h + 1))
                    until(act, s_of, NO * (h - 2) + HPG)
                    act.activation(v[0][b][:, :, :], vraw[:, :, :], ACT.Copy).then_inc(s_hi, 1)

                for name in FRONT[:HI - 1]:
                    front(0, 0, name)
                high_values(0, 0)

                def body(g, b, part):
                    h, before, own, ahead = B * g + b, part != "first", part != "after", part in ("first", "")
                    for n in range(NS):
                        if own:
                            act.wait_ge(s_sm, NS * h + n + 1)
                            act.activation(p[n][:, :], p[n][:, :], ACT.Exp, scale=-1.0, bias=least[:, n:n + 1],
                                           accum_out=total[:, n:n + 1]).then_inc(s_ex, 1)
                        if ahead and n < HI - 1:
                            front(h + 1, 1 - b, PROJECT[n])
                        if ahead and n == SPLIT:
                            high_values(h + 1, 1 - b)
                        if before and n in READY:
                            u = READY.index(n)
                            act.wait_ge(s_of, NO * (h - 1) + u + 1)
                            act.activation(oT[u][:, :], OB[:, :], ACT.Copy).then_inc(s_oa, 1)
                        if own if n >= LAG else before:
                            q = (n - LAG) % QT
                            for j in range(2):
                                act.wait_ge(s_tr, 2 * (NS * h + n - LAG) + j + 1)
                                act.activation(pT[0][:, j * NK // 2:(j + 1) * NK // 2, q * P:(q + 1) * P],
                                               TR[j][:, :].rearrange("p (k n) -> p k n", n=P), ACT.Copy).then_inc(s_ta, 1)

                turns(act, body)

            def gpsimd(pool):
                def body(g, b, part):
                    if part == "after":
                        return
                    h = B * g + b
                    pool.wait_ge(s_hi, HI * (h + 1))
                    pool.tensor_tensor(v[1][b][:, :, :], vraw[:, :, :], v[0][b][:, :, :].bitcast(F32), ALU.subtract).then_inc(s_pn, 1)
                    for n in range(NS):
                        pool.wait_ge(s_rt, NS * h + n + 1)
                        pool.tensor_tensor(carry[:, n:n + 1], rtotal[:, n:n + 1], rtotal[:, n:n + 1], ALU.mult)
                        pool.tensor_scalar(p[n][:, :], p[n][:, :], rtotal[:, n:n + 1], 1.0, ALU.mult, ALU.mult).then_inc(s_pn, 1)

                turns(pool, body)

            def tensor(pe):
                pe.wait_ge(s_lnev, NT)
                pe.wait_ge(s_ctxev, PAIRS)
                pe.wait_ge(s_low, 2)
                pe.transpose(PJ[:, 0:B * NK], mrow[:, :], ident[0:B * NK, 0:B * NK]).then_inc(s_mtr, 1)
                pe.wait_ge(s_low, 3)

                def front(h, b, name):
                    i, j = FRONT.index(name), int(name[1])
                    if i:
                        pe.wait_ge(s_pjd, NF * h + i)
                    else:
                        until(pe, s_pjd, NF * h)
                        until(pe, s_wd, QT * (h - 1))
                    if name[0] == "k":
                        for c in range(VC):
                            mm = pe.matmul(PJ[:, :], wk[:, c, :], ctxT3[:, c, b * S2 + j * BANK:b * S2 + (j + 1) * BANK],
                                           start=(c == 0), stop=(c == VC - 1))
                    elif name[0] == "q":
                        for c in range(KC):
                            mm = pe.matmul(PJ[:, :], wq[:, c, j * HD:(j + 1) * HD], hT3[:, c, b * S:(b + 1) * S],
                                           start=(c == 0), stop=(c == KC - 1))
                    else:
                        for k in range(NK // 2):
                            tok = b * S2 + (j * NK // 2 + k) * P
                            for c in range(VC):
                                mm = pe.matmul(PJ[:, k * HD:(k + 1) * HD], ctxT3[:, c, tok:tok + P], wv[:, c, :],
                                               start=(c == 0), stop=(c == VC - 1))
                    mm.then_inc(s_pj, 1)

                pe.wait_ge(s_w, 16 * LOADS)
                for name in FRONT:
                    front(0, 0, name)

                def body(g, b, part):
                    h, before, own, ahead = B * g + b, part != "first", part != "after", part in ("first", "")

                    def transposes(n):
                        pe.wait_ge(s_pn, POOL * h + n + (2 if n >= 0 else 1))
                        for j in range(2):
                            until(pe, s_td, 2 * (NS * h + n) - 1 + j)
                            for k in range(NK // 2):
                                kk = j * NK // 2 + k
                                mm = pe.transpose(TR[j][:, k * P:(k + 1) * P], p[n % NS][:, kk * P:(kk + 1) * P], ident[:, :])
                            mm.then_inc(s_tr, 1)

                    def values(m, turn, b):
                        u, half = m // 2, m % 2
                        cols = slice(half * HALF, (half + 1) * HALF)
                        if half == 0:
                            until(pe, s_oa, HPG * turn + u)
                        if m == 0:
                            pe.wait_ge(s_pn, POOL * turn + 1)
                        pe.wait_ge(s_td, 2 * (NS * turn + 2 * (m + 1)))
                        for n, (x0, x1) in enumerate(ACCURATE):
                            for k in range(NK):
                                mm = pe.matmul(OB[:, cols], v[x0][b][:, k, :], pT[x1][:, k, cols],
                                               start=(half == 0 and n == 0 and k == 0), stop=(half == 1 and n == 2 and k == NK - 1))
                        if half:
                            mm.then_inc(s_of, 1)

                    def project_out(t):
                        if t == 0:
                            pe.wait_ge(s_oa, HPG * h)
                            pe.wait_ge(s_wo, 16 * (g + b))
                        if t == 0 and ahead:
                            pe.wait_ge(s_pjd, NF * (h + 2))
                        else:
                            pe.wait_ge(s_wd, QT * h + t)
                        for u in range(HPG):
                            mm = pe.matmul(PJ[:, :], oT[u][:, t * P:(t + 1) * P], wo[:, u, :], start=(u == 0), stop=(u == HPG - 1))
                        mm.then_inc(s_of, 1)

                    for n in range(NS):
                        if own:
                            if n == 0:
                                pe.wait_ge(s_pjd, NF * h + HI - 1)
                            until(pe, s_sm, NS * h + n - 1)
                            for j in range(2):
                                for m, (x0, x1) in enumerate(ACCURATE):
                                    mm = pe.matmul(SC[n % 2][:, j * BANK:(j + 1) * BANK], qT[x0][b][n // QT][:, n % QT * P:(n % QT + 1) * P],
                                                   kT[x1][b][:, j * BANK:(j + 1) * BANK], start=(m == 0), stop=(m == 2))
                            mm.then_inc(s_sc, 1)
                        if ahead and n in PROJECT:
                            if n == 0 and b == 1:
                                pe.wait_ge(s_w, 16 * LOADS * (g + 2))
                            front(h + 1, 1 - b, PROJECT[n])
                        if before and n in OUT_BEFORE:
                            project_out(OUT_BEFORE[n])
                        if n >= VALUES and own and (n - VALUES) % 2 == 0:
                            values((n - VALUES) // 2, h, b)
                        elif n < VALUES and before and (n - VALUES) % 2 == 0:
                            values(NS // 2 + (n - VALUES) // 2, h - 1, 1 - b)
                        if own if n >= LAG else before:
                            transposes(n - LAG)
                        if before and n in OUT_BEHIND:
                            project_out(OUT_BEHIND[n])

                turns(pe, body)

            programs["SP"].append(sync)
            programs["DVE"].append(vector)
            programs["ACT"].append(scalar)
            programs["POOL"].append(gpsimd)
            programs["PE"].append(tensor)
            return s_wd, QT * (TURNS + 1)

        x_done = cross_attention_0()

        def layernorm_to_y(n, before):
            s_y = sem("s_y")
            statistics(n, before)

            def vector(dve):
                dve.wait_ge(s_rstd, n + 1)
                for t in range(NT):
                    dve.tensor_scalar(y3[:, t, :], x3[:, t, :], mv[:, 2 * t:2 * t + 1], rstd[:, t:t + 1],
                                      ALU.subtract, ALU.mult).then_inc(s_y, 1)

            programs["DVE"].append(vector)
            return s_y

        s_rnw, s_rnsq, s_rnstd, s_rnrstd, s_rnh, s_rntr, s_rnhi, s_rnlo = [
            sem(f"rn_{n}") for n in ("w", "sq", "std", "rstd", "h", "tr", "hi", "lo")]

        def rmsnorm(k, s_y, y_count, weight, hi, lo, rows=None):
            sumsq = sb(f"rn{k}_sumsq", [P, NT])
            rms = sb(f"rn{k}_rms", [P, NT])
            rrms = sb(f"rn{k}_rrms", [P, NT])
            own = ExitStack() if k == 0 else phase
            wrow = own.enter_context(nc.sbuf_tensor(f"rn{k}_wrow", [P, D], F32))
            square = own.enter_context(nc.sbuf_tensor(f"rn{k}_square", [P, 2 * D], F32))
            if k == 0:
                own.close()

            def sync(sp):
                sp.wait_ge(s_y, y_count(0))
                sp.dma_start(wrow[:, :], a[weight].partition_broadcast(P)).then_inc(s_rnw, 16)
                if rows:
                    for t in range(NT):
                        sp.wait_ge(s_rnh, k * NT + t + 1)
                        sp.dma_start(rows[0][t * P:(t + 1) * P, :], hslot[:, (t % 2) * D:(t % 2 + 1) * D]).then_inc(rows[1][t % 2], 16)

            def scalar(act):
                for t in range(NT):
                    act.wait_ge(s_y, y_count(t))
                    if t >= 2:
                        act.wait_ge(s_rnsq, k * NT + t - 1)
                    act.activation(square[:, (t % 2) * D:(t % 2 + 1) * D], y3[:, t, :], ACT.Square,
                                   accum_out=sumsq[:, t:t + 1]).then_inc(s_rnsq, 1)
                act.wait_ge(s_rnsq, (k + 1) * NT)
                act.activation(rms[:, :], sumsq[:, :], ACT.Sqrt, scale=1.0 / D, bias=eps[:, 0:1]).then_inc(s_rnstd, 1)
                for t in range(NT):
                    act.wait_ge(s_rntr, k * NT + t + 1)
                    act.activation(hi[:, :, t * P:(t + 1) * P], banks[t % 2][:, :].rearrange("p (c n) -> p c n", c=KC),
                                   ACT.Copy).then_inc(s_rnhi, 1)

            def vector(dve):
                dve.wait_ge(s_rnstd, k + 1)
                dve.reciprocal(rrms[:, :], rms[:, :]).then_inc(s_rnrstd, 1)
                dve.wait_ge(s_rnrstd, k + 1)
                dve.wait_ge(s_rnw, 16 * (k + 1))

                def low(t):
                    dve.wait_ge(s_rnhi, k * NT + t + 1)
                    part = slice(t * P, (t + 1) * P)
                    dve.tensor_tensor(lo[:, :, part], banks[t % 2][:, :].rearrange("p (c n) -> p c n", c=KC),
                                      hi[:, :, part].bitcast(F32), ALU.subtract).then_inc(s_rnlo, 1)

                for t in range(NT):
                    if t >= 2:
                        dve.wait_ge(s_rntr, k * NT + t - 1)
                        if rows:
                            dve.wait_ge(rows[1][t % 2], 16 * (t // 2))
                    dve.scalar_tensor_tensor(hslot[:, (t % 2) * D:(t % 2 + 1) * D], y3[:, t, :], rrms[:, t:t + 1],
                                             wrow[:, :], ALU.mult, ALU.mult).then_inc(s_rnh, 1)
                    if t >= 1:
                        low(t - 1)
                low(NT - 1)

            def tensor(pe):
                for t in range(NT):
                    pe.wait_ge(s_rnh, k * NT + t + 1)
                    if t >= 2:
                        pe.wait_ge(s_rnlo, k * NT + t - 1)
                    for c in range(KC):
                        mm = pe.transpose(banks[t % 2][:, c * P:(c + 1) * P],
                                          hslot[:, (t % 2) * D + c * P:(t % 2) * D + (c + 1) * P], ident[:, :])
                    mm.then_inc(s_rntr, 1)

            programs["SP"].append(sync)
            programs["ACT"].append(scalar)
            programs["DVE"].append(vector)
            programs["PE"].append(tensor)

        phase.close()
        phase = ExitStack()
        y = sb("y", [P, NT * D])
        y3 = y[:, :].rearrange("p (t d) -> p t d", t=NT)
        inner = ExitStack()
        phase, outer = inner, phase
        s_y0 = layernorm_to_y(1, x_done)
        hTa = [sb(f"hT_attn{i}", [P, KC, T], F32R) for i in range(2)]
        rmsnorm(0, s_y0, lambda t: t + 1, "L0_ffn_ln_w", hTa[0], hTa[1])

        def self_attention():
            NKV, HPG, HD = 8, 4, 64
            TURNS = B * NKV
            PPB = HPG // 2
            GW = HPG * HD
            NQK = HPG + 1
            PW = (NQK + 1) * HD
            NST = HPG + 2
            SCALE = 1.0 / float(np.sqrt(HD))
            HALF = S // 2
            NS = HPG * QT
            LAG, RING = 5, 8
            assert LAG % 2 and B == 2 and NS % RING == 0 and LAG < RING
            PROJECT = (1, 2, 3, 4)
            ROTATE, ROTATED = (3, 5), (6, 7)
            HIGH, LOW = (7, 8, 9, 10), (9, 9, 10, 11)
            WEIGHTS, OUT_WEIGHTS = (5, 6), (3, 4)
            STACK = (13, 13, 14, 14, 15, 15)
            PAIR = NS // PPB
            PAIR_DONE = PAIR + LAG + 1
            OUT = (9, 10, 11, 12)
            assert PAIR_DONE + PAIR - NS < OUT[0] and B * PAIR <= NS
            raw = sb("s_raw", [P, QT, PW])
            wraw = sb("s_wraw", [P, KC, PW])
            w = [sb(f"s_w{i}", [P, KC, PW], F32R) for i in range(2)]
            woraw = sb("s_woraw", [P, PPB, D])
            wo = [sb(f"s_wo{i}", [P, PPB, D], F32R) for i in range(2)]
            rot = sb("s_rot", [P, QT, NQK, HD])
            turned = sb("s_turned", [P, QT, NQK, HD])
            q2 = sb("s_q2", [P, QT, HPG, 2, HD], F32R)
            k2 = sb("s_k2", [P, QT, 3, HD], F32R)
            qS = [sb(f"s_qS{b}", [P, HPG, S], F32R) for b in range(B)]
            kS = [sb(f"s_kS{b}", [P, S], F32R) for b in range(B)]
            kL = [sb(f"s_kL{b}", [HD, S], F32R) for b in range(B)]
            v = [sb(f"s_v{b}", [P, QT, 5, HD], F32R) for b in range(B)]
            p = [sb(f"s_p{i}", [P, S]) for i in range(RING)]
            pT = [sb(f"s_pT{i}", [P, QT, S], F32R) for i in range(2)]
            oT = [sb(f"s_oT{i}", [P, PPB, S], F32R) for i in range(2)]
            least = sb("s_least", [P, RING])
            total = sb("s_total", [P, RING])
            rtotal = sb("s_rtotal", [P, RING])
            carry = sb("s_carry", [P, RING])
            causal = sb("s_causal", [P, S])
            cos, sin = sb("s_cos", [P, QT, HD]), sb("s_sin", [P, QT, HD])

            PJ, OB, TR = banks[0:2], banks[2], banks[3:5]
            SC = [banks[5][:, 0:P], banks[5][:, P:3 * P], banks[6][:, 0:3 * P], banks[7][:, 0:S]]
            s_c, s_w, s_wo, s_wh, s_wl = [sem(f"s_{n}") for n in ("c", "w", "wo", "wh", "wl")]
            s_pr, s_pra, s_wf, s_wd, s_of, s_oh, s_ol = [
                sem(f"s_{n}") for n in ("pr", "pra", "wf", "wd", "of", "oh", "ol")]
            s_cos, s_hi, s_lo, s_sc, s_sm, s_ex, s_rt, s_pn, s_tr, s_th, s_tl = [
                sem(f"s_{n}") for n in ("cos", "hi", "lo", "sc", "sm", "ex", "rt", "pn", "tr", "th", "tl")]
            w_count, wo_count = lambda g: 2 if isinstance(g, int) and g == 0 else 4 * g, lambda g: 4 * g + 6
            FRONT = QT + NST
            LOADS, PARTS, DERIVED = 3, 4, 8
            ORDER = {"turned": 1, "rotated": 3, "value": 5}
            PAIRS = [slice(2 * i, 2 * i + 2) for i in range(QT // 2)]

            def until(engine, s, count):
                if not isinstance(count, int) or count > 0:
                    engine.wait_ge(s, count)

            def halves(weights, i):
                return weights[:, i * weights.shape[1] // 2:(i + 1) * weights.shape[1] // 2, :]

            def turns(engine, body):
                body(0, 0, "first")
                with engine.Fori(0, NKV - 1) as g:
                    body(g, 1, "")
                    body(g + 1, 0, "")
                body(NKV - 1, 1, "last")
                body(NKV, 0, "after")

            def sync(sp):
                for dst, name in ((causal[:, :], "c_causal"), (cos[:, :, :], "c_cos"), (sin[:, :, :], "c_sin")):
                    sp.dma_start(dst, a[name]).then_inc(s_c, 16)

                def load(g):
                    c1, c2 = (slice(g * HD, (g + 1) * HD), slice(g * GW, (g + 1) * GW)) if isinstance(g, int) else (
                        bass.ds(g * HD, HD), bass.ds(g * GW, GW))
                    for name, cols, dst in (("wq", c2, slice(0, GW)), ("wk", c1, slice(GW, GW + HD)), ("wv", c1, slice(GW + HD, PW))):
                        sp.dma_start(wraw[:, :, dst], a[f"L0_ffn_{name}"].rearrange("(c p) n -> p c n", p=P)[:, :, cols]).then_inc(s_w, 16)

                def load_out(g):
                    rows = slice(g * GW, (g + 1) * GW) if isinstance(g, int) else bass.ds(g * GW, GW)
                    sp.dma_start(woraw[:, :, :], a["L0_ffn_wo"][rows, :].rearrange("(c p) n -> p c n", p=P)).then_inc(s_wo, 16)

                load(0)
                load_out(0)
                with sp.Fori(0, NKV - 1) as g:
                    sp.wait_ge(s_wl, 4 * g + 2)
                    load(g + 1)
                    sp.wait_ge(s_wl, wo_count(g))
                    load_out(g + 1)
                sp.wait_ge(s_wl, 4 * NKV - 2)
                load(0)

            def vector(dve):
                dve.wait_ge(s_c, 48)

                def rotate(h, i):
                    t = PAIRS[i]
                    dve.wait_ge(s_pra, FRONT * h + t.stop)
                    src = raw[:, t, 0:NQK * HD].rearrange("p t (h d) -> p t h d", d=HD)
                    for n in range(2):
                        to, other = slice(n * HD // 2, (n + 1) * HD // 2), slice((1 - n) * HD // 2, (2 - n) * HD // 2)
                        ins = dve.tensor_tensor(turned[:, t, :, to], src[:, :, :, other],
                                                sin[:, t, to].unsqueeze(2).to_broadcast([P, 2, NQK, HD // 2]), ALU.mult)
                    ins.then_inc(s_lo, 1)

                def rotated(h, i):
                    t = PAIRS[i]
                    dve.wait_ge(s_lo, DERIVED * h + ORDER["turned"] + i)
                    dve.wait_ge(s_cos, QT * h + t.stop)
                    dve.tensor_tensor(rot[:, t, :, :], rot[:, t, :, :], turned[:, t, :, :], ALU.add).then_inc(s_lo, 1)

                def low_value(h, b):
                    dve.wait_ge(s_hi, PARTS * h + 1)
                    dve.tensor_tensor(v[b][:, :, 3, :], raw[:, :, NQK * HD:], v[b][:, :, 1, :].bitcast(F32),
                                      ALU.subtract).then_inc(s_lo, 1)

                def low_queries(h, i):
                    t = PAIRS[i]
                    dve.wait_ge(s_hi, PARTS * h + 3 + i)
                    dve.tensor_tensor(q2[:, t, :, 1, :], rot[:, t, 0:HPG, :], q2[:, t, :, 0, :].bitcast(F32),
                                      ALU.subtract).then_inc(s_lo, 1)

                def low_keys(h):
                    dve.wait_ge(s_hi, PARTS * h + 2)
                    dve.tensor_tensor(k2[:, :, 0, :], rot[:, :, HPG, :], k2[:, :, 1, :].bitcast(F32),
                                      ALU.subtract).then_inc(s_lo, 1)

                for i in range(2):
                    rotate(0, i)
                for i in range(2):
                    rotated(0, i)
                low_value(0, 0)
                low_keys(0)
                for i in range(2):
                    low_queries(0, i)

                def body(g, b, part):
                    h, before, own, ahead = B * g + b, part != "first", part != "after", part in ("first", "")

                    def reciprocal(n):
                        if n < 0 and not before:
                            dve.memset(scrap[:, 16 + n % 2:17 + n % 2], 0.0)
                            return
                        dve.wait_ge(s_ex, NS * h + n + 1)
                        col = slice(n % RING, n % RING + 1)
                        dve.reciprocal(rtotal[:, col], total[:, col]).then_inc(s_rt, 1)

                    def low(n):
                        q = n % QT
                        dve.wait_ge(s_th, NS * h + n + 1)
                        cols = slice(q * P, (q + 1) * P)
                        dve.tensor_tensor(pT[1][:, 0:q + 1, cols], TR[n % 2][:, 0:(q + 1) * P].rearrange("p (k n) -> p k n", n=P),
                                          pT[0][:, 0:q + 1, cols].bitcast(F32), ALU.subtract).then_inc(s_tl, 1)

                    def low_outputs(i, turn):
                        dve.wait_ge(s_oh, PPB * turn + i + 1)
                        dve.tensor_tensor(oT[1][:, i, :], OB[:, :], oT[0][:, i, :].bitcast(F32), ALU.subtract).then_inc(s_ol, 1)

                    def add_out(t):
                        dve.wait_ge(s_wf, QT * (h - 1) + t + 1)
                        yt = y3[:, (1 - b) * QT + t, :]
                        dve.tensor_tensor(yt, PJ[t % 2][:, :], yt, ALU.add).then_inc(s_wd, 1)

                    for n in range(NS):
                        q = n % QT
                        if before and n == PAIR_DONE + PAIR - NS + 1:
                            low_outputs(PPB - 1, h - 1)
                        if own and n == PAIR_DONE + 1:
                            low_outputs(0, h)
                        if own:
                            dve.wait_ge(s_sc, NS * h + n + (2 if q == 0 else 1))
                            reciprocal(n - 2)
                            width = (q + 1) * P
                            dve.tensor_tensor_reduce(
                                p[n % RING][:, 0:width], SC[q][:, 0:width], causal[:, S - width:S], -SCALE, 3.0e38, ALU.add, ALU.min,
                                least[:, n % RING:n % RING + 1]).then_inc(s_sm, 1)
                        elif n < 2:
                            reciprocal(n - 2)
                        if n - LAG - 1 >= 0 and own or before and n <= LAG:
                            low(n - LAG - 1)
                        for t in range(QT):
                            if before and n == OUT[t]:
                                add_out(t)
                        if ahead:
                            for i in range(2):
                                if n == ROTATE[i]:
                                    rotate(h + 1, i)
                            for i in range(2):
                                if n == ROTATED[i]:
                                    rotated(h + 1, i)
                            if n == LOW[0]:
                                low_value(h + 1, 1 - b)
                            if n == LOW[1]:
                                low_keys(h + 1)
                            for i in range(2):
                                if n == LOW[2 + i]:
                                    low_queries(h + 1, i)

                turns(dve, body)

            def scalar(act):
                for b in range(B):
                    act.activation(v[b][:, :, 0:5:2, :],
                                   scrap[:, 63:64].unsqueeze(2).unsqueeze(3).to_broadcast([P, QT, 3, HD]), ACT.Copy)
                act.wait_ge(s_w, 16 * LOADS)
                for i in range(2):
                    act.activation(halves(w[0], i), halves(wraw, i), ACT.Copy).then_inc(s_wh, 1)

                def projection(h, t):
                    act.wait_ge(s_pr, FRONT * h + t + 1)
                    if t == 0:
                        until(act, s_lo, DERIVED * h)
                    act.activation(raw[:, t, :], PJ[t % 2][:, 0:PW], ACT.Copy).then_inc(s_pra, 1)

                def high_value(h, b):
                    act.wait_ge(s_pra, FRONT * h + QT)
                    until(act, s_of, PPB * (h - 1))
                    act.activation(v[b][:, :, 1, :], raw[:, :, NQK * HD:], ACT.Copy).then_inc(s_hi, 1)

                def high_keys(h):
                    act.wait_ge(s_lo, DERIVED * h + ORDER["rotated"] + 1)
                    until(act, s_pr, FRONT * h)
                    act.activation(k2[:, :, 1:3, :], rot[:, :, HPG:NQK, :].to_broadcast([P, QT, 2, HD]), ACT.Copy).then_inc(s_hi, 1)

                def high_queries(i):
                    t = PAIRS[i]
                    act.activation(q2[:, t, :, 0, :], rot[:, t, 0:HPG, :], ACT.Copy).then_inc(s_hi, 1)

                def stacked(h, b, r):
                    act.wait_ge(s_pr, FRONT * h + QT + r + 1)
                    rows, dst = (P, kS[b][:, :]) if r == 0 else (HD, kL[b][:, :]) if r == 1 else (P, qS[b][:, r - 2, :])
                    act.activation(dst, PJ[r % 2][0:rows, :].bitcast(F32R), ACT.Copy).then_inc(s_pra, 1)

                for t in range(QT):
                    projection(0, t)
                high_value(0, 0)
                high_keys(0)
                for i in range(2):
                    high_queries(i)
                for r in range(NST):
                    stacked(0, 0, r)

                def body(g, b, part):
                    h, before, own, ahead = B * g + b, part != "first", part != "after", part in ("first", "")

                    def high(n):
                        q = n % QT
                        act.wait_ge(s_tr, NS * h + n + 1)
                        act.activation(pT[0][:, 0:q + 1, q * P:(q + 1) * P],
                                       TR[n % 2][:, 0:(q + 1) * P].rearrange("p (k n) -> p k n", n=P), ACT.Copy).then_inc(s_th, 1)

                    def outputs(i, turn):
                        act.wait_ge(s_of, PPB * turn + i + 1)
                        act.activation(oT[0][:, i, :], OB[:, :], ACT.Copy).then_inc(s_oh, 1)

                    for n in range(NS):
                        if n - LAG - 1 >= 0 and own or before and n <= LAG:
                            high(n - LAG - 1)
                        if own:
                            act.wait_ge(s_sm, NS * h + n + 1)
                            k = n % RING
                            row = p[k][:, 0:(n % QT + 1) * P]
                            act.activation(row, row, ACT.Exp, scale=-1.0, bias=least[:, k:k + 1],
                                           accum_out=total[:, k:k + 1]).then_inc(s_ex, 1)
                        if before and n == PAIR_DONE + PAIR - NS:
                            outputs(PPB - 1, h - 1)
                        if own and n == PAIR_DONE:
                            outputs(0, h)
                        if ahead:
                            for t in range(QT):
                                if n == PROJECT[t]:
                                    projection(h + 1, t)
                            if n == HIGH[0]:
                                high_value(h + 1, 1 - b)
                            if n == HIGH[1]:
                                high_keys(h + 1)
                            for i in range(2):
                                if n == HIGH[2 + i]:
                                    high_queries(i)
                            for i in range(2):
                                if n == WEIGHTS[i] and b == 0:
                                    act.wait_ge(s_w, 16 * LOADS * (g + 2))
                                    act.wait_ge(s_pr, FRONT * (h + 1) + QT)
                                    act.activation(halves(w[0], i), halves(wraw, i), ACT.Copy).then_inc(s_wh, 1)
                            for r in range(NST):
                                if n == STACK[r]:
                                    stacked(h + 1, 1 - b, r)
                        for i in range(2):
                            if own and b == 1 and n == OUT_WEIGHTS[i]:
                                act.wait_ge(s_wo, 16 * (g + 1))
                                act.activation(halves(wo[0], i), halves(woraw, i), ACT.Copy).then_inc(s_wh, 1)

                turns(act, body)

            def gpsimd(pool):
                pool.wait_ge(s_c, 48)

                def low(dst, src, i, count):
                    pool.wait_ge(s_wh, count - 1 + i)
                    pool.tensor_tensor(halves(dst[1], i), halves(src, i), halves(dst[0], i).bitcast(F32), ALU.subtract).then_inc(s_wl, 1)

                def cosine(h, t):
                    pool.wait_ge(s_pra, FRONT * h + t + 1)
                    pool.tensor_tensor(rot[:, t, :, :], raw[:, t, 0:NQK * HD].rearrange("p (h d) -> p h d", d=HD),
                                       cos[:, t, :].unsqueeze(1).to_broadcast([P, NQK, HD]), ALU.mult).then_inc(s_cos, 1)

                for i in range(2):
                    low(w, wraw, i, w_count(0))
                for t in range(QT):
                    cosine(0, t)

                def body(g, b, part):
                    h, ahead = B * g + b, part in ("first", "")
                    if part == "after":
                        return
                    for n in range(NS):
                        k = n % RING
                        row = p[k][:, 0:(n % QT + 1) * P]
                        pool.wait_ge(s_rt, NS * h + n + 1)
                        pool.tensor_tensor(carry[:, k:k + 1], rtotal[:, k:k + 1], rtotal[:, k:k + 1], ALU.mult)
                        pool.tensor_scalar(row, row, rtotal[:, k:k + 1], 1.0, ALU.mult, ALU.mult).then_inc(s_pn, 1)
                        for t in range(QT):
                            if ahead and n == max(PROJECT[t] - 1, 0):
                                cosine(h + 1, t)
                        for i in range(2):
                            if ahead and b == 0 and n == WEIGHTS[i]:
                                low(w, wraw, i, w_count(g + 1))
                            if b == 1 and n == OUT_WEIGHTS[i]:
                                low(wo, woraw, i, wo_count(g))

                turns(pool, body)

            def tensor(pe):
                pe.wait_ge(s_rnlo, NT)
                pe.wait_ge(s_idr, 1)

                def project_in(h, b, t):
                    if t >= 2:
                        pe.wait_ge(s_pra, FRONT * h + t - 1)
                    else:
                        until(pe, s_pra, FRONT * h - 1 + t)
                    o = PJ[t % 2]
                    rows = slice((b * QT + t) * P, (b * QT + t + 1) * P)
                    for n, (x0, x1) in enumerate(ACCURATE):
                        for c in range(KC):
                            mm = pe.matmul(o[:, 0:PW], hTa[x0][:, c, rows], w[x1][:, c, :],
                                           start=(n == 0 and c == 0), stop=(n == 2 and c == KC - 1))
                    mm.then_inc(s_pr, 1)

                def stack(h, r, after_out):
                    if r >= 2:
                        pe.wait_ge(s_pra, FRONT * h + QT + r - 1)
                    elif after_out:
                        pe.wait_ge(s_wd, QT * (h - 2) + QT - 1 + r)
                    else:
                        pe.wait_ge(s_pra, FRONT * h + QT - 1 + r)
                    if r in (0, 2):
                        pe.wait_ge(s_lo, DERIVED * h + ORDER["value"] + 1 if r == 0 else DERIVED * (h + 1))
                    for t in range(QT):
                        src = k2[:, t, 1:3, :] if r == 0 else k2[:, t, 0:2, :] if r == 1 else q2[:, t, r - 2, :, :]
                        mm = pe.transpose(PJ[r % 2][:, t * P:(t + 1) * P].bitcast(F32R), src.rearrange("p k d -> p (k d)"), identr[:, :])
                    mm.then_inc(s_pr, 1)

                pe.wait_ge(s_wl, w_count(0))
                for t in range(QT):
                    project_in(0, 0, t)
                for r in range(NST):
                    stack(0, r, False)

                def body(g, b, part):
                    h, before, own, ahead = B * g + b, part != "first", part != "after", part in ("first", "")

                    def transposes(n):
                        q = n % QT
                        pe.wait_ge(s_pn, NS * h + n + 1)
                        until(pe, s_tl, NS * h + n - 1)
                        for k in range(q + 1):
                            mm = pe.transpose(TR[n % 2][:, k * P:(k + 1) * P], p[n % RING][:, k * P:(k + 1) * P], ident[:, :])
                        mm.then_inc(s_tr, 1)

                    def values(m, turn, b):
                        i, half = m // 2, m % 2
                        if half == 0 and i == 0:
                            pe.wait_ge(s_lo, DERIVED * turn + ORDER["value"])
                        if half == 0 and i % 2 == 0:
                            until(pe, s_ol, PPB * turn + i // 2)
                        pe.wait_ge(s_tl, NS * turn + 2 * (m + 1))
                        for k in range(2 * half + 2):
                            cols = slice(max(k * P, half * HALF), (half + 1) * HALF)
                            for n, (x0, x1) in enumerate(ACCURATE):
                                first = 2 * x0 + (1 - i % 2)
                                mm = pe.matmul(OB[:, cols], v[b][:, k, first:first + 2, :].rearrange("p k d -> p (k d)"),
                                               pT[x1][:, k, cols], start=(i % 2 == 0 and half == 0 and k == 0 and n == 0),
                                               stop=(i % 2 == 1 and half == 1 and k == QT - 1 and n == 2))
                        if i % 2 and half:
                            mm.then_inc(s_of, 1)

                    def project_out(t):
                        if t == 0:
                            pe.wait_ge(s_ol, PPB * h)
                            pe.wait_ge(s_wl, wo_count(g + b - 1))
                        if t >= 2:
                            pe.wait_ge(s_wd, QT * (h - 1) + t - 1)
                        elif ahead:
                            pe.wait_ge(s_pra, FRONT * (h + 1) + QT - 1 + t)
                        elif own:
                            pe.wait_ge(s_pra, FRONT * (h + 1) - 1 + t)
                        else:
                            pe.wait_ge(s_wd, QT * (h - 1) - 1 + t)
                        for n, (x0, x1) in enumerate(ACCURATE):
                            for i in range(PPB):
                                mm = pe.matmul(PJ[t % 2][:, :], oT[x0][:, i, t * P:(t + 1) * P], wo[x1][:, i, :],
                                               start=(n == 0 and i == 0), stop=(n == 2 and i == PPB - 1))
                        mm.then_inc(s_wf, 1)

                    for n in range(NS):
                        u, q = n // QT, n % QT
                        if own:
                            if q == 0:
                                pe.wait_ge(s_pra, FRONT * h + QT + 3 + u)
                            for k in () if q == 1 else (0, 1) if q == 0 else (q,):
                                if k != 1:
                                    until(pe, s_sm, NS * h + n - (2 if q == 0 else 3))
                                cols, width = slice(k * P, (k + 1) * P), (k + 1) * P
                                pe.matmul(SC[k][:, 0:width], qS[b][:, u, cols], kS[b][:, 0:width], start=True, stop=False)
                                mm = pe.matmul(SC[k][:, 0:width], qS[b][0:HD, u, cols], kL[b][:, 0:width], start=False, stop=True)
                            if q != 1:
                                mm.then_inc(s_sc, 2 if q == 0 else 1)
                        for t in range(QT):
                            if ahead and n == PROJECT[t]:
                                if t == 0 and b == 1:
                                    pe.wait_ge(s_wl, w_count(g + 1))
                                project_in(h + 1, 1 - b, t)
                            if before and n == OUT[t]:
                                project_out(t)
                        for r in range(NST):
                            if ahead and n == STACK[r]:
                                stack(h + 1, r, before)
                        m = (n - LAG - 3) // 2
                        if (n - LAG - 3) % 2 == 0:
                            if m >= 0 and own:
                                values(m, h, b)
                            elif m < 0 and before:
                                values(NS // 2 + m, h - 1, 1 - b)
                        if n >= LAG and own or n < LAG and before:
                            transposes(n - LAG)

                turns(pe, body)

            programs["SP"].append(sync)
            programs["DVE"].append(vector)
            programs["ACT"].append(scalar)
            programs["POOL"].append(gpsimd)
            programs["PE"].append(tensor)
            return s_wd, QT * TURNS

        y_done = self_attention()
        inner.close()
        phase = outer
        NE, TOPK, HID = 16, 4, 512
        HC = HID // P
        hh = [sb(f"m_h{i}", [P, KC, T], F32R) for i in range(2)]
        gate = sb("m_gate", [P, NE, NT])
        CAP = T * TOPK // NE * 3 // 2
        CT = CAP // P
        place = sb("m_place", [P, NE + 2, NT])
        where = sb("m_where", [P, TOPK, NT], I32)
        share = sb("m_share", [P, TOPK, NT])
        crowded = sb("m_crowded", [P, 1], I32)
        token = sb("m_token", [P, NT, 2], BF16)
        h_rows = nc.dram_tensor("h_rows", (T, D), F32, kind="Internal").ap()
        y_rows = nc.dram_tensor("y_rows", (NE * CAP, D), F32, kind="Internal").ap()
        s_hrow = [sem(f"m_hrow{i}") for i in range(2)]
        moe_small = ExitStack()
        phase, outer = moe_small, phase
        rmsnorm(1, y_done[0], lambda t: y_done[1], "L0_ffn_ff_ln_w", hh[0], hh[1], (h_rows, s_hrow))

        def route():
            wg = sb("r_wg", [P, KC, NE])
            wgs = [sb(f"r_wg{i}", [P, KC, NE], F32R) for i in range(2)]
            logit = sb("r_logit", [P, NT, NE])
            top = sb("r_top", [P, NT, 8])
            low = sb("r_low", [P, NT])
            rest = sb("r_rest", [P, NT, NE])
            chosen = sb("r_chosen", [P, NT, NE])
            total = sb("r_total", [P, NT])
            rtotal = sb("r_rtotal", [P, NT])
            before = sb("r_before", [P, P])
            ones = sb("r_ones", [P, P])
            first = sb("r_first", [P, NE])
            token32 = sb("r_token", [P, NT, 2])
            run = sb("r_run", [P, NT + 1, NE])
            pos = sb("r_pos", [P, NT, NE])
            row = sb("r_row", [P, NT, NE])
            rank = [sb(f"r_rank{i}", [P, NT, NE]) for i in range(2)]
            pick = sb("r_pickm", [P, NT, NE])
            row_k = sb("r_row_k", [P, TOPK, NT])
            most = sb("r_most", [P, 1])
            s_const2, s_cnt = sem("r_const"), sem("r_cnt")
            s_w, s_hi, s_lo, s_l, s_pick, s_ch, s_ex, s_gate = [
                sem(f"r_{n}") for n in ("w", "hi", "lo", "l", "pick", "ch", "ex", "gate")]

            def sync(sp):
                sp.dma_start(wg[:, :, :], a["L0_ffn_wg"].rearrange("(c p) n -> p c n", p=P)).then_inc(s_w, 16)
                for dst, name in ((before, "c_before"), (ones, "c_ones")):
                    sp.dma_start(dst[:, :], a[name]).then_inc(s_const2, 16)
                sp.dma_start(first[:, :], a["c_first"].partition_broadcast(P)).then_inc(s_const2, 16)
                sp.dma_start(token32[:, :, :], a["c_token"]).then_inc(s_const2, 16)

            def scalar(act):
                act.wait_ge(s_w, 16)
                act.activation(wgs[0][:, :, :], wg[:, :, :], ACT.Copy).then_inc(s_hi, 1)
                act.wait_ge(s_ch, NT + 3)
                act.activation(logit[:, :, :], logit[:, :, :], ACT.Exp).then_inc(s_ex, 1)

            def tensor(pe):
                pe.wait_ge(s_lo, 1)
                pe.wait_ge(s_rnlo, NT)
                for t in range(NT):
                    for n, (i, j) in enumerate(ACCURATE):
                        for c in range(KC):
                            mm = pe.matmul(banks[2][:, t * NE:(t + 1) * NE], hh[i][:, c, t * P:(t + 1) * P], wgs[j][:, c, :],
                                           start=(n == 0 and c == 0), stop=(n == 2 and c == KC - 1))
                mm.then_inc(s_l, 1)
                pe.wait_ge(s_const2, 64)
                pe.wait_ge(s_pick, NT + 2)
                flat = chosen[:, :, :].rearrange("p t e -> p (t e)")
                pe.matmul(banks[3][:, 0:NT * NE], before[:, :], flat, start=True, stop=True)
                pe.matmul(banks[3][:, NT * NE:2 * NT * NE], ones[:, :], flat, start=True, stop=True).then_inc(s_cnt, 1)

            def vector(dve):
                steps = 0

                def step(ins):
                    nonlocal steps
                    steps += 1
                    ins.then_inc(s_ch, 1)
                    dve.wait_ge(s_ch, steps)

                dve.wait_ge(s_hi, 1)
                dve.tensor_tensor(wgs[1][:, :, :], wg[:, :, :], wgs[0][:, :, :].bitcast(F32), ALU.subtract).then_inc(s_lo, 1)
                dve.wait_ge(s_l, 1)
                dve.tensor_copy(logit[:, :, :], banks[2][:, 0:NT * NE].rearrange("p (t e) -> p t e", e=NE)).then_inc(s_pick, 1)
                dve.wait_ge(s_pick, 1)
                for t in range(NT):
                    ins = dve.max(top[:, t, :], logit[:, t, :])
                    ins.then_inc(s_ch, 1)
                steps = NT
                dve.wait_ge(s_ch, NT)
                step(dve.tensor_copy(low[:, :], top[:, :, 0]))
                step(dve.memset(top[:, :, TOPK:], 3.0e38))
                for t in range(NT):
                    dve.match_replace(rest[:, t, :], top[:, t, :], logit[:, t, :], -3.0e38).then_inc(s_pick, 1)
                dve.wait_ge(s_pick, NT + 1)
                dve.tensor_tensor(chosen[:, :, :], logit[:, :, :], rest[:, :, :], ALU.not_equal).then_inc(s_pick, 1)
                dve.wait_ge(s_pick, NT + 2)
                step(dve.tensor_tensor(logit[:, :, :], logit[:, :, :], low[:, :].unsqueeze(2).to_broadcast([P, NT, NE]), ALU.subtract))
                dve.wait_ge(s_ex, 1)
                step(dve.tensor_tensor(logit[:, :, :], logit[:, :, :], chosen[:, :, :], ALU.mult))
                step(dve.tensor_reduce(total[:, :], logit[:, :, :], AX.X, ALU.add))
                step(dve.reciprocal(rtotal[:, :], total[:, :]))
                by_token = gate[:, :, :].rearrange("p e t -> p t e")
                step(dve.tensor_tensor(by_token, logit[:, :, :], rtotal[:, :].unsqueeze(2).to_broadcast([P, NT, NE]), ALU.mult))
                dve.wait_ge(s_const2, 64)
                dve.wait_ge(s_cnt, 1)
                step(dve.tensor_copy(token[:, :, :], token32[:, :, :]))
                step(dve.memset(place[:, :, :], 0.0))
                step(dve.memset(run[:, 0, :], 0.0))
                counts = banks[3][:, 0:2 * NT * NE].rearrange("p (n t e) -> p n t e", n=2, e=NE)
                for t in range(NT):
                    step(dve.tensor_tensor(run[:, t + 1, :], run[:, t, :], counts[:, 1, t, :], ALU.add))
                step(dve.tensor_tensor(pos[:, :, :], run[:, 0:NT, :], counts[:, 0, :, :], ALU.add))
                placed = place[:, 0:NE, :].rearrange("p e t -> p t e")
                step(dve.scalar_tensor_tensor(placed, pos[:, :, :], 1.0, chosen[:, :, :], ALU.add, ALU.mult))
                step(dve.tensor_tensor(row[:, :, :], placed, first[:, :].unsqueeze(1).to_broadcast([P, NT, NE]), ALU.add))
                src = chosen
                for k in range(4):
                    n, dst = 1 << k, rank[k % 2]
                    step(dve.tensor_copy(dst[:, :, 0:n], src[:, :, 0:n]))
                    step(dve.tensor_tensor(dst[:, :, n:], src[:, :, n:], src[:, :, 0:NE - n], ALU.add))
                    src = dst
                step(dve.tensor_tensor(rank[0][:, :, :], src[:, :, :], chosen[:, :, :], ALU.mult))
                for k in range(TOPK):
                    for value, dst in ((row[:, :, :], row_k), (by_token, share)):
                        step(dve.scalar_tensor_tensor(pick[:, :, :], rank[0][:, :, :], k + 1.0, value, ALU.is_equal, ALU.mult))
                        step(dve.tensor_reduce(dst[:, k, :], pick[:, :, :], AX.X, ALU.add))
                step(dve.tensor_copy(where[:, :, :], row_k[:, :, :]))
                step(dve.tensor_reduce(most[:, :], run[:, NT, :], AX.X, ALU.max))
                dve.tensor_scalar(crowded[:, :], most[:, :], float(CAP), None, ALU.is_gt).then_inc(s_gate, 1)

            programs["SP"].append(sync)
            programs["ACT"].append(scalar)
            programs["PE"].append(tensor)
            programs["DVE"].append(vector)
            return s_gate

        s_gated = route()
        moe_small.close()
        phase = outer

        def experts():
            NH = T // BANK
            TPH = NT // NH
            NS = NH * HC
            raw = [sb(f"e_raw{i}", [P, KC, HID]) for i in range(2)]
            w1 = [[sb(f"e_w1{s}{i}", [P, KC, HID], F32R) for i in range(2)] for s in range(2)]
            w3 = [[sb(f"e_w3{s}{i}", [P, KC, HID], F32R) for i in range(2)] for s in range(2)]
            w2 = [sb(f"e_w2{i}", [P, HC, D], F32R) for i in range(2)]
            silu = [sb(f"e_silu{i}", [P, BANK]) for i in range(2)]
            act32 = [sb(f"e_act{i}", [P, BANK]) for i in range(2)]
            carry = sb("e_carry", [P, 2])
            aT0 = [sb(f"e_aT0{i}", [P, HC, BANK], F32R) for i in range(2)]
            with ExitStack() as every_only:
                aT = [aT0, [every_only.enter_context(nc.sbuf_tensor(f"e_aT1{i}", [P, HC, BANK], F32R)) for i in range(2)]]
            with ExitStack() as few_only:
                rows = few_only.enter_context(nc.sbuf_tensor("e_rows", [P, CT, D], F32))
                mine = few_only.enter_context(nc.sbuf_tensor("e_mine", [P, NT, CAP], BF16))
                count_up = few_only.enter_context(nc.sbuf_tensor("e_count_up", [P, CAP], F32))
                ids32 = few_only.enter_context(nc.sbuf_tensor("e_ids32", [P, CT], F32))
                ids = [few_only.enter_context(nc.sbuf_tensor(f"e_ids{i}", [P, CT], I32)) for i in range(2)]
            GU, Y = pairs[0:2], banks[4:6]
            s_in = [sem(f"e_in{i}") for i in range(2)]
            s_mine, s_list, s_id, s_xt, s_xh, s_xl, s_got, s_add, s_done = [
                sem(f"e_{n}") for n in ("mine", "list", "id", "xt", "xh", "xl", "got", "add", "done")]
            s_up = sem("e_up")
            s_back = [sem(f"e_back{i}") for i in range(2)]
            s_st = [sem(f"e_st{i}") for i in range(2)]
            s_hi, s_lo, s_gu, s_sg, s_a, s_ah, s_al, s_y, s_yd = [
                sem(f"e_{n}") for n in ("hi", "lo", "gu", "sg", "a", "ah", "al", "y", "yd")]
            NW = 3 * NE

            def load(sp, n, e, kind):
                if not isinstance(e, int):
                    src = a[f"L0_ffn_{kind}"][bass.ds(e, 1), :, :].rearrange("e (c p) n -> p (e c) n", p=P)
                else:
                    src = a[f"L0_ffn_{kind}"][e].rearrange("(c p) n -> p c n", p=P)
                sp.dma_start(raw[n % 2][:, :, :], src).then_inc(s_in[n % 2], 16)

            def every_sync(sp):
                load(sp, 0, 0, "w1")
                load(sp, 1, 0, "w3")

                def body(i, s, last):
                    e = i * 2 + s
                    for k, kind in enumerate(("w2", "w1", "w3")):
                        if last and k:
                            continue
                        sp.wait_ge(s_lo, 3 * e + k + 1)
                        load(sp, 3 * s + k, e + (1 if k else 0), kind)

                with sp.Fori(0, NE // 2 - 1) as i:
                    for s in range(2):
                        body(i, s, False)
                body(NE // 2 - 1, 0, False)
                body(NE // 2 - 1, 1, True)

            def high(act, dst, n_in, parity):
                act.wait_ge(s_in[parity], n_in)
                act.activation(dst[:, :, :], raw[parity][:, :, :], ACT.Copy).then_inc(s_hi, 1)

            def every_scalar(act):
                high(act, w1[0][0], 16, 0)
                high(act, w3[0][0], 16, 1)

                def body(i, s, last):
                    e = i * 2 + s

                    def part_high(k):
                        act.wait_ge(s_a, NS * (e + 1) + k + 1)
                        act.activation(aT[k // HC][0][:, k % HC, :], act32[k % 2][:, :], ACT.Copy).then_inc(s_ah, 1)

                    act.wait_ge(s_y, NS * (e + 1))
                    high(act, w2[0], 16 * (3 * i + (1 if s == 0 else 3)) + (0 if s else 16), s)
                    for k in range(NS):
                        act.wait_ge(s_gu, NS * (e + 1) + k + 1)
                        act.activation(silu[k % 2][:, :], GU[k % 2][:, 0:BANK], ACT.Silu).then_inc(s_sg, 1)
                        if k >= 1:
                            part_high(k - 1)
                        if not last and k in (2, 5):
                            m = 3 * s + (1 if k == 2 else 2)
                            high(act, (w1 if k == 2 else w3)[1 - s][0], 16 * (3 * i + 1 + m // 2 + 1), m % 2)
                    part_high(NS - 1)

                with act.Fori(0, NE // 2 - 1) as i:
                    for s in range(2):
                        body(i, s, False)
                body(NE // 2 - 1, 0, False)
                body(NE // 2 - 1, 1, True)

            def low(pool, dst, n, parity):
                pool.wait_ge(s_hi, n)
                pool.tensor_tensor(dst[1][:, :, :], raw[parity][:, :, :], dst[0][:, :, :].bitcast(F32),
                                   ALU.subtract).then_inc(s_lo, 1)

            def every_gpsimd(pool):
                low(pool, w1[0], 1, 0)
                low(pool, w3[0], 2, 1)

                def body(i, s, last):
                    e = i * 2 + s
                    low(pool, w2, 3 * e + 3, s)
                    if not last:
                        low(pool, w1[1 - s], 3 * e + 4, (3 * s + 1) % 2)
                        low(pool, w3[1 - s], 3 * e + 5, (3 * s + 2) % 2)

                with pool.Fori(0, NE // 2 - 1) as i:
                    for s in range(2):
                        body(i, s, False)
                body(NE // 2 - 1, 0, False)
                body(NE // 2 - 1, 1, True)

            def every_vector(dve):
                dve.memset(scrap[:, 24:25], 0.0).then_inc(s_a, NS)
                dve.memset(scrap[:, 25:26], 0.0).then_inc(s_yd, NT)

                def body(i, s):
                    e = i * 2 + s

                    def part_low(k):
                        dve.wait_ge(s_ah, NS * e + k + 1)
                        dve.tensor_tensor(aT[k // HC][1][:, k % HC, :], act32[k % 2][:, :],
                                          aT[k // HC][0][:, k % HC, :].bitcast(F32), ALU.subtract).then_inc(s_al, 1)

                    for k in range(NS):
                        if k >= 2:
                            dve.wait_ge(s_al, NS * e + k - 1)
                        dve.wait_ge(s_sg, NS * e + k + 1)
                        dve.tensor_tensor(act32[k % 2][:, :], silu[k % 2][:, :], GU[k % 2][:, BANK:], ALU.mult).then_inc(s_a, 1)
                        if k >= 1:
                            part_low(k - 1)
                    part_low(NS - 1)
                    for t in range(NT):
                        dve.wait_ge(s_y, NS * (e + 1) + t + 1)
                        yt = y3[:, t, :]
                        g = gate[:, :, :].rearrange("p e t -> p (e t)")[:, bass.ds(e * NT + t, 1)]
                        dve.scalar_tensor_tensor(yt, Y[t % 2][:, :], g, yt, ALU.mult, ALU.add).then_inc(s_yd, 1)

                with dve.Fori(0, NE // 2) as i:
                    for s in range(2):
                        body(i, s)
                dve.wait_ge(s_yd, NT * (NE + 1))
                dve.memset(scrap[:, 26:27], 0.0).then_inc(s_done, 1)

            def every_tensor(pe):
                pe.transpose(banks[6][:, 0:P], ident[:, :], ident[:, :]).then_inc(s_gu, NS)
                pe.transpose(banks[6][:, 0:P], ident[:, :], ident[:, :]).then_inc(s_y, NS)

                def body(i, s):
                    e = i * 2 + s
                    for k in range(NS):
                        h, m = k // HC, k % HC
                        if k == 0:
                            pe.wait_ge(s_lo, 3 * e + 2)
                        pe.wait_ge(s_a, NS * (e + 1) + k - 1)
                        for j, w in enumerate((w1[s], w3[s])):
                            for n, (x0, x1) in enumerate(ACCURATE):
                                for c in range(KC):
                                    mm = pe.matmul(GU[k % 2][:, j * BANK:(j + 1) * BANK], w[x0][:, c, m * P:(m + 1) * P],
                                                   hh[x1][:, c, h * BANK:(h + 1) * BANK],
                                                   start=(n == 0 and c == 0), stop=(n == 2 and c == KC - 1))
                        mm.then_inc(s_gu, 1)
                    pe.wait_ge(s_lo, 3 * e + 3)
                    for t in range(NT):
                        h = t // TPH
                        if t % TPH == 0:
                            pe.wait_ge(s_al, NS * e + (h + 1) * HC)
                        pe.wait_ge(s_yd, NT * (e + 1) + t - 1)
                        for n, (x0, x1) in enumerate(ACCURATE):
                            for m in range(HC):
                                mm = pe.matmul(Y[t % 2][:, :], aT[h][x0][:, m, (t % TPH) * P:(t % TPH + 1) * P], w2[x1][:, m, :],
                                               start=(n == 0 and m == 0), stop=(n == 2 and m == HC - 1))
                        mm.then_inc(s_y, 1)

                with pe.Fori(0, NE // 2) as i:
                    for s in range(2):
                        body(i, s)

            TR = banks[6:8]
            XS = [[hh[i][:, :, s * CAP:(s + 1) * CAP] for i in range(2)] for s in range(2)]

            def few_sync(sp):
                def store(e, s):
                    for r in range(CT):
                        sp.wait_ge(s_yd, CT * (e + 1) + r + 1)
                        k = (CT * s + r) % 2
                        row = e * CAP + r * P
                        dst = y_rows[row:row + P, :] if isinstance(e, int) else y_rows[bass.ds(row, P), :]
                        sp.dma_start(dst, hslot[:, k * D:(k + 1) * D]).then_inc(s_st[k], 16)

                def body(i, s, first, last):
                    e = i * 2 + s
                    for k, kind in enumerate(("w2", "w1", "w3")):
                        if not (last and k):
                            sp.wait_ge(s_lo, 3 * e + k + 1)
                            load(sp, 3 * s + k, e + (1 if k else 0), kind)
                        if k == 1 and not first:
                            store(e - 1, 1 - s)

                sp.dma_start(count_up[:, :], a["c_count_up"].partition_broadcast(P)).then_inc(s_up, 16)
                load(sp, 0, 0, "w1")
                load(sp, 1, 0, "w3")
                body(0, 0, True, False)
                body(0, 1, False, False)
                with sp.Fori(1, NE // 2 - 1) as i:
                    for s in range(2):
                        body(i, s, False, False)
                body(NE // 2 - 1, 0, False, False)
                body(NE // 2 - 1, 1, False, True)
                store(NE - 1, 1)

            def few_scalar(act):
                high(act, w1[0][0], 16, 0)
                high(act, w3[0][0], 16, 1)

                def tokens(e, s):
                    for c in range(KC):
                        act.wait_ge(s_xt, KC * e + c + 1)
                        act.activation(XS[s][0][:, c, :], TR[c % 2][:, 0:CAP], ACT.Copy).then_inc(s_xh, 1)

                tokens(0, 0)

                def body(i, s, last):
                    e = i * 2 + s

                    def part_high(m):
                        act.wait_ge(s_a, HC * (e + 1) + m + 1)
                        act.activation(aT0[0][:, m, 0:CAP], act32[m % 2][:, 0:CAP], ACT.Copy).then_inc(s_ah, 1)

                    act.wait_ge(s_y, CT * (e + 1))
                    high(act, w2[0], 16 * (3 * i + (1 if s == 0 else 3)) + (0 if s else 16), s)
                    for m in range(HC):
                        act.wait_ge(s_gu, HC * (e + 1) + m + 1)
                        act.activation(silu[m % 2][:, 0:CAP], GU[m % 2][:, 0:CAP], ACT.Silu).then_inc(s_sg, 1)
                        if m >= 1:
                            part_high(m - 1)
                        if not last and m in (1, 2):
                            n = 3 * s + m
                            high(act, (w1 if m == 1 else w3)[1 - s][0], 16 * (3 * i + 1 + n // 2 + 1), n % 2)
                    part_high(HC - 1)
                    tokens(e + 1, 1 - s)

                with act.Fori(0, NE // 2 - 1) as i:
                    for s in range(2):
                        body(i, s, False)
                body(NE // 2 - 1, 0, False)
                body(NE // 2 - 1, 1, True)

            def few_gpsimd(pool):
                pool.wait_ge(s_hrow[0], 16 * NT // 2)
                pool.wait_ge(s_hrow[1], 16 * NT // 2)

                def gather(e, s):
                    pool.wait_ge(s_id, 2 * e + 2)
                    if not (isinstance(e, int) and e == 0):
                        pool.wait_ge(s_xt, KC * e)
                    pool.tensor_tensor(carry[:, s:s + 1], eps[:, 0:1], eps[:, 0:1], ALU.mult)
                    for r in range(CT):
                        pool.indirect_dma_start(rows[:, r, :], None, h_rows,
                                                bass.IndirectOffsetOnAxis(ap=ids[s][:, r:r + 1], axis=0)).then_inc(s_got, 16)

                gather(0, 0)
                low(pool, w1[0], 1, 0)
                low(pool, w3[0], 2, 1)

                def body(i, s, last):
                    e = i * 2 + s
                    gather(e + 1, 1 - s)
                    low(pool, w2, 3 * e + 3, s)
                    if not last:
                        low(pool, w1[1 - s], 3 * e + 4, (3 * s + 1) % 2)
                        low(pool, w3[1 - s], 3 * e + 5, (3 * s + 2) % 2)

                with pool.Fori(0, NE // 2 - 1) as i:
                    for s in range(2):
                        body(i, s, False)
                body(NE // 2 - 1, 0, False)
                body(NE // 2 - 1, 1, True)
                for k in range(2):
                    pool.wait_ge(s_st[k], 16 * (NE * CT // 2 + 1))
                pool.wait_ge(s_lo, 3 * NE)
                for t in range(NT):
                    if t >= 2:
                        pool.wait_ge(s_add, TOPK * (t - 1))
                    for k in range(TOPK):
                        pool.indirect_dma_start(raw[t % 2][:, k, :], None, y_rows,
                                                bass.IndirectOffsetOnAxis(ap=where[:, k, t:t + 1], axis=0)).then_inc(s_back[t % 2], 16)

            def few_vector(dve):
                dve.memset(scrap[:, 44:45], 0.0).then_inc(s_a, HC)
                dve.memset(scrap[:, 45:46], 0.0).then_inc(s_yd, CT)
                dve.memset(scrap[:, 46:47], 0.0).then_inc(s_al, 2)
                dve.memset(scrap[:, 47:48], 0.0).then_inc(s_st[0], 16)
                dve.memset(scrap[:, 48:49], 0.0).then_inc(s_st[1], 16)
                flat = place[:, :, :].rearrange("p e t -> p (e t)")

                def mark(e):
                    if not (isinstance(e, int) and e == 0):
                        dve.wait_ge(s_list, e)
                    for t in range(NT):
                        col = flat[:, t + e * NT:t + e * NT + 1] if isinstance(e, int) else flat[:, bass.ds(e * NT + t, 1)]
                        dve.tensor_scalar(mine[:, t, :], count_up[:, :], col, None, ALU.is_equal).then_inc(s_mine, 1)

                def listed(e, s):
                    dve.wait_ge(s_list, e + 1)
                    lists = Y[0][:, 0:2 * CT].rearrange("p (r k) -> p r k", k=2)
                    dve.tensor_reduce(ids32[:, :], lists, AX.X, ALU.add).then_inc(s_id, 1)
                    dve.wait_ge(s_id, 2 * e + 1)
                    dve.tensor_copy(ids[s][:, :], ids32[:, :]).then_inc(s_id, 1)

                def tokens(e, s):
                    for c in range(KC):
                        dve.wait_ge(s_xh, KC * e + c + 1)
                        dve.tensor_tensor(XS[s][1][:, c, :], TR[c % 2][:, 0:CAP], XS[s][0][:, c, :].bitcast(F32),
                                          ALU.subtract).then_inc(s_xl, 1)

                dve.wait_ge(s_up, 16)
                mark(0)
                listed(0, 0)
                mark(1)
                listed(1, 1)
                tokens(0, 0)

                def body(i, s):
                    e = i * 2 + s

                    def part_low(m):
                        dve.wait_ge(s_ah, HC * e + m + 1)
                        dve.tensor_tensor(aT0[1][:, m, 0:CAP], act32[m % 2][:, 0:CAP], aT0[0][:, m, 0:CAP].bitcast(F32),
                                          ALU.subtract).then_inc(s_al, 1)

                    mark(e + 2)
                    for m in range(HC):
                        dve.wait_ge(s_al, HC * e + m + 1)
                        dve.wait_ge(s_sg, HC * e + m + 1)
                        dve.tensor_tensor(act32[m % 2][:, 0:CAP], silu[m % 2][:, 0:CAP], GU[m % 2][:, BANK:BANK + CAP],
                                          ALU.mult).then_inc(s_a, 1)
                        if m >= 1:
                            part_low(m - 1)
                    part_low(HC - 1)
                    listed(e + 2, s)
                    tokens(e + 1, 1 - s)
                    for r in range(CT):
                        k = (CT * s + r) % 2
                        dve.wait_ge(s_y, CT * (e + 1) + r + 1)
                        dve.wait_ge(s_st[k], (CT * 16) * i + 16 * ((CT * s + r) // 2 + (0 if k == (CT * s + r) % 2 else 1)) + 16)
                        dve.tensor_copy(hslot[:, k * D:(k + 1) * D], Y[(r + 1) % 2][:, :]).then_inc(s_yd, 1)

                with dve.Fori(0, NE // 2) as i:
                    for s in range(2):
                        body(i, s)
                for t in range(NT):
                    dve.wait_ge(s_back[t % 2], 16 * TOPK * (t // 2 + 1))
                    for k in range(TOPK):
                        yt = y3[:, t, :]
                        dve.scalar_tensor_tensor(yt, raw[t % 2][:, k, :], share[:, k, t:t + 1], yt, ALU.mult, ALU.add).then_inc(s_add, 1)
                        dve.wait_ge(s_add, TOPK * t + k + 1)
                dve.memset(scrap[:, 49:50], 0.0).then_inc(s_done, 1)

            def few_tensor(pe):
                pe.transpose(banks[6][:, 0:P], ident[:, :], ident[:, :]).then_inc(s_gu, HC)
                pe.transpose(banks[6][:, 0:P], ident[:, :], ident[:, :]).then_inc(s_y, CT)

                def order(e):
                    pe.wait_ge(s_mine, NT * (e + 1))
                    for r in range(CT):
                        for t in range(NT):
                            mm = pe.matmul(Y[0][:, 2 * r:2 * r + 2], mine[:, t, r * P:(r + 1) * P], token[:, t, :],
                                           start=(t == 0), stop=(t == NT - 1))
                    mm.then_inc(s_list, 1)

                def turn(e):
                    pe.wait_ge(s_got, 16 * CT * (e + 1))
                    for c in range(KC):
                        if not (isinstance(e, int) and e == 0 and c < 2):
                            pe.wait_ge(s_xl, KC * e + c - 1)
                        for r in range(CT):
                            mm = pe.transpose(TR[c % 2][:, r * P:(r + 1) * P], rows[:, r, c * P:(c + 1) * P], ident[:, :])
                        mm.then_inc(s_xt, 1)

                order(0)
                pe.wait_ge(s_id, 1)
                order(1)
                turn(0)

                def body(i, s):
                    e = i * 2 + s
                    pe.wait_ge(s_lo, 3 * e + 2)
                    pe.wait_ge(s_xl, KC * (e + 1))
                    for m in range(HC):
                        pe.wait_ge(s_a, HC * (e + 1) + m - 1)
                        for j, w in enumerate((w1[s], w3[s])):
                            for n, (x0, x1) in enumerate(ACCURATE):
                                for c in range(KC):
                                    mm = pe.matmul(GU[m % 2][:, j * BANK:j * BANK + CAP], w[x0][:, c, m * P:(m + 1) * P],
                                                   XS[s][x1][:, c, :], start=(n == 0 and c == 0), stop=(n == 2 and c == KC - 1))
                        mm.then_inc(s_gu, 1)
                    pe.wait_ge(s_yd, CT * (e + 1) - 1)
                    order(e + 2)
                    turn(e + 1)
                    pe.wait_ge(s_lo, 3 * e + 3)
                    pe.wait_ge(s_al, HC * (e + 1) + 2)
                    for r in range(CT):
                        pe.wait_ge(s_yd, CT * (e + 1) + max(r - 1, 0))
                        if r == 1:
                            pe.wait_ge(s_id, 2 * e + 5)
                        for n, (x0, x1) in enumerate(ACCURATE):
                            for m in range(HC):
                                mm = pe.matmul(Y[(r + 1) % 2][:, :], aT0[x0][:, m, r * P:(r + 1) * P], w2[x1][:, m, :],
                                               start=(n == 0 and m == 0), stop=(n == 2 and m == HC - 1))
                        mm.then_inc(s_y, 1)

                with pe.Fori(0, NE // 2) as i:
                    for s in range(2):
                        body(i, s)

            def either(every, few):
                def stage(engine):
                    engine.wait_ge(s_gated, 1)
                    flag = engine.value_load(crowded[0:1, 0:1], min_val=0, max_val=1)
                    with engine.If(flag > 0):
                        every(engine)
                    with engine.Else():
                        few(engine)
                return stage

            programs["SP"].append(either(every_sync, few_sync))
            programs["ACT"].append(either(every_scalar, few_scalar))
            programs["POOL"].append(either(every_gpsimd, few_gpsimd))
            programs["DVE"].append(either(every_vector, few_vector))
            programs["PE"].append(either(every_tensor, few_tensor))
            return s_done, 1


        moe_done = experts()

        s_x1 = sem("s_x1")

        def add_inner(dve):
            dve.wait_ge(*moe_done)
            for t in range(NT):
                dve.scalar_tensor_tensor(x3[:, t, :], y3[:, t, :], tgate[:, 2:3], x3[:, t, :], ALU.mult, ALU.add).then_inc(s_x1, 1)

        programs["DVE"].append(add_inner)
        phase.close()
        phase = ExitStack()

        xT3 = sb("hT_x1", [P, KC * T])[:, :].rearrange("p (c t) -> p c t", c=KC)
        cxT3 = sb("ctxT1", [P, VC * B * S2])[:, :].rearrange("p (c t) -> p c t", c=VC)
        cslot1 = sb("cslot1", [P, 4 * DV])
        transpose_context(1, cxT3, cslot1, (s_x1, NT))
        layernorm(2, 1, (s_x1, NT), xT3)

        def cross_attention_1():
            HD, HPG, NG = 32, 4, 4
            DCA = 16
            GW = HPG * HD
            UN = B * HPG
            NK = S2 // P
            MAIN = S2 - DCA
            SCALE = 1.0 / float(np.sqrt(HD))
            HALF = S // 2
            LAG, RING = 3, 4
            STACK = 3 * HD
            PAIR = HPG // 2
            wq = sb("z_wq", [P, KC, GW])
            wkv = sb("z_wkv", [P, VC, HPG, 2 * HD])
            wd = sb("z_wd", [P, VC, 2, GW])
            wo = sb("z_wo", [P, PAIR, D])
            bq, bkv, bd = sb("z_bq", [P, GW]), sb("z_bkv", [P, HPG, 2 * HD]), sb("z_bd", [P, 2, GW])
            GM = (KC + 2 * VC + 3) * HPG
            wmean = sb("z_wmean", [P, GM])
            norms = sb("z_norms", [P, 6, HD])
            qnorm = sb("z_qnorm", [P, 2, HD])
            tbo = sb("z_tbo", [P, D])
            part = sb("z_part", [P, 2])
            RQ, RK = NT * HPG, NK * HPG
            RD = B * HPG
            var = sb("z_var", [P, RQ + RD + B * RK])
            dev = sb("z_dev", [P, RQ + RD + B * RK])
            rdev = sb("z_rdev", [P, RQ + RD + B * RK])
            qS = sb("z_qS", [STACK, HPG, T], F32R)
            kS = sb("z_kS", [STACK, HPG, B * S2], F32R)
            vS = sb("z_vS", [P, NC_T, PAIR, 6 * HD], F32R)
            oT = [sb(f"z_oT{b}", [P, PAIR, S]) for b in range(B)]
            most = sb("z_most", [P, RING, 2])
            total = sb("z_total", [P, RING, 2])
            rtotal = sb("z_rtotal", [P, RING, 2])
            carry = sb("z_carry", [P, RING])
            with ExitStack() as front:
                def fb(name, shape, dt=F32):
                    return front.enter_context(nc.sbuf_tensor(name, shape, dt))
                kv = fb("z_kv", [P, NC_T, HPG, 2 * HD])
                cq = fb("z_cq", [P, NT + B, GW])
                dv = fb("z_dv", [P, B, GW])
                dk = fb("z_dk", [P, B, GW])
                sq = fb("z_sq", [P, RQ + RD, HD])
                split = [fb(f"z_split{i}", [P, RK, 3, HD], F32R) for i in range(2)]
            with ExitStack() as back:
                p = [back.enter_context(nc.sbuf_tensor(f"z_p{i}", [P, S2], F32)) for i in range(RING)]
                pT = [back.enter_context(nc.sbuf_tensor(f"z_pT{i}", [P, NK, S], F32R)) for i in range(2)]

            plan = [(f"d{b}", "D") for b in range(B)] + [("q0", "D"), ("q1", "D")] + [(f"kv{n}", "D") for n in range(PAIRS)]
            plan += [(f"tq{h}{i}", "A") for h in range(HPG) for i in range(2)]
            plan += [(f"tk{b}{h}{i}", "A") for b in range(B) for h in range(HPG) for i in range(2)]
            for b in range(B):
                plan += [(f"o{b}{i}", "A") for i in range(PAIR)] + [(f"w{b}{t}", "D") for t in range(QT)]
            use = Use(plan)
            assert use.total % 2 == 0
            PJ, SC, TR = banks[0:2], pairs[1:3], banks[6:8]
            NS = UN * QT
            OUT = HPG * QT + LAG + 2
            assert LAG % 2
            s_c, s_qn, s_tbo, s_w, s_wo = sem("z_c"), sem("z_qn"), sem("z_tbo"), sem("z_w"), sem("z_wo")
            s_pj, s_pja, s_pjd, s_cw, s_ch, s_sq, s_dev, s_nrm, s_aff, s_hi, s_lo, s_sc, s_sm, s_ex, s_rt, s_pn, s_tr, s_th, s_tl = [
                sem(f"z_{n}") for n in ("pj", "pja", "pjd", "cw", "ch", "sq", "dev", "nrm", "aff", "hi", "lo", "sc", "sm", "ex",
                                        "rt", "pn", "tr", "th", "tl")]
            emptied = {"A": s_pja, "D": s_pjd}
            LOADS = 8
            STEPS = 16
            rows = [slice(0, RQ + RD)] + [slice(RQ + RD + b * RK, RQ + RD + (b + 1) * RK) for b in range(B)]

            def headrows(b):
                r = kv[:, b * NK:(b + 1) * NK, :, :].rearrange("p t h d -> p (t h) d")
                return r[:, :, 0:HD], r[:, :, HD:]

            cqrows = cq[:, :, :].rearrange("p t (h d) -> p (t h) d", d=HD)
            centred = [wq[:, :, :].rearrange("p c (h d) -> p (c h) d", d=HD),
                       wkv[:, :, :, :].rearrange("p c h d -> p (c h) d")[:, :, 0:HD],
                       wd[:, 0, 0, :].rearrange("p (h d) -> p h d", d=HD), wd[:, 1, 0, :].rearrange("p (h d) -> p h d", d=HD),
                       bq[:, :].rearrange("p (h d) -> p h d", d=HD), bkv[:, :, 0:HD],
                       bd[:, 0, :].rearrange("p (h d) -> p h d", d=HD)]
            assert VC == 2 and sum(w.shape[1] for w in centred) == GM
            NCW = 2 * len(centred) + 1

            def done(engine, j, name):
                e, count = use.emptied(use.index[name], j)
                engine.wait_ge(emptied[e], count)

            def sync(sp):
                sp.wait_ge(s_x1, NT)
                for k, name in enumerate(("qn_w", "qn_b", "kn_w", "kn_b", "kn_dca_w", "kn_dca_b")):
                    sp.dma_start(norms[:, k, :], a[f"L1_xattn_{name}"].partition_broadcast(P)).then_inc(s_c, 16)
                sp.dma_start(tbo[:, :], a["L1_xattn_bo"].partition_broadcast(P)).then_inc(s_c, 16)
                sp.dma_start(part[:, :], a["c_part"]).then_inc(s_c, 16)

                def load(j):
                    one = slice(0, GW) if isinstance(j, int) else bass.ds(j * GW, GW)
                    two = slice(0, 2 * GW) if isinstance(j, int) else bass.ds(j * 2 * GW, 2 * GW)
                    val = slice(D, D + GW) if isinstance(j, int) else bass.ds(j * GW + D, GW)
                    wd_d = a["L1_xattn_Wkv_dca"].rearrange("(c p) n -> p c n", p=P)
                    sp.dma_start(wq[:, :, :], a["L1_xattn_Wq"].rearrange("(c p) n -> p c n", p=P)[:, :, one]).then_inc(s_w, 16)
                    sp.dma_start(wkv[:, :, :, :].rearrange("p c h d -> p c (h d)"),
                                 a["wkv"].rearrange("(c p) n -> p c n", p=P)[:, :, two]).then_inc(s_w, 16)
                    sp.dma_start(wd[:, :, 0, :], wd_d[:, :, one]).then_inc(s_w, 16)
                    sp.dma_start(wd[:, :, 1, :], wd_d[:, :, val]).then_inc(s_w, 16)
                    sp.dma_start(bq[:, :], a["L1_xattn_bq"][one].partition_broadcast(P)).then_inc(s_w, 16)
                    sp.dma_start(bkv[:, :, :].rearrange("p h d -> p (h d)"), a["bkv"][two].partition_broadcast(P)).then_inc(s_w, 16)
                    sp.dma_start(bd[:, 0, :], a["L1_xattn_bkv_dca"][one].partition_broadcast(P)).then_inc(s_w, 16)
                    sp.dma_start(bd[:, 1, :], a["L1_xattn_bkv_dca"][val].partition_broadcast(P)).then_inc(s_w, 16)

                def load_out(j):
                    for i in range(PAIR):
                        for h in range(2):
                            first = (i * 2 + h) * HD
                            src = a["L1_xattn_Wo"][(slice(first, first + HD) if isinstance(j, int) else bass.ds(j * GW + first, HD)), :]
                            for n in range(2):
                                sp.dma_start(wo[(2 * h + n) * HD:(2 * h + n + 1) * HD, i, :], src).then_inc(s_wo, 16)

                load(0)
                load_out(0)
                with sp.Fori(0, NG - 1) as j:
                    sp.wait_ge(s_pjd, use.per["D"] * (j + 1) + use.nth[use.index[f"kv{PAIRS - 1}"]][1])
                    load(j + 1)
                    sp.wait_ge(s_pjd, use.per["D"] * (j + 2))
                    load_out(j + 1)
                sp.wait_ge(s_pjd, use.per["D"] * NG + use.nth[use.index[f"kv{PAIRS - 1}"]][1])
                load(0)

            def vector(dve):
                dve.wait_ge(s_c, 16 * 8)
                dve.tensor_scalar(qnorm[:, :, :], norms[:, 0:2, :], SCALE, None, ALU.mult).then_inc(s_qn, 1)
                dve.tensor_scalar(tbo[:, :], tbo[:, :], tgate[:, 1:2], None, ALU.mult).then_inc(s_tbo, 1)
                dve.memset(scrap[:, 28:29], 0.0).then_inc(s_pjd, use.per["D"])
                dve.memset(scrap[:, 29:30], 0.0).then_inc(s_tl, 2 * NS)
                dve.wait_ge(s_qn, 2)

                def centre(j):
                    dve.wait_ge(s_w, 16 * LOADS * (j + 1))
                    at = 0
                    for w in centred:
                        dve.tensor_reduce(wmean[:, at:at + w.shape[1]], w, AX.X, ALU.add).then_inc(s_cw, 1)
                        at += w.shape[1]
                    dve.wait_ge(s_cw, NCW * j + NCW // 2)
                    dve.tensor_scalar(wmean[:, :], wmean[:, :], 1.0 / HD, None, ALU.mult).then_inc(s_cw, 1)
                    dve.wait_ge(s_cw, NCW * j + NCW // 2 + 1)
                    at = 0
                    for w in centred:
                        dve.tensor_tensor(w, w, wmean[:, at:at + w.shape[1]].unsqueeze(2).to_broadcast(list(w.shape)),
                                          ALU.subtract).then_inc(s_cw, 1)
                        at += w.shape[1]
                    dve.wait_ge(s_cw, NCW * (j + 1))

                def body(j):
                    steps = 0

                    def step(ins):
                        nonlocal steps
                        steps += 1
                        ins.then_inc(s_ch, 1)
                        dve.wait_ge(s_ch, STEPS * j + steps)

                    def empty(name):
                        dve.wait_ge(s_pj, use.total * (j + 1) + use.index[name] + 1)
                        return PJ[use.index[name] % 2]

                    def keys_values(n):
                        o = empty(f"kv{n}")
                        dve.tensor_tensor(kv[:, 2 * n:2 * n + 2, :, :].rearrange("p t h d -> p t (h d)"),
                                          o[:, :].rearrange("p (t d) -> p t d", t=2),
                                          bkv[:, :, :].rearrange("p h d -> p (h d)").unsqueeze(1).to_broadcast([P, 2, 2 * GW]),
                                          ALU.add).then_inc(s_pjd, 1)

                    def spread(k):
                        g = rows[k]
                        dve.wait_ge(s_sq, 3 * j + k + 1)
                        step(dve.tensor_reduce(var[:, g], sq[:, 0:g.stop - g.start, :], AX.X, ALU.add))

                    def normalise(k, x):
                        g = rows[k]
                        dve.wait_ge(s_dev, 3 * j + k + 1)
                        step(dve.reciprocal(rdev[:, g], dev[:, g]))
                        return dve.tensor_tensor(x, x, rdev[:, g].unsqueeze(2).to_broadcast(list(x.shape)), ALU.mult)

                    def row(w, x):
                        return w.unsqueeze(1).to_broadcast(list(x.shape))

                    for b in range(B):
                        o = empty(f"d{b}")
                        dve.tensor_tensor(cq[:, NT + b, :], o[:, 0:GW], bd[:, 0, :], ALU.add)
                        dve.tensor_tensor(dv[:, b, :], o[:, GW:2 * GW], bd[:, 1, :], ALU.add).then_inc(s_pjd, 1)
                    for n in range(2):
                        o = empty(f"q{n}")
                        dve.tensor_tensor(cq[:, 4 * n:4 * n + 4, :], o[:, :].rearrange("p (t d) -> p t d", t=4),
                                          bq[:, :].unsqueeze(1).to_broadcast([P, 4, GW]), ALU.add).then_inc(s_pjd, 1)
                    q, d = cqrows[:, 0:RQ, :], cqrows[:, RQ:, :]
                    keys_values(0)
                    spread(0)
                    keys_values(1)
                    step(normalise(0, cqrows))
                    keys_values(2)
                    dve.tensor_tensor(q, q, row(qnorm[:, 0, :], q), ALU.mult)
                    step(dve.tensor_tensor(d, d, row(norms[:, 4, :], d), ALU.mult))
                    keys_values(3)
                    dve.tensor_tensor(q, q, row(qnorm[:, 1, :], q), ALU.add).then_inc(s_nrm, 1)
                    step(dve.tensor_tensor(d, d, row(norms[:, 5, :], d), ALU.add))
                    keys_values(4)
                    dve.tensor_scalar(dk[:, :, :], cq[:, NT:, :], part[:, 1:2], None, ALU.mult)
                    step(dve.tensor_scalar(dv[:, :, :], dv[:, :, :], part[:, 1:2], None, ALU.mult))
                    spread(1)
                    keys_values(5)
                    normalise(1, headrows(0)[0]).then_inc(s_nrm, 1)
                    keys_values(6)
                    dve.wait_ge(s_hi, 5 * j + 1)
                    dve.tensor_tensor(split[0][:, :, 1, :], q, split[0][:, :, 0, :].bitcast(F32), ALU.subtract).then_inc(s_lo, 1)
                    keys_values(7)
                    done(dve, j, f"kv{PAIRS - 1}")
                    for b in range(B):
                        vt = kv[:, (b + 1) * NK - 1, :, HD:]
                        ins = dve.scalar_tensor_tensor(vt, vt, part[:, 0:1], dv[:, b, :].rearrange("p (h d) -> p h d", d=HD),
                                                       ALU.mult, ALU.add)
                    step(ins)

                    def last_keys(b):
                        kt = kv[:, (b + 1) * NK - 1, :, 0:HD]
                        return dve.scalar_tensor_tensor(kt, kt, part[:, 0:1], dk[:, b, :].rearrange("p (h d) -> p h d", d=HD),
                                                        ALU.mult, ALU.add)

                    def low_keys(b):
                        part_k = split[(1 + b) % 2]
                        dve.wait_ge(s_hi, 5 * j + 2 * b + 2)
                        dve.tensor_tensor(part_k[:, :, 2, :], headrows(b)[0], part_k[:, :, 0, :].bitcast(F32),
                                          ALU.subtract).then_inc(s_lo, 1)

                    def low_values(b):
                        dve.wait_ge(s_hi, 5 * j + 2 * b + 3)
                        v_hi, v_lo, v = values_of(b)
                        dve.tensor_tensor(v_lo, v, v_hi.bitcast(F32), ALU.subtract).then_inc(s_lo, 1)

                    dve.wait_ge(s_aff, 2 * (j + 1))
                    step(last_keys(0))
                    spread(2)
                    low_keys(0)
                    k = headrows(1)[0]
                    step(normalise(2, k))
                    low_values(0)
                    step(dve.tensor_tensor(k, k, row(norms[:, 2, :], k), ALU.mult))
                    step(dve.tensor_tensor(k, k, row(norms[:, 3, :], k), ALU.add))
                    step(last_keys(1))
                    low_keys(1)
                    low_values(1)
                    assert steps == STEPS, steps

                    def reciprocal(n):
                        dve.wait_ge(s_ex, 2 * (NS * (j + 1) + n + 1))
                        dve.reciprocal(rtotal[:, n % RING, :], total[:, n % RING, :]).then_inc(s_rt, 1)

                    def low(n):
                        u, q = n // QT, n % QT
                        for i in range(2):
                            dve.wait_ge(s_th, 2 * (NS * j + n) + i + 1)
                            k = slice(i * NK // 2, (i + 1) * NK // 2)
                            cols = slice(q * P, (q + 1) * P)
                            dve.tensor_tensor(pT[1][:, k, cols], TR[i][:, :].rearrange("p (k n) -> p k n", n=P),
                                              pT[0][:, k, cols].bitcast(F32), ALU.subtract).then_inc(s_tl, 1)

                    def add_out(b, t):
                        o = empty(f"w{b}{t}")
                        xt = x3[:, b * QT + t, :]
                        dve.scalar_tensor_tensor(xt, o[:, :], tgate[:, 1:2], xt, ALU.mult, ALU.add).then_inc(s_pjd, 1)

                    for n in range(NS):
                        w = n % RING
                        dve.wait_ge(s_sc, NS * j + n + 1)
                        dve.tensor_reduce(most[:, w, 0:1], SC[n % 2][:, 0:MAIN], AX.X, ALU.max, negate=True)
                        dve.tensor_reduce(most[:, w, 1:2], SC[n % 2][:, MAIN:], AX.X, ALU.max, negate=True).then_inc(s_sm, 1)
                        if n >= 1:
                            reciprocal(n - 1)
                        if n >= LAG:
                            low(n - LAG)
                        if OUT <= n <= OUT + 1:
                            for t in (2 * (n - OUT), 2 * (n - OUT) + 1):
                                add_out(0, t)
                    reciprocal(NS - 1)
                    for n in range(NS - LAG, NS):
                        low(n)
                    centre(j + 1)
                    for t in range(QT):
                        add_out(1, t)

                centre(0)
                with dve.Fori(0, NG) as j:
                    body(j)
                dve.wait_ge(s_pjd, use.per["D"] * (NG + 1))
                for t in range(NT):
                    dve.tensor_tensor(x3[:, t, :], x3[:, t, :], tbo[:, :], ALU.add).then_inc(s_tbo, 1)

            def values_of(b):
                t = vS[:, b * NK:(b + 1) * NK, :, :].rearrange("p t i (k d) -> p (t i) k d", d=HD)
                v = kv[:, b * NK:(b + 1) * NK, :, HD:].rearrange("p t (i h) d -> p (t i) h d", h=2)
                return t[:, :, 0:5:4, :], t[:, :, 1:6:4, :], v

            def scalar(act):
                act.wait_ge(s_qn, 1)
                flat = vS[:, :, :, :].rearrange("p t i d -> p (t i d)")
                act.activation(flat, scrap[:, 63:64].to_broadcast(list(flat.shape)), ACT.Copy).then_inc(s_qn, 1)
                act.wait_ge(s_qn, 2)
                act.activation(scrap[:, 32:33], eps[:, 0:1], ACT.Copy).then_inc(s_pja, use.per["A"])
                act.activation(scrap[:, 34:35], eps[:, 0:1], ACT.Copy).then_inc(s_ex, 2 * NS)

                def body(j):
                    def filled(name):
                        act.wait_ge(s_pj, use.total * (j + 1) + use.index[name] + 1)
                        return PJ[use.index[name] % 2]

                    def square(k, x, name):
                        done(act, j, name)
                        act.activation(sq[:, 0:x.shape[1], :], x, ACT.Square).then_inc(s_sq, 1)

                    def root(k, steps):
                        act.wait_ge(s_ch, STEPS * j + steps)
                        act.activation(dev[:, rows[k]], var[:, rows[k]], ACT.Sqrt, scale=1.0 / HD, bias=eps[:, 1:2]).then_inc(s_dev, 1)

                    def stacked(b, h, i):
                        first = b * S2 + i * BANK
                        act.activation(kS[:, h, first:first + BANK], filled(f"tk{b}{h}{i}")[0:STACK, :].bitcast(F32R),
                                       ACT.Copy).then_inc(s_pja, 1)

                    def high_keys_values(b):
                        act.activation(split[(1 + b) % 2][:, :, 0:2, :], headrows(b)[0].unsqueeze(2).to_broadcast([P, RK, 2, HD]),
                                       ACT.Copy).then_inc(s_hi, 1)
                        v_hi, _, v = values_of(b)
                        act.activation(v_hi, v, ACT.Copy).then_inc(s_hi, 1)

                    square(0, cqrows, "q1")
                    root(0, 1)
                    square(1, headrows(0)[0], f"kv{PAIRS // 2 - 1}")
                    act.wait_ge(s_nrm, 2 * j + 1)
                    act.activation(split[0][:, :, 0:3:2, :], cqrows[:, 0:RQ, :].unsqueeze(2).to_broadcast([P, RQ, 2, HD]),
                                   ACT.Copy).then_inc(s_hi, 1)
                    root(1, 7)
                    square(2, headrows(1)[0], f"kv{PAIRS - 1}")
                    act.wait_ge(s_ch, STEPS * j + 10)
                    high_keys_values(0)
                    root(2, 11)
                    for h in range(HPG):
                        for i in range(2):
                            act.activation(qS[:, h, i * BANK:(i + 1) * BANK], filled(f"tq{h}{i}")[0:STACK, :].bitcast(F32R),
                                           ACT.Copy).then_inc(s_pja, 1)
                    for h in range(HPG):
                        for i in range(2):
                            stacked(0, h, i)
                    act.wait_ge(s_ch, STEPS * j + 16)
                    high_keys_values(1)

                    def high(n):
                        q = n % QT
                        for i in range(2):
                            act.wait_ge(s_tr, 2 * (NS * j + n) + i + 1)
                            act.activation(pT[0][:, i * NK // 2:(i + 1) * NK // 2, q * P:(q + 1) * P],
                                           TR[i][:, :].rearrange("p (k n) -> p k n", n=P), ACT.Copy).then_inc(s_th, 1)

                    def outputs(b, i):
                        act.activation(oT[b][:, i, :], filled(f"o{b}{i}")[:, :], ACT.Copy).then_inc(s_pja, 1)

                    for n in range(NS):
                        u, q = n // QT, n % QT
                        w = n % RING
                        if n >= LAG:
                            high(n - LAG)
                        act.wait_ge(s_sm, NS * j + n + 1)
                        for k, cols in enumerate((slice(0, MAIN), slice(MAIN, S2))):
                            act.activation(p[w][:, cols], SC[n % 2][:, cols], ACT.Exp,
                                           bias=most[:, w, k:k + 1], accum_out=total[:, w, k:k + 1]).then_inc(s_ex, 1)
                        if n < HPG:
                            for i in range(2):
                                stacked(1, n, i)
                        i = (n - LAG - 1) // (2 * QT) - 1
                        if i >= 0 and (n - LAG - 1) % (2 * QT) == 0:
                            outputs(i // PAIR, i % PAIR)
                    for n in range(NS - LAG, NS):
                        high(n)
                    outputs(B - 1, PAIR - 1)

                with act.Fori(0, NG) as j:
                    body(j)

            def gpsimd(pool):
                pool.wait_ge(s_c, 16 * 8)
                with pool.Fori(0, NG) as j:
                    k = headrows(0)[0]
                    pool.wait_ge(s_nrm, 2 * (j + 1))
                    pool.tensor_tensor(k, k, norms[:, 2, :].unsqueeze(1).to_broadcast(list(k.shape)), ALU.mult).then_inc(s_aff, 1)
                    pool.wait_ge(s_aff, 2 * j + 1)
                    pool.tensor_tensor(k, k, norms[:, 3, :].unsqueeze(1).to_broadcast(list(k.shape)), ALU.add).then_inc(s_aff, 1)
                    for n in range(NS):
                        w = n % RING
                        pool.wait_ge(s_rt, NS * j + n + 1)
                        pool.tensor_tensor(carry[:, w:w + 1], rtotal[:, w, 0:1], rtotal[:, w, 0:1], ALU.mult)
                        for k, cols in enumerate((slice(0, MAIN), slice(MAIN, S2))):
                            pool.tensor_scalar(p[w][:, cols], p[w][:, cols], rtotal[:, w, k:k + 1], 1.0,
                                               ALU.mult, ALU.mult).then_inc(s_pn, 1)

            def tensor(pe):
                pe.wait_ge(s_lnev, 2 * NT)
                pe.wait_ge(s_ctxev, 2 * PAIRS)
                pe.transpose(PJ[0][:, 0:P], ident[:, :], ident[:, :]).then_inc(s_pj, use.total)
                pe.wait_ge(s_idr, 1)

                def body(j):
                    def bank(name):
                        n = use.index[name]
                        e, count = use.emptied(n - 2, j) if n >= 2 else use.emptied(use.total + n - 2, j - 1)
                        pe.wait_ge(emptied[e], count)
                        return PJ[n % 2]

                    pe.wait_ge(s_cw, NCW * (j + 1))
                    for b in range(B):
                        o = bank(f"d{b}")
                        for c in range(VC):
                            mm = pe.matmul(o[:, 0:2 * GW], cxT3[:, c, (b + 1) * S2 - P:(b + 1) * S2],
                                           wd[:, c, :, :].rearrange("p k d -> p (k d)"), start=(c == 0), stop=(c == VC - 1))
                        mm.then_inc(s_pj, 1)
                    for n in range(2):
                        o = bank(f"q{n}")
                        for i in range(4):
                            for c in range(KC):
                                mm = pe.matmul(o[:, i * GW:(i + 1) * GW], xT3[:, c, (4 * n + i) * P:(4 * n + i + 1) * P], wq[:, c, :],
                                               start=(c == 0), stop=(c == KC - 1))
                        mm.then_inc(s_pj, 1)
                    for n in range(PAIRS):
                        o = bank(f"kv{n}")
                        for i in range(2):
                            for c in range(VC):
                                mm = pe.matmul(o[:, i * 2 * GW:(i + 1) * 2 * GW], cxT3[:, c, (2 * n + i) * P:(2 * n + i + 1) * P],
                                               wkv[:, c, :, :].rearrange("p h d -> p (h d)"), start=(c == 0), stop=(c == VC - 1))
                        mm.then_inc(s_pj, 1)

                    def stack(name, parts, row0):
                        o = bank(name)
                        for i in range(4):
                            mm = pe.transpose(o[0:STACK, i * P:(i + 1) * P].bitcast(F32R),
                                              parts[:, row0 + i * HPG, :, :].rearrange("p k d -> p (k d)"), identr[:, :])
                        mm.then_inc(s_pj, 1)

                    pe.wait_ge(s_lo, 5 * j + 1)
                    for h in range(HPG):
                        for i in range(2):
                            stack(f"tq{h}{i}", split[0], i * 4 * HPG + h)
                    pe.wait_ge(s_lo, 5 * j + 2)
                    for h in range(HPG):
                        for i in range(2):
                            stack(f"tk0{h}{i}", split[1], i * 4 * HPG + h)
                    done(pe, j, f"tk0{HPG - 1}1")
                    pe.wait_ge(s_wo, 16 * 8 * (j + 1))

                    def transposes(n):
                        pe.wait_ge(s_pn, 2 * (NS * j + n + 1))
                        for i in range(2):
                            pe.wait_ge(s_tl, 2 * (NS * (j + 1) + n - 1) + i + 1)
                            for k in range(NK // 2):
                                kk = i * NK // 2 + k
                                mm = pe.transpose(TR[i][:, k * P:(k + 1) * P], p[n % RING][:, kk * P:(kk + 1) * P], ident[:, :])
                            mm.then_inc(s_tr, 1)

                    def values(m):
                        u, half = m // 2, m % 2
                        b, h = u // HPG, u % HPG
                        cols = slice(half * HALF, (half + 1) * HALF)
                        name = f"o{b}{h // 2}"
                        o = bank(name) if h % 2 == 0 and half == 0 else PJ[use.index[name] % 2]
                        if half == 0 and u % HPG == 0:
                            pe.wait_ge(s_lo, 5 * j + 2 * b + 3)
                        pe.wait_ge(s_tl, 2 * (NS * (j + 1) + 2 * (m + 1)))
                        for k in range(NK):
                            v = vS[:, b * NK + k, h // 2, (h % 2) * 2 * HD:(h % 2) * 2 * HD + P]
                            for i in range(2):
                                mm = pe.matmul(o[:, cols], v, pT[i][:, k, cols], start=(h % 2 == 0 and half == 0 and k == 0 and i == 0),
                                               stop=(h % 2 == 1 and half == 1 and k == NK - 1 and i == 1))
                        if h % 2 and half:
                            mm.then_inc(s_pj, 1)

                    def project(b, t):
                        o = bank(f"w{b}{t}")
                        if t == 0:
                            done(pe, j, f"o{b}{PAIR - 1}")
                        for i in range(PAIR):
                            mm = pe.matmul(o[:, :], oT[b][:, i, t * P:(t + 1) * P], wo[:, i, :], start=(i == 0), stop=(i == PAIR - 1))
                        mm.then_inc(s_pj, 1)

                    for n in range(NS):
                        u, q = n // QT, n % QT
                        b, h = u // HPG, u % HPG
                        if n == HPG * QT:
                            done(pe, j, f"tk1{HPG - 1}1")
                        pe.wait_ge(s_ex, 2 * (NS * (j + 1) + n - 1))
                        for i in range(2):
                            mm = pe.matmul(SC[n % 2][:, i * BANK:(i + 1) * BANK], qS[:, h, b * S + q * P:b * S + (q + 1) * P],
                                           kS[:, h, b * S2 + i * BANK:b * S2 + (i + 1) * BANK], start=True, stop=True)
                        mm.then_inc(s_sc, 1)
                        if n == 0:
                            pe.wait_ge(s_lo, 5 * j + 4)
                        if n < HPG:
                            for i in range(2):
                                stack(f"tk1{n}{i}", split[0], i * 4 * HPG + n)
                        if n >= LAG:
                            transposes(n - LAG)
                        if OUT <= n <= OUT + 1:
                            for t in (2 * (n - OUT), 2 * (n - OUT) + 1):
                                project(0, t)
                        m = (n - LAG - 2) // 2
                        if n == OUT + 1:
                            values(m)
                        elif m >= 0 and (n - LAG) % 2 == 0 and n != OUT:
                            values(m)
                    for n in range(NS - LAG, NS):
                        transposes(n)
                        if n % 2 and n < NS - 1:
                            values(n // 2)
                    values(NS // 2 - 1)
                    for t in range(QT):
                        project(B - 1, t)

                with pe.Fori(0, NG) as j:
                    body(j)

            programs["SP"].append(sync)
            programs["DVE"].append(vector)
            programs["ACT"].append(scalar)
            programs["POOL"].append(gpsimd)
            programs["PE"].append(tensor)
            return s_tbo, NT + 1

        x2_done = cross_attention_1()
        phase.close()
        phase = ExitStack()

        statistics(3, x2_done)

        def bit_ffn():
            HID = 2048
            HC = HID // P
            HB = HID // BANK
            LEAST = 1e-5
            MAGIC = 1.5 * 2.0 ** 23
            TOP, BOTTOM = 127.0, -128.0
            GROUPS = 8
            raw = [sb("f_raw1", [P, HC, D]), sb("f_raw2", [P, KC, HID])]
            wq = [sb("f_wq1", [P, HC, D], BF16), sb("f_wq2", [P, KC, HID], BF16)]
            w1T, w2T = sb("f_w1T", [P, KC, HID], BF16), sb("f_w2T", [P, HC, D], BF16)
            identb, ones = sb("f_identb", [P, P], BF16), sb("f_ones", [P, P])
            size, wmean, winv = sb("f_size", [P, 2]), sb("f_wmean", [P, 2]), sb("f_winv", [P, 2])
            b1, b2 = sb("f_b1", [P, HID]), sb("f_b2", [P, D])
            h = [sb(f"f_h{s}", [P, D]) for s in range(2)]
            hq = [sb(f"f_hq{s}", [P, D], BF16) for s in range(2)]
            hqT = [sb(f"f_hqT{s}", [P, KC, P], BF16) for s in range(2)]
            z = [sb(f"f_z{s}", [P, HID]) for s in range(2)]
            zq = [sb(f"f_zq{s}", [P, HID], BF16) for s in range(2)]
            zqT = [sb(f"f_zqT{s}", [P, HC, P], BF16) for s in range(2)]
            o = [sb(f"f_o{s}", [P, D]) for s in range(2)]
            most = sb("f_most", [P, 4])
            scale = sb("f_scale", [P, 4])
            unscale = sb("f_unscale", [P, 4])
            HID_B, OUT_B = [banks[k] for k in range(HB)], banks[4:6]
            TRB = [pairs[3][:, i * BANK:(i + 1) * BANK].bitcast(BF16) for i in range(2)]
            WTB = [pairs[2 + i // 2][:, (i % 2) * BANK:(i % 2 + 1) * BANK].bitcast(BF16) for i in range(4)]

            s_w = [sem("f_w1"), sem("f_w2")]
            s_b, s_id, s_one = [sem(f"f_{n}") for n in ("b", "id", "one")]
            s_size, s_sum, s_mean, s_wc, s_wr, s_wq, s_wt, s_wa, s_wd = [
                sem(f"f_{n}") for n in ("size", "sum", "mean", "wc", "wr", "wq", "wt", "wa", "wd")]
            s_ch, s_r, s_q, s_tr, s_te, s_m1, s_z, s_g, s_m2, s_o, s_x2 = [
                sem(f"f_{n}") for n in ("ch", "r", "q", "tr", "te", "m1", "z", "g", "m2", "o", "x2")]
            CH = 4
            STEPS = 26
            TURNS = 6

            def chunk(t3, k):
                n = t3.shape[1] // CH
                return t3[:, k * n:(k + 1) * n, :]

            def sync(sp):
                sp.wait_ge(*x2_done)
                sp.dma_start(raw[0][:, :, :], a["L1_ffn_w1"].rearrange("(t p) d -> p t d", p=P)).then_inc(s_w[0], 16)
                sp.dma_start(raw[1][:, :, :], a["L1_ffn_w2"].rearrange("(t p) d -> p t d", p=P)).then_inc(s_w[1], 16)
                sp.dma_start(b1[:, :], a["L1_ffn_b1"].partition_broadcast(P)).then_inc(s_b, 16)
                sp.dma_start(b2[:, :], a["L1_ffn_b2"].partition_broadcast(P)).then_inc(s_b, 16)
                out3 = out.rearrange("b (t p) d -> p (b t) d", p=P)
                with sp.Fori(0, NT // 2) as i:
                    sp.wait_ge(s_x2, 2 * (i + 1))
                    sp.dma_start(out3[:, bass.ds(i * 2, 2), :], x3[:, bass.ds(i * 2, 2), :]).then_inc(s_out, 16)
                sp.wait_ge(s_out, 16 * (NT // 2))

            def vector(dve):
                dve.wait_ge(*x2_done)
                dve.memset(ones[:, :], 1.0).then_inc(s_one, 1)
                dve.memset(scrap[:, 36:37], 0.0).then_inc(s_z, HB)
                dve.memset(scrap[:, 37:38], 0.0).then_inc(s_o, 2)
                dve.wait_ge(s_sum, 1)
                dve.tensor_scalar(wmean[:, :], HID_B[0][:, 0:2], 1.0 / (HID * D), LEAST, ALU.mult, ALU.max).then_inc(s_mean, 1)
                dve.wait_ge(s_mean, 1)
                dve.reciprocal(winv[:, :], wmean[:, :]).then_inc(s_mean, 1)
                dve.wait_ge(s_mean, 2)
                for w in range(2):
                    for k in range(CH):
                        c = chunk(raw[w], k)
                        dve.tensor_scalar(c, c, winv[:, w:w + 1], 1.0, ALU.mult, ALU.min).then_inc(s_wc, 1)
                        dve.wait_ge(s_wc, w * CH + k + 1)
                        dve.tensor_scalar(c, c, -1.0, MAGIC, ALU.max, ALU.add).then_inc(s_wr, 1)
                for g in range(1, 2 * GROUPS, 2):
                    dve.wait_ge(s_wt, g + 1)
                    turned(dve, g)
                dve.wait_ge(s_rstd, 4)
                dve.wait_ge(s_b, 32)

                def body(i):
                    steps = 0

                    def step(ins):
                        nonlocal steps
                        steps += 1
                        ins.then_inc(s_ch, 1)
                        dve.wait_ge(s_ch, STEPS * i + steps)

                    def quantise(src, n, w):
                        m, q = most[:, n:n + 1], scale[:, n:n + 1]
                        step(dve.tensor_scalar(m, m, LEAST, None, ALU.max))
                        step(dve.reciprocal(q, m))
                        step(dve.tensor_scalar(q, q, TOP, None, ALU.mult))
                        step(dve.tensor_scalar(unscale[:, n:n + 1], m, 1.0 / TOP, wmean[:, w:w + 1], ALU.mult, ALU.mult))
                        step(dve.tensor_scalar(src, src, q, MAGIC, ALU.mult, ALU.add))
                        dve.tensor_scalar(src, src, MAGIC + TOP, MAGIC + BOTTOM, ALU.min, ALU.max).then_inc(s_r, 1)

                    for s in range(2):
                        t = i * 2 + s
                        step(dve.tensor_scalar(h[s][:, :], x3[:, bass.ds(t, 1), :].rearrange("p t d -> p (t d)"),
                                               mv[:, bass.ds(t * 2, 1)], rstd[:, bass.ds(t, 1)], ALU.subtract, ALU.mult))
                        step(dve.tensor_reduce(most[:, s:s + 1], h[s][:, :], AX.X, ALU.max, apply_absolute_value=True))
                        quantise(h[s][:, :], s, 0)
                    for s in range(2):
                        for k in range(HB):
                            dve.wait_ge(s_m1, 2 * HB * i + HB * s + k + 1)
                            cols = slice(k * BANK, (k + 1) * BANK)
                            dve.scalar_tensor_tensor(z[s][:, cols], HID_B[k][:, :], unscale[:, s:s + 1], b1[:, cols],
                                                     ALU.mult, ALU.add).then_inc(s_z, 1)
                    for s in range(2):
                        dve.wait_ge(s_g, 2 * i + s + 1)
                        step(dve.tensor_reduce(most[:, 2 + s:3 + s], z[s][:, :], AX.X, ALU.max, apply_absolute_value=True))
                        quantise(z[s][:, :], 2 + s, 1)
                    for s in range(2):
                        dve.wait_ge(s_m2, 2 * i + s + 1)
                        dve.scalar_tensor_tensor(o[s][:, :], OUT_B[s][:, :], unscale[:, 2 + s:3 + s], b2[:, :],
                                                 ALU.mult, ALU.add).then_inc(s_o, 1)
                        dve.wait_ge(s_o, 2 * i + s + 3)
                        xt = x3[:, bass.ds(i * 2 + s, 1), :].rearrange("p t d -> p (t d)")
                        dve.scalar_tensor_tensor(xt, o[s][:, :], tgate[:, 3:4], xt, ALU.mult, ALU.add).then_inc(s_x2, 1)
                    assert steps == STEPS

                with dve.Fori(0, NT // 2) as i:
                    body(i)

            def turned(engine, g):
                src = WTB[g % 4][:, :]
                if g < GROUPS:
                    dst = w1T[:, g // 2, (g % 2) * 8 * P:(g % 2 + 1) * 8 * P]
                else:
                    m = (g - GROUPS) * 2
                    dst, src = w2T[:, m:m + 2, :], src.rearrange("p (m d) -> p m d", m=2)
                if g % 2:
                    engine.tensor_copy(dst, src).then_inc(s_wd, 1)
                else:
                    engine.activation(dst, src, ACT.Copy).then_inc(s_wa, 1)

            def scalar(act):
                act.wait_ge(*x2_done)
                act.activation(identb[:, :], ident[:, :], ACT.Copy).then_inc(s_id, 1)
                act.activation(scrap[:, 40:41], eps[:, 0:1], ACT.Copy).then_inc(s_te, 2)
                for w in range(2):
                    act.wait_ge(s_w[w], 16)
                    act.activation(wq[w][:, :, :], raw[w][:, :, :], ACT.Abs, accum_out=size[:, w:w + 1]).then_inc(s_size, 1)
                act.wait_ge(s_size, 2)
                for w in range(2):
                    for k in range(CH):
                        act.wait_ge(s_wr, w * CH + k + 1)
                        act.activation(chunk(wq[w], k), chunk(raw[w], k), ACT.Copy, bias=-MAGIC).then_inc(s_wq, 1)
                for g in range(0, 2 * GROUPS, 2):
                    act.wait_ge(s_wt, g + 1)
                    turned(act, g)

                def body(i):
                    def whole(dst, src, n):
                        act.wait_ge(s_r, 4 * i + n + 1)
                        act.activation(dst[:, :], src[:, :], ACT.Copy, bias=-MAGIC).then_inc(s_q, 1)

                    def copy(dst, n, m):
                        act.wait_ge(s_tr, TURNS * i + n + 1)
                        act.activation(dst, TRB[n % 2][:, 0:m * P].rearrange("p (m n) -> p m n", m=m), ACT.Copy).then_inc(s_te, 1)

                    for s in range(2):
                        whole(hq[s], h[s], s)
                    for s in range(2):
                        copy(hqT[s][:, :, :], s, KC)
                    for s in range(2):
                        act.wait_ge(s_z, HB * (2 * i + s + 2))
                        act.activation(z[s][:, :], z[s][:, :], ACT.Gelu).then_inc(s_g, 1)
                    for s in range(2):
                        whole(zq[s], z[s], 2 + s)
                        for k in range(2):
                            copy(zqT[s][:, k * 8:(k + 1) * 8, :], 2 + 2 * s + k, 8)

                with act.Fori(0, NT // 2) as i:
                    body(i)

            def tensor(pe):
                pe.wait_ge(s_one, 1)
                pe.wait_ge(s_size, 2)
                pe.matmul(HID_B[0][:, 0:2], ones[:, :], size[:, :], start=True, stop=True).then_inc(s_sum, 1)
                pe.wait_ge(s_id, 1)
                for g in range(2 * GROUPS):
                    if g < GROUPS:
                        pe.wait_ge(s_wq, CH)
                    else:
                        pe.wait_ge(s_wq, 2 * CH)
                    if g >= 4:
                        pe.wait_ge((s_wa, s_wd)[g % 2], (g - 4) // 2 + 1)
                    for k in range(8):
                        if g < GROUPS:
                            src = wq[0][:, (g % 2) * 8 + k, (g // 2) * P:(g // 2 + 1) * P]
                        else:
                            m = (g - GROUPS) * 2 + k // 4
                            src = wq[1][:, k % 4, m * P:(m + 1) * P]
                        mm = pe.transpose(WTB[g % 4][:, k * P:(k + 1) * P], src, identb[:, :])
                    mm.then_inc(s_wt, 1)
                pe.wait_ge(s_wa, GROUPS)
                pe.wait_ge(s_wd, GROUPS)

                def body(i):
                    def turn(src, n, m):
                        pe.wait_ge(s_te, TURNS * i + n + 1)
                        for k in range(m):
                            mm = pe.transpose(TRB[n % 2][:, k * P:(k + 1) * P], src[:, k * P:(k + 1) * P], identb[:, :])
                        mm.then_inc(s_tr, 1)

                    for s in range(2):
                        pe.wait_ge(s_q, 4 * i + s + 1)
                        turn(hq[s][:, :], s, KC)
                    for s in range(2):
                        pe.wait_ge(s_te, TURNS * i + s + 3)
                        for k in range(HB):
                            pe.wait_ge(s_z, HB * (2 * i + s) + k + 1)
                            for c in range(KC):
                                mm = pe.matmul(HID_B[k][:, :], hqT[s][:, c, :], w1T[:, c, k * BANK:(k + 1) * BANK],
                                               start=(c == 0), stop=(c == KC - 1))
                            mm.then_inc(s_m1, 1)
                    for s in range(2):
                        pe.wait_ge(s_q, 4 * i + 2 + s + 1)
                        for k in range(2):
                            turn(zq[s][:, k * 8 * P:(k + 1) * 8 * P], 2 + 2 * s + k, 8)
                        pe.wait_ge(s_te, TURNS * i + 2 * s + 6)
                        pe.wait_ge(s_o, 2 * i + s + 1)
                        for m in range(HC):
                            mm = pe.matmul(OUT_B[s][:, :], zqT[s][:, m, :], w2T[:, m, :], start=(m == 0), stop=(m == HC - 1))
                        mm.then_inc(s_m2, 1)

                with pe.Fori(0, NT // 2) as i:
                    body(i)

            programs["SP"].append(sync)
            programs["DVE"].append(vector)
            programs["ACT"].append(scalar)
            programs["PE"].append(tensor)

        bit_ffn()
        phase.close()

        block = ctx.enter_context(nc.Block())

        @block.sync
        def _(sp):
            for stage in programs["SP"]:
                stage(sp)

        @block.scalar
        def _(act):
            for stage in programs["ACT"]:
                stage(act)

        @block.tensor
        def _(pe):
            for stage in programs["PE"]:
                stage(pe)

        @block.vector
        def _(dve):
            for stage in programs["DVE"]:
                stage(dve)

        @block.gpsimd
        def _(pool):
            for stage in programs["POOL"]:
                stage(pool)


def constants():
    half = 32
    inv = (np.float32(1.0) / np.float32(150000.0) ** (np.arange(half, dtype=np.float32) / np.float32(half))).astype(np.float32)
    angle = (np.arange(S, dtype=np.float32)[:, None] * inv).astype(np.float32)
    cos, sin = np.cos(angle), np.sin(angle)
    rows = np.arange(P)
    causal = np.zeros((P, S), np.float32)
    causal[:, S - P:] = np.where(rows[None, :] <= rows[:, None], 0.0, -BIG)
    part = np.stack([np.arange(P) < P - 16, np.arange(P) >= P - 16], axis=1).astype(np.float32)
    ne, cap = 16, T * 4 // 16 * 3 // 2
    token = np.stack(np.broadcast_arrays(rows[:, None], P * np.arange(NT)[None, :]), axis=2).astype(np.float32)
    return {"c_before": np.triu(np.ones((P, P), np.float32), 1), "c_ones": np.ones((P, P), np.float32),
            "c_first": (np.arange(ne) * cap - 1).astype(np.float32), "c_count_up": np.arange(1, cap + 1).astype(np.float32),
            "c_token": token, "c_part": part, "c_ident": np.eye(P, dtype=np.float32), "c_causal": causal,
            "c_cos": np.concatenate([cos, cos], 1).reshape(QT, P, 2 * half).transpose(1, 0, 2).astype(np.float32),
            "c_sin": np.concatenate([-sin, sin], 1).reshape(QT, P, 2 * half).transpose(1, 0, 2).astype(np.float32)}


def kernel(**inputs):
    import concourse.bacc as _bacc
    from concourse.bass_utils import run_bass_kernel_spmd as _run

    nc = _bacc.Bacc("TRN2", target_bir_lowering=False, num_devices=1)
    arrays, args = {}, {}
    wkv = np.concatenate([inputs["L1_xattn_Wk"], inputs["L1_xattn_Wv"]], axis=1)
    bkv = np.concatenate([inputs["L1_xattn_bk"], inputs["L1_xattn_bv"]])
    for name, value in {**inputs, **constants(), "wkv": wkv, "bkv": bkv}.items():
        value = np.ascontiguousarray(value)
        if value.dtype == np.bool_:
            value = value.view(np.uint8)
        arrays[f"in_{name}"] = value
        args[name] = nc.dram_tensor(f"in_{name}", value.shape, mybir.dt.from_np(value.dtype), kind="ExternalInput").ap()
    out = nc.dram_tensor("out_x", (B, S, D), F32, kind="ExternalOutput").ap()
    program(nc, args, out)
    r = _run(nc, [arrays], core_ids=[0])
    return r.results[0]["out_x"]
```
